# Optimizing a Trainium2 kernel written in Bass

```python
import numpy as np
import jax
import jax.numpy as jnp

def _softmax(x, axis=-1):
    return jax.nn.softmax(x, axis=axis)

def _gelu(x):
    return jax.nn.gelu(x, approximate=True)

def _silu(x):
    return jax.nn.silu(x)

def _sigmoid(x):
    return jax.nn.sigmoid(x)

def _layernorm(x, axis=-1, eps=1e-05):
    m = jnp.mean(x, axis=axis, keepdims=True)
    v = jnp.var(x, axis=axis, keepdims=True)
    return (x - m) / jnp.sqrt(v + eps)

def _scatter_add(tgt, idx, src, axis=0):
    return tgt.at[idx].add(src)

def _segment_sum(src, seg, n):
    return jax.ops.segment_sum(src, seg, n)
kernel_name = 'mk_lm_tower_d4_tok_ids1024_r4_8aca5d'

def setup_inputs(seed: int=0):
    np.random.seed(seed)
    _w = jnp.asarray

    def _rec_inputs():
        import jax
        import jax.numpy as jnp
        _rk = jax.random.key(seed)
        x = jax.random.randint(jax.random.fold_in(_rk, 1), (4, 512), 0, 12564, jnp.int32)
        return x
    x = _rec_inputs()

    def _L0_tok_setup():
        import jax, jax.numpy as jnp
        import numpy as np
        FP4_GRID = jnp.array([0.0, 0.5, 1.0, 1.5, 2.0, 3.0, 4.0, 6.0], dtype=jnp.float32)
        FP4_BOUNDS = jnp.array([0.25, 0.75, 1.25, 1.75, 2.5, 3.5, 5.0], dtype=jnp.float32)
        VOCAB = 50257
        FEATURES = 256
        BLOCK_SIZE = 32

        def mxfp4_quant_dequant(table, block_size):
            V, F = table.shape
            nb = F // block_size
            x = table.reshape(V, nb, block_size)
            max_abs = jnp.max(jnp.abs(x), axis=-1, keepdims=True)
            scale = jnp.where(max_abs == 0, 1.0, max_abs / 6.0)
            s = x / scale
            sign = jnp.where(s < 0, -1.0, 1.0)
            code = jnp.searchsorted(FP4_BOUNDS, jnp.abs(s))
            deq = sign * FP4_GRID[code] * scale
            return deq.reshape(V, F)
        key = jax.random.key(seed)
        k1, k2 = jax.random.split(key)
        inputs = jax.random.randint(k1, (4, 1024), 0, VOCAB, dtype=jnp.int32)
        embedding = jax.random.normal(k2, (VOCAB, FEATURES), dtype=jnp.float32) * 0.02
        return {'inputs': inputs, 'embedding': embedding}
    _L0_tok_all = _L0_tok_setup()
    _L0_tok_in = {k: v for k, v in _L0_tok_all.items() if k in ('embedding',)}
    del _L0_tok_all

    def _L0_attn_setup():
        import jax, jax.numpy as jnp
        import numpy as np
        EMBED = 256
        HEADS = 8
        D1 = 512
        HEAD_DIM = D1 // HEADS
        SEQ = 512
        BATCH = 4
        MAXL = 512
        EPS = 1e-08

        def simple_rms_norm(x, d):
            rms = jnp.linalg.norm(x, axis=-1, keepdims=True) * d ** (-0.5)
            return x / (rms + EPS)

        def toeplitz_causal(v, t_zero, t_pos):
            n = v.shape[2]
            t = jnp.concatenate([t_zero, t_pos[:, :n - 1]], axis=-1)
            m = 2 * n
            vf = jnp.fft.rfft(v, m, axis=2)
            tf = jnp.fft.rfft(t, m, axis=-1)
            y = jnp.fft.irfft(vf * tf[None, :, :, None], m, axis=2)
            return y[:, :, :n]
        key = jax.random.key(seed)
        ks = jax.random.split(key, 9)
        s = 0.02
        return {'x': jax.random.normal(ks[0], (SEQ, BATCH, EMBED), jnp.float32), 'u_w': jax.random.normal(ks[1], (D1, EMBED), jnp.float32) * s, 'u_b': jax.random.normal(ks[2], (D1,), jnp.float32) * s, 'v_w': jax.random.normal(ks[3], (D1, EMBED), jnp.float32) * s, 'v_b': jax.random.normal(ks[4], (D1,), jnp.float32) * s, 'o_w': jax.random.normal(ks[5], (EMBED, D1), jnp.float32) * s, 'o_b': jax.random.normal(ks[6], (EMBED,), jnp.float32) * s, 't_zero': jax.random.normal(ks[7], (HEADS, 1), jnp.float32), 't_pos': jax.random.normal(ks[8], (HEADS, MAXL - 1), jnp.float32)}
    _L0_attn_all = _L0_attn_setup()
    _L0_attn_in = {k: v for k, v in _L0_attn_all.items() if k in ('u_w', 'u_b', 'v_w', 'v_b', 'o_w', 'o_b', 't_zero', 't_pos')}
    del _L0_attn_all

    def _L0_ffn_setup():
        import jax, jax.numpy as jnp
        import numpy as np
        B, S, H, E, K, I = (1, 128, 256, 16, 4, 256)
        ALPHA, LIMIT = (1.702, 7.0)
        key = jax.random.key(seed)
        ks = jax.random.split(key, 7)
        return {'hidden_states': jax.random.normal(ks[0], (B, S, H), jnp.float32), 'router_w': jax.random.normal(ks[1], (H, E), jnp.float32) * 0.02, 'router_b': jax.random.normal(ks[2], (E,), jnp.float32) * 0.02, 'gate_up_proj': jax.random.normal(ks[3], (E, H, 2 * I), jnp.float32) * 0.02, 'gate_up_bias': jax.random.normal(ks[4], (E, 2 * I), jnp.float32) * 0.02, 'down_proj': jax.random.normal(ks[5], (E, I, H), jnp.float32) * 0.02, 'down_bias': jax.random.normal(ks[6], (E, H), jnp.float32) * 0.02}
    _L0_ffn_all = _L0_ffn_setup()
    _L0_ffn_in = {k: v for k, v in _L0_ffn_all.items() if k in ('router_w', 'router_b', 'gate_up_proj', 'gate_up_bias', 'down_proj', 'down_bias')}
    del _L0_ffn_all

    def _L1_attn_setup():
        import jax, jax.numpy as jnp
        import numpy as np
        import math
        B, S, D = (4, 512, 256)
        H, HD, L = (16, 64, 128)
        ROPE_BASE = 10000.0
        EPS = 1e-06

        def _rope_angles(seq_len, head_dim, base):
            inv_freq = 1.0 / base ** (jnp.arange(0, head_dim, 2, dtype=jnp.float32) / head_dim)
            pos = jnp.arange(seq_len, dtype=jnp.float32)
            return pos[:, None] * inv_freq[None, :]

        def _apply_rope(t, ang):
            cos = jnp.cos(ang)
            sin = jnp.sin(ang)
            t1, t2 = jnp.split(t, 2, axis=-1)
            return jnp.concatenate([t1 * cos - t2 * sin, t1 * sin + t2 * cos], axis=-1)
        key = jax.random.key(seed)
        ks = jax.random.split(key, 7)

        def w(k, shape, fan_in):
            return jax.random.normal(k, shape, jnp.float32) * fan_in ** (-0.5)
        return {'x': jax.random.normal(ks[0], (B, S, D), jnp.float32), 'norm_w': jnp.ones((D,), jnp.float32), 'wq': w(ks[1], (D, H * HD), D), 'kv_down': w(ks[2], (D, L), D), 'wk': w(ks[3], (L, H * HD), L), 'wv': w(ks[4], (L, H * HD), L), 'wo': w(ks[5], (H * HD, D), H * HD)}
    _L1_attn_all = _L1_attn_setup()
    _L1_attn_in = {k: v for k, v in _L1_attn_all.items() if k in ('norm_w', 'wq', 'kv_down', 'wk', 'wv', 'wo')}
    del _L1_attn_all

    def _L1_ffn_setup():
        import jax, jax.numpy as jnp
        import numpy as np
        DIM = 256
        INTER = 256
        E = 32
        K = 4
        G = 8
        LG = 4
        ROUTE_SCALE = 1.0
        CAP_FACTOR = 1.25
        B, S = (4, 512)

        def _gate(xf, wg):
            logits = xf @ wg.T
            scores = jax.nn.softmax(logits, axis=-1)
            sg = scores.reshape(-1, G, E // G)
            group_scores = sg.max(axis=-1)
            _, gtop = jax.lax.top_k(group_scores, LG)
            keep_g = jnp.sum(jax.nn.one_hot(gtop, G, dtype=jnp.float32), axis=1) > 0
            masked = jnp.where(keep_g[:, :, None], sg, -jnp.inf).reshape(-1, E)
            _, idx = jax.lax.top_k(masked, K)
            w = jnp.take_along_axis(scores, idx, axis=1)
            w = w / (w.sum(-1, keepdims=True) + 1e-09) * ROUTE_SCALE
            return (w.astype(xf.dtype), idx)

        def _forward(x, wg, w1, w2, w3, sw1, sw2, sw3):
            shape = x.shape
            xf = x.reshape(-1, DIM)
            N = xf.shape[0]
            cap = max(1, int(CAP_FACTOR * N * K / E))
            w, idx = _gate(xf, wg)
            fe = idx.reshape(-1)
            oh = jax.nn.one_hot(fe, E, dtype=jnp.int32)
            pos = (jnp.cumsum(oh, axis=0) * oh).sum(-1) - 1
            keep = pos < cap
            dest = jnp.where(keep, fe * cap + pos, E * cap)
            tok = jnp.arange(N * K, dtype=jnp.int32) // K
            buf_tok = jnp.full((E * cap + 1,), N, jnp.int32).at[dest].set(tok)[:-1]
            buf_w = jnp.zeros((E * cap + 1,), x.dtype).at[dest].set(w.reshape(-1))[:-1]
            xp = jnp.concatenate([xf, jnp.zeros((1, DIM), x.dtype)], axis=0)
            xe = xp[buf_tok].reshape(E, cap, DIM)
            h = jax.nn.silu(jnp.einsum('ecd,edh->ech', xe, w1)) * jnp.einsum('ecd,edh->ech', xe, w3)
            out = jnp.einsum('ech,ehd->ecd', h, w2) * buf_w.reshape(E, cap, 1)
            y = jnp.zeros((N + 1, DIM), x.dtype).at[buf_tok].add(out.reshape(E * cap, DIM))[:N]
            z = jax.nn.silu(xf @ sw1) * (xf @ sw3) @ sw2
            return (y + z).reshape(shape)
        key = jax.random.key(seed)
        ks = jax.random.split(key, 9)
        sd = DIM ** (-0.5)
        si = INTER ** (-0.5)
        x = jax.random.normal(ks[0], (B, S, DIM), jnp.float32)
        wg = jax.random.normal(ks[1], (E, DIM), jnp.float32) * sd
        w1 = jax.random.normal(ks[2], (E, DIM, INTER), jnp.float32) * sd
        w3 = jax.random.normal(ks[3], (E, DIM, INTER), jnp.float32) * sd
        w2 = jax.random.normal(ks[4], (E, INTER, DIM), jnp.float32) * si
        sw1 = jax.random.normal(ks[5], (DIM, INTER), jnp.float32) * sd
        sw3 = jax.random.normal(ks[6], (DIM, INTER), jnp.float32) * sd
        sw2 = jax.random.normal(ks[7], (INTER, DIM), jnp.float32) * si
        return dict(x=x, wg=wg, w1=w1, w2=w2, w3=w3, sw1=sw1, sw2=sw2, sw3=sw3)
    _L1_ffn_all = _L1_ffn_setup()
    _L1_ffn_in = {k: v for k, v in _L1_ffn_all.items() if k in ('wg', 'w1', 'w2', 'w3', 'sw1', 'sw2', 'sw3')}
    del _L1_ffn_all

    def _L2_attn_setup():
        import jax, jax.numpy as jnp
        import numpy as np
        NUM_LANDMARKS = 64
        key = jax.random.key(seed)
        ks = jax.random.split(key, 4)
        B, S, D = (4, 1024, 256)
        init = 0.02
        return {'hidden_states': jax.random.normal(ks[0], (B, S, D), dtype=jnp.float32), 'Wq': jax.random.normal(ks[1], (D, D), dtype=jnp.float32) * init, 'bq': jnp.zeros((D,), dtype=jnp.float32), 'Wk': jax.random.normal(ks[2], (D, D), dtype=jnp.float32) * init, 'bk': jnp.zeros((D,), dtype=jnp.float32), 'Wv': jax.random.normal(ks[3], (D, D), dtype=jnp.float32) * init, 'bv': jnp.zeros((D,), dtype=jnp.float32)}
    _L2_attn_all = _L2_attn_setup()
    _L2_attn_in = {k: v for k, v in _L2_attn_all.items() if k in ('Wq', 'bq', 'Wk', 'bk', 'Wv', 'bv')}
    del _L2_attn_all

    def _L2_ffn_setup():
        import jax, jax.numpy as jnp
        import numpy as np
        EMB = 256
        FF = 4 * EMB

        def _ternary(w):
            scale = jnp.maximum(jnp.mean(jnp.abs(w)), 1e-08)
            w_t = jnp.clip(jnp.round(w / scale), -1.0, 1.0)
            return w + jax.lax.stop_gradient(w_t - w)
        key = jax.random.key(seed)
        kx, k1, k2, kb1, kb2 = jax.random.split(key, 5)
        x = jax.random.normal(kx, (4, 512, EMB), dtype=jnp.float32)
        lim1 = 1.0 / np.sqrt(EMB)
        lim2 = 1.0 / np.sqrt(FF)
        W1 = jax.random.uniform(k1, (FF, EMB), jnp.float32, -lim1, lim1)
        b1 = jax.random.uniform(kb1, (FF,), jnp.float32, -lim1, lim1)
        W2 = jax.random.uniform(k2, (EMB, FF), jnp.float32, -lim2, lim2)
        b2 = jax.random.uniform(kb2, (EMB,), jnp.float32, -lim2, lim2)
        return {'x': x, 'W1': W1, 'b1': b1, 'W2': W2, 'b2': b2}
    _L2_ffn_all = _L2_ffn_setup()
    _L2_ffn_in = {k: v for k, v in _L2_ffn_all.items() if k in ('W1', 'b1', 'W2', 'b2')}
    del _L2_ffn_all

    def _L3_attn_setup():
        import jax, jax.numpy as jnp
        import numpy as np
        B, S, E, H = (2, 512, 256, 16)
        D = E // H
        key = jax.random.key(seed)
        k1, k2, k3 = jax.random.split(key, 3)
        x = jax.random.normal(k1, (B, S, E), dtype=jnp.float32)
        lim_qkv = np.sqrt(6.0 / (E + 3 * E)).astype(np.float32)
        lim_out = np.sqrt(6.0 / (E + E)).astype(np.float32)
        w_qkv = jax.random.uniform(k2, (E, 3 * E), jnp.float32, -lim_qkv, lim_qkv)
        w_out = jax.random.uniform(k3, (E, E), jnp.float32, -lim_out, lim_out)
        return {'x': x, 'w_qkv': w_qkv, 'w_out': w_out}
    _L3_attn_all = _L3_attn_setup()
    _L3_attn_in = {k: v for k, v in _L3_attn_all.items() if k in ('w_qkv', 'w_out')}
    del _L3_attn_all

    def _L3_ffn_setup():
        import jax, jax.numpy as jnp
        import numpy as np
        BLOCK = 16
        _GRID = jnp.array([0.0, 0.5, 1.0, 1.5, 2.0, 3.0, 4.0, 6.0], dtype=jnp.float32)
        _MID = jnp.array([0.25, 0.75, 1.25, 1.75, 2.5, 3.5, 5.0], dtype=jnp.float32)

        def fp4_quant_dequant(x):
            shape = x.shape
            xb = x.reshape(shape[:-1] + (shape[-1] // BLOCK, BLOCK))
            scale = jnp.max(jnp.abs(xb), axis=-1, keepdims=True) / 6.0
            scale = jnp.maximum(scale, jnp.float32(1e-12))
            xn = xb / scale
            idx = jnp.searchsorted(_MID, jnp.abs(xn))
            q = _GRID[idx] * jnp.sign(xn) * scale
            return q.reshape(shape)

        def fp4_linear(x, w):
            xq = fp4_quant_dequant(x)
            wq = fp4_quant_dequant(w)
            return jnp.einsum('bsk,nk->bsn', xq, wq)
        key = jax.random.key(seed)
        k1, k2, k3, k4 = jax.random.split(key, 4)
        H, I = (256, 704)
        x = jax.random.normal(k1, (4, 1024, H), dtype=jnp.float32)
        w_gate = jax.random.normal(k2, (I, H), dtype=jnp.float32) * 0.02
        w_up = jax.random.normal(k3, (I, H), dtype=jnp.float32) * 0.02
        w_down = jax.random.normal(k4, (H, I), dtype=jnp.float32) * 0.02
        return {'x': x, 'w_gate': w_gate, 'w_up': w_up, 'w_down': w_down}
    _L3_ffn_all = _L3_ffn_setup()
    _L3_ffn_in = {k: v for k, v in _L3_ffn_all.items() if k in ('w_gate', 'w_up', 'w_down')}
    del _L3_ffn_all
    return {'x': x, 'L0_tok_embedding': _L0_tok_in['embedding'], 'L0_attn_u_w': _L0_attn_in['u_w'], 'L0_attn_u_b': _L0_attn_in['u_b'], 'L0_attn_v_w': _L0_attn_in['v_w'], 'L0_attn_v_b': _L0_attn_in['v_b'], 'L0_attn_o_w': _L0_attn_in['o_w'], 'L0_attn_o_b': _L0_attn_in['o_b'], 'L0_attn_t_zero': _L0_attn_in['t_zero'], 'L0_attn_t_pos': _L0_attn_in['t_pos'], 'L0_ffn_router_w': _L0_ffn_in['router_w'], 'L0_ffn_router_b': _L0_ffn_in['router_b'], 'L0_ffn_gate_up_proj': _L0_ffn_in['gate_up_proj'], 'L0_ffn_gate_up_bias': _L0_ffn_in['gate_up_bias'], 'L0_ffn_down_proj': _L0_ffn_in['down_proj'], 'L0_ffn_down_bias': _L0_ffn_in['down_bias'], 'L1_attn_norm_w': _L1_attn_in['norm_w'], 'L1_attn_wq': _L1_attn_in['wq'], 'L1_attn_kv_down': _L1_attn_in['kv_down'], 'L1_attn_wk': _L1_attn_in['wk'], 'L1_attn_wv': _L1_attn_in['wv'], 'L1_attn_wo': _L1_attn_in['wo'], 'L1_ffn_wg': _L1_ffn_in['wg'], 'L1_ffn_w1': _L1_ffn_in['w1'], 'L1_ffn_w2': _L1_ffn_in['w2'], 'L1_ffn_w3': _L1_ffn_in['w3'], 'L1_ffn_sw1': _L1_ffn_in['sw1'], 'L1_ffn_sw2': _L1_ffn_in['sw2'], 'L1_ffn_sw3': _L1_ffn_in['sw3'], 'L2_attn_Wq': _L2_attn_in['Wq'], 'L2_attn_bq': _L2_attn_in['bq'], 'L2_attn_Wk': _L2_attn_in['Wk'], 'L2_attn_bk': _L2_attn_in['bk'], 'L2_attn_Wv': _L2_attn_in['Wv'], 'L2_attn_bv': _L2_attn_in['bv'], 'L2_ffn_W1': _L2_ffn_in['W1'], 'L2_ffn_b1': _L2_ffn_in['b1'], 'L2_ffn_W2': _L2_ffn_in['W2'], 'L2_ffn_b2': _L2_ffn_in['b2'], 'L3_attn_w_qkv': _L3_attn_in['w_qkv'], 'L3_attn_w_out': _L3_attn_in['w_out'], 'L3_ffn_w_gate': _L3_ffn_in['w_gate'], 'L3_ffn_w_up': _L3_ffn_in['w_up'], 'L3_ffn_w_down': _L3_ffn_in['w_down']}

def reference(x, L0_tok_embedding, L0_attn_u_w, L0_attn_u_b, L0_attn_v_w, L0_attn_v_b, L0_attn_o_w, L0_attn_o_b, L0_attn_t_zero, L0_attn_t_pos, L0_ffn_router_w, L0_ffn_router_b, L0_ffn_gate_up_proj, L0_ffn_gate_up_bias, L0_ffn_down_proj, L0_ffn_down_bias, L1_attn_norm_w, L1_attn_wq, L1_attn_kv_down, L1_attn_wk, L1_attn_wv, L1_attn_wo, L1_ffn_wg, L1_ffn_w1, L1_ffn_w2, L1_ffn_w3, L1_ffn_sw1, L1_ffn_sw2, L1_ffn_sw3, L2_attn_Wq, L2_attn_bq, L2_attn_Wk, L2_attn_bk, L2_attn_Wv, L2_attn_bv, L2_ffn_W1, L2_ffn_b1, L2_ffn_W2, L2_ffn_b2, L3_attn_w_qkv, L3_attn_w_out, L3_ffn_w_gate, L3_ffn_w_up, L3_ffn_w_down):
    import jax
    import jax.numpy as jnp

    def _L0_tok_ref(inputs, embedding):
        import jax, jax.numpy as jnp
        import numpy as np
        FP4_GRID = jnp.array([0.0, 0.5, 1.0, 1.5, 2.0, 3.0, 4.0, 6.0], dtype=jnp.float32)
        FP4_BOUNDS = jnp.array([0.25, 0.75, 1.25, 1.75, 2.5, 3.5, 5.0], dtype=jnp.float32)
        VOCAB = 50257
        FEATURES = 256
        BLOCK_SIZE = 32

        def mxfp4_quant_dequant(table, block_size):
            V, F = table.shape
            nb = F // block_size
            x = table.reshape(V, nb, block_size)
            max_abs = jnp.max(jnp.abs(x), axis=-1, keepdims=True)
            scale = jnp.where(max_abs == 0, 1.0, max_abs / 6.0)
            s = x / scale
            sign = jnp.where(s < 0, -1.0, 1.0)
            code = jnp.searchsorted(FP4_BOUNDS, jnp.abs(s))
            deq = sign * FP4_GRID[code] * scale
            return deq.reshape(V, F)
        deq = mxfp4_quant_dequant(embedding, BLOCK_SIZE)
        return deq[inputs]

    def _L0_attn_ref(x, u_w, u_b, v_w, v_b, o_w, o_b, t_zero, t_pos):
        import jax, jax.numpy as jnp
        import numpy as np
        EMBED = 256
        HEADS = 8
        D1 = 512
        HEAD_DIM = D1 // HEADS
        SEQ = 512
        BATCH = 4
        MAXL = 512
        EPS = 1e-08

        def simple_rms_norm(x, d):
            rms = jnp.linalg.norm(x, axis=-1, keepdims=True) * d ** (-0.5)
            return x / (rms + EPS)

        def toeplitz_causal(v, t_zero, t_pos):
            n = v.shape[2]
            t = jnp.concatenate([t_zero, t_pos[:, :n - 1]], axis=-1)
            m = 2 * n
            vf = jnp.fft.rfft(v, m, axis=2)
            tf = jnp.fft.rfft(t, m, axis=-1)
            y = jnp.fft.irfft(vf * tf[None, :, :, None], m, axis=2)
            return y[:, :, :n]
        shortcut = x
        xn = simple_rms_norm(x, EMBED)
        u = jax.nn.silu(xn @ u_w.T + u_b)
        v = jax.nn.silu(xn @ v_w.T + v_b)
        n, b, _ = v.shape
        vh = v.reshape(n, b, HEADS, HEAD_DIM).transpose(1, 2, 0, 3)
        y = toeplitz_causal(vh, t_zero, t_pos)
        y = y.transpose(2, 0, 1, 3).reshape(n, b, D1)
        out = u * y
        out = out @ o_w.T + o_b + shortcut
        return out

    def _L0_ffn_ref(hidden_states, router_w, router_b, gate_up_proj, gate_up_bias, down_proj, down_bias):
        import jax, jax.numpy as jnp
        import numpy as np
        B, S, H, E, K, I = (1, 128, 256, 16, 4, 256)
        ALPHA, LIMIT = (1.702, 7.0)
        b, s, h = hidden_states.shape
        x = hidden_states.reshape(-1, h)
        logits = x @ router_w + router_b
        topv, topi = jax.lax.top_k(logits, K)
        topw = jax.nn.softmax(topv, axis=-1)
        one_hot = (topi[..., None] == jnp.arange(E)).astype(topw.dtype)
        scores = jnp.einsum('tk,tke->te', topw, one_hot)
        gu = jnp.einsum('th,ehf->tef', x, gate_up_proj) + gate_up_bias
        gate = jnp.minimum(gu[..., ::2], LIMIT)
        up = jnp.clip(gu[..., 1::2], -LIMIT, LIMIT)
        glu = gate * jax.nn.sigmoid(gate * ALPHA)
        act = (up + 1.0) * glu
        expert_out = jnp.einsum('tei,eih->teh', act, down_proj) + down_bias
        out = jnp.einsum('te,teh->th', scores, expert_out)
        return out.reshape(b, s, h)

    def _L1_attn_ref(x, norm_w, wq, kv_down, wk, wv, wo):
        import jax, jax.numpy as jnp
        import numpy as np
        import math
        B, S, D = (4, 512, 256)
        H, HD, L = (16, 64, 128)
        ROPE_BASE = 10000.0
        EPS = 1e-06

        def _rope_angles(seq_len, head_dim, base):
            inv_freq = 1.0 / base ** (jnp.arange(0, head_dim, 2, dtype=jnp.float32) / head_dim)
            pos = jnp.arange(seq_len, dtype=jnp.float32)
            return pos[:, None] * inv_freq[None, :]

        def _apply_rope(t, ang):
            cos = jnp.cos(ang)
            sin = jnp.sin(ang)
            t1, t2 = jnp.split(t, 2, axis=-1)
            return jnp.concatenate([t1 * cos - t2 * sin, t1 * sin + t2 * cos], axis=-1)
        residual = x
        var = jnp.mean(x * x, axis=-1, keepdims=True)
        xn = x * jax.lax.rsqrt(var + EPS) * norm_w
        q = (xn @ wq).reshape(B, S, H, HD).transpose(0, 2, 1, 3)
        kv = xn @ kv_down
        k = (kv @ wk).reshape(B, S, H, HD).transpose(0, 2, 1, 3)
        v = (kv @ wv).reshape(B, S, H, HD).transpose(0, 2, 1, 3)
        ang = _rope_angles(S, HD, ROPE_BASE)
        q = _apply_rope(q, ang)
        k = _apply_rope(k, ang)
        scale = 1.0 / math.sqrt(HD)
        attn = jnp.einsum('bhsd,bhtd->bhst', q, k) * scale
        attn = jax.nn.softmax(attn, axis=-1)
        out = jnp.einsum('bhst,bhtd->bhsd', attn, v)
        out = out.transpose(0, 2, 1, 3).reshape(B, S, H * HD) @ wo
        return residual + out

    def _L1_ffn_ref(x, wg, w1, w2, w3, sw1, sw2, sw3):
        import jax, jax.numpy as jnp
        import numpy as np
        DIM = 256
        INTER = 256
        E = 32
        K = 4
        G = 8
        LG = 4
        ROUTE_SCALE = 1.0
        CAP_FACTOR = 1.25
        B, S = (4, 512)

        def _gate(xf, wg):
            logits = xf @ wg.T
            scores = jax.nn.softmax(logits, axis=-1)
            sg = scores.reshape(-1, G, E // G)
            group_scores = sg.max(axis=-1)
            _, gtop = jax.lax.top_k(group_scores, LG)
            keep_g = jnp.sum(jax.nn.one_hot(gtop, G, dtype=jnp.float32), axis=1) > 0
            masked = jnp.where(keep_g[:, :, None], sg, -jnp.inf).reshape(-1, E)
            _, idx = jax.lax.top_k(masked, K)
            w = jnp.take_along_axis(scores, idx, axis=1)
            w = w / (w.sum(-1, keepdims=True) + 1e-09) * ROUTE_SCALE
            return (w.astype(xf.dtype), idx)

        def _forward(x, wg, w1, w2, w3, sw1, sw2, sw3):
            shape = x.shape
            xf = x.reshape(-1, DIM)
            N = xf.shape[0]
            cap = max(1, int(CAP_FACTOR * N * K / E))
            w, idx = _gate(xf, wg)
            fe = idx.reshape(-1)
            oh = jax.nn.one_hot(fe, E, dtype=jnp.int32)
            pos = (jnp.cumsum(oh, axis=0) * oh).sum(-1) - 1
            keep = pos < cap
            dest = jnp.where(keep, fe * cap + pos, E * cap)
            tok = jnp.arange(N * K, dtype=jnp.int32) // K
            buf_tok = jnp.full((E * cap + 1,), N, jnp.int32).at[dest].set(tok)[:-1]
            buf_w = jnp.zeros((E * cap + 1,), x.dtype).at[dest].set(w.reshape(-1))[:-1]
            xp = jnp.concatenate([xf, jnp.zeros((1, DIM), x.dtype)], axis=0)
            xe = xp[buf_tok].reshape(E, cap, DIM)
            h = jax.nn.silu(jnp.einsum('ecd,edh->ech', xe, w1)) * jnp.einsum('ecd,edh->ech', xe, w3)
            out = jnp.einsum('ech,ehd->ecd', h, w2) * buf_w.reshape(E, cap, 1)
            y = jnp.zeros((N + 1, DIM), x.dtype).at[buf_tok].add(out.reshape(E * cap, DIM))[:N]
            z = jax.nn.silu(xf @ sw1) * (xf @ sw3) @ sw2
            return (y + z).reshape(shape)
        return _forward(x, wg, w1, w2, w3, sw1, sw2, sw3)

    def _L2_attn_ref(hidden_states, Wq, bq, Wk, bk, Wv, bv):
        import jax, jax.numpy as jnp
        import numpy as np
        NUM_LANDMARKS = 64
        B, S, D = hidden_states.shape
        L = NUM_LANDMARKS
        q = hidden_states @ Wq + bq
        k = hidden_states @ Wk + bk
        v = hidden_states @ Wv + bv
        q = jax.nn.softmax(q, axis=-1)
        k = jax.nn.softmax(k, axis=-1)
        k_landmarks = k.reshape(B, L, S // L, D).mean(axis=2)
        kernel_1 = jnp.einsum('bqd,bkd->bqk', q, k_landmarks)
        kernel_2 = jnp.einsum('bkd,bld->bkl', k_landmarks, k)
        kernel_3 = k * v
        mid = jnp.einsum('bkl,bld->bkd', kernel_2, kernel_3)
        output = jnp.einsum('bqk,bkd->bqd', kernel_1, mid)
        return output

    def _L2_ffn_ref(x, W1, b1, W2, b2):
        import jax, jax.numpy as jnp
        import numpy as np
        EMB = 256
        FF = 4 * EMB

        def _ternary(w):
            scale = jnp.maximum(jnp.mean(jnp.abs(w)), 1e-08)
            w_t = jnp.clip(jnp.round(w / scale), -1.0, 1.0)
            return w + jax.lax.stop_gradient(w_t - w)
        h = jnp.einsum('bsd,fd->bsf', x, _ternary(W1)) + b1
        h = jax.nn.gelu(h, approximate=False)
        out = jnp.einsum('bsf,df->bsd', h, _ternary(W2)) + b2
        return out

    def _L3_attn_ref(x, w_qkv, w_out):
        import jax, jax.numpy as jnp
        import numpy as np
        B, S, E, H = (2, 512, 256, 16)
        D = E // H
        b, s, e = x.shape
        qkv = jnp.einsum('bse,ef->bsf', x, w_qkv)
        qkv = qkv.reshape(b, s, 3, H, D).transpose(2, 0, 3, 1, 4)
        q, k, v = (qkv[0], qkv[1], qkv[2])
        scale = 1.0 / np.sqrt(D).astype(np.float32)
        scores = jnp.einsum('bhsd,bhtd->bhst', q, k) * scale
        attn = jax.nn.softmax(scores, axis=-1)
        out = jnp.einsum('bhst,bhtd->bhsd', attn, v)
        out = out.transpose(0, 2, 1, 3).reshape(b, s, e)
        return jnp.einsum('bse,ef->bsf', out, w_out)

    def _L3_ffn_ref(x, w_gate, w_up, w_down):
        import jax, jax.numpy as jnp
        import numpy as np
        BLOCK = 16
        _GRID = jnp.array([0.0, 0.5, 1.0, 1.5, 2.0, 3.0, 4.0, 6.0], dtype=jnp.float32)
        _MID = jnp.array([0.25, 0.75, 1.25, 1.75, 2.5, 3.5, 5.0], dtype=jnp.float32)

        def fp4_quant_dequant(x):
            shape = x.shape
            xb = x.reshape(shape[:-1] + (shape[-1] // BLOCK, BLOCK))
            scale = jnp.max(jnp.abs(xb), axis=-1, keepdims=True) / 6.0
            scale = jnp.maximum(scale, jnp.float32(1e-12))
            xn = xb / scale
            idx = jnp.searchsorted(_MID, jnp.abs(xn))
            q = _GRID[idx] * jnp.sign(xn) * scale
            return q.reshape(shape)

        def fp4_linear(x, w):
            xq = fp4_quant_dequant(x)
            wq = fp4_quant_dequant(w)
            return jnp.einsum('bsk,nk->bsn', xq, wq)
        gate = fp4_linear(x, w_gate)
        y = fp4_linear(x, w_up)
        h = jax.nn.silu(gate) * y
        return fp4_linear(h, w_down)
    h = _L0_tok_ref(x, L0_tok_embedding)
    h = h + _L0_attn_ref(_layernorm(h, axis=-1), L0_attn_u_w, L0_attn_u_b, L0_attn_v_w, L0_attn_v_b, L0_attn_o_w, L0_attn_o_b, L0_attn_t_zero, L0_attn_t_pos)
    h = h + _L0_ffn_ref(_layernorm(h, axis=-1), L0_ffn_router_w, L0_ffn_router_b, L0_ffn_gate_up_proj, L0_ffn_gate_up_bias, L0_ffn_down_proj, L0_ffn_down_bias)
    h = h + _L1_attn_ref(_layernorm(h, axis=-1), L1_attn_norm_w, L1_attn_wq, L1_attn_kv_down, L1_attn_wk, L1_attn_wv, L1_attn_wo)
    h = h + _L1_ffn_ref(_layernorm(h, axis=-1), L1_ffn_wg, L1_ffn_w1, L1_ffn_w2, L1_ffn_w3, L1_ffn_sw1, L1_ffn_sw2, L1_ffn_sw3)
    h = h + _L2_attn_ref(_layernorm(h, axis=-1), L2_attn_Wq, L2_attn_bq, L2_attn_Wk, L2_attn_bk, L2_attn_Wv, L2_attn_bv)
    h = h + _L2_ffn_ref(_layernorm(h, axis=-1), L2_ffn_W1, L2_ffn_b1, L2_ffn_W2, L2_ffn_b2)
    h = h + _L3_attn_ref(_layernorm(h, axis=-1), L3_attn_w_qkv, L3_attn_w_out)
    h = h + _L3_ffn_ref(_layernorm(h, axis=-1), L3_ffn_w_gate, L3_ffn_w_up, L3_ffn_w_down)
    return h

_drawn_inputs = setup_inputs


def setup_inputs(seed=0):
    import zlib

    import numpy as np

    out = dict(_drawn_inputs(seed))
    spreads = {'L1_attn_norm_w': (1.0, 0.572),
     'L2_attn_bq': (0.0, 2.0),
     'L2_attn_bk': (0.0, 2.0),
     'L2_attn_bv': (0.0, 2.0)}
    factors = {'L0_attn_u_b': 8.0,
     'L0_attn_v_b': 8.0,
     'L0_attn_t_zero': 3.274,
     'L0_ffn_router_b': 5.914,
     'L0_ffn_gate_up_bias': 8.0,
     'L0_ffn_down_bias': 3.846,
     'L2_attn_Wq': 64.0,
     'L2_attn_Wk': 64.0,
     'L2_attn_Wv': 64.0,
     'L2_ffn_b1': 8.0,
     'L2_ffn_b2': 64.0,
     'L3_attn_w_qkv': 8.0,
     'L3_attn_w_out': 8.0,
     'L3_ffn_w_gate': 8.0,
     'L3_ffn_w_up': 8.0,
     'L3_ffn_w_down': 8.0}
    for name, (base, spread) in spreads.items():
        noise = np.random.default_rng([zlib.crc32(name.encode()), seed]).standard_normal(out[name].shape)
        drawn = base * np.exp(spread * noise) if base else spread * noise
        out[name] = jnp.asarray(drawn.astype(out[name].dtype))
    for name, factor in factors.items():
        out[name] = (out[name] * factor).astype(out[name].dtype)
    return out
```

```python
import concourse.bass as bass
from concourse import mybir
from contextlib import ExitStack, contextmanager

F32 = mybir.dt.float32
I32 = mybir.dt.int32
ALU = mybir.AluOpType
ACT = mybir.ActivationFunctionType
AX = mybir.AxisListType

P = 128
B, S, D = 4, 512, 256
N = B * S
NT = N // P
TB = S // P
KD = D // P
LN_EPS = 1e-5
SIGN_BIT = -(1 << 31)


class Steps:

    def __init__(self, eng, sem, base=0):
        self.eng, self.sem, self.base, self.n = eng, sem, base, 0

    def step(self, ins):
        self.n += 1
        ins.then_inc(self.sem, 1)

    def settled(self):
        self.eng.wait_ge(self.sem, self.base + self.n)

    def link(self, ins):
        self.step(ins)
        self.settled()


def spread(ap, n):
    return ap.unsqueeze(2).broadcast_to([ap.shape[0], ap.shape[1], n])



class Fp4Scratch:

    def __init__(self, T, sb, name, n, block):
        self.half_step = T.half_step
        self.a, self.m, self.t = (sb(f"{name}_{k}", [P, n]) for k in "amt")
        self.sc, self.rc = (sb(f"{name}_{k}", [P, n // block]) for k in ("sc", "rc"))


def fp4_blocks(dve, st, x, out, tmp, block, table):
    n = x.shape[1]
    nb = n // block
    sc, rc = tmp.sc[:, 0:nb], tmp.rc[:, 0:nb]
    a, m, t = tmp.a[:, 0:n], tmp.m[:, 0:n], tmp.t[:, 0:n]

    def v(ap):
        return ap.rearrange("p (g e) -> p g e", e=block)

    st.link(dve.tensor_reduce(sc, v(x), AX.X, ALU.max, apply_absolute_value=True))
    if table:
        st.link(dve.tensor_scalar(rc, sc, 0.0, None, ALU.is_equal))
        st.link(dve.scalar_tensor_tensor(sc, sc, 1.0 / 6.0, rc, ALU.mult, ALU.add))
    else:
        st.link(dve.tensor_scalar(sc, sc, 1.0 / 6.0, 1e-12, ALU.mult, ALU.max))
    st.link(dve.reciprocal(rc, sc))
    st.link(dve.tensor_tensor(v(a), v(x), spread(rc, block), ALU.mult))
    st.link(dve.tensor_scalar(a.bitcast(I32), a.bitcast(I32), 0x7FFFFFFF, None, ALU.bitwise_and))
    st.step(dve.tensor_scalar(m, a, 1.0, None, ALU.max))
    st.link(dve.tensor_scalar(t, a, 0.25, None, ALU.is_gt))
    st.step(dve.scalar_tensor_tensor(t, a, 0.75, t, ALU.is_gt, ALU.add))
    st.link(dve.tensor_tensor(m.bitcast(I32), m.bitcast(I32), tmp.half_step[:, 0:1].broadcast_to([P, n]), ALU.add))
    st.link(dve.tensor_scalar(m.bitcast(I32), m.bitcast(I32), -0x400000, None, ALU.bitwise_and))
    st.link(dve.scalar_tensor_tensor(m, t, 0.5, m, ALU.mult, ALU.add))
    st.link(dve.scalar_tensor_tensor(v(m), v(m), -1.0, spread(sc, block), ALU.add, ALU.mult))
    st.link(dve.scalar_tensor_tensor(out.bitcast(I32), x.bitcast(I32), SIGN_BIT, m.bitcast(I32),
                                     ALU.bitwise_and, ALU.bitwise_or))



class Places:
    pass


def places(nc, ctx):
    T = Places()
    T.nc = nc
    T.sb = lambda name, shape, dt=F32: ctx.enter_context(nc.sbuf_tensor(name, shape, dt))
    T.sem = lambda name: ctx.enter_context(nc.semaphore(name))
    T.PS = ctx.enter_context(nc.psum_tensor("PS", [P, 8, 512], F32))
    T.H = T.sb("H", [P, NT * D])
    T.XT = T.sb("XT", [P, KD, N])
    T.stats = T.sb("stats", [P, 2, TB, 6])
    T.mv = T.sb("mv", [P, 2, TB, 2])
    T.var = T.sb("var", [P, 2, TB])
    T.std = T.sb("std", [P, 2, TB])
    T.rstd = T.sb("rstd", [P, 2, TB])
    T.ss = T.sb("ss", [P, 2, TB])
    T.sq = T.sb("sq", [P, D])
    T.xn = T.sb("xn", [P, 2, TB, D])
    T.ident = T.sb("ident", [P, P])
    T.tri = T.sb("tri", [P, P])
    T.ones = T.sb("ones", [P, P])
    T.half_step = T.sb("half_step", [P, 1], I32)
    T.norm_sems = [T.sem("norm_" + x) for x in ("dve_steps", "var_ready", "std_ready", "xn_ready", "transposed",
                                                "evacuated")]
    T.norms = T.norm_roots = T.norm_dve_steps = 0
    T.s_const = T.sem("s_const")
    return T


@contextmanager
def layers_semaphores(T):
    of_program, taken = T.sem, []

    def sem(name):
        taken.append(T.nc.alloc_semaphore(name=name))
        return taken[-1]
    T.sem = sem
    yield
    T.sem = of_program
    with T.nc.Block() as block:
        @block.gpsimd
        def _(pool):
            T.nc.clear_and_free_semaphores(taken)


def token_tile(T, t):
    return T.H[:, bass.ds(t * D, D)]


def constants(T):
    nc = T.nc
    made = T.sem("s_const_made")
    with nc.Block() as block:
        @block.gpsimd
        def _(pool):
            pool.memset(T.ones[:, :], 1.0).then_inc(made, 1)
            pool.memset(T.ident[:, :], 0.0).then_inc(made, 1)
            pool.wait_ge(made, 2)
            pool.affine_select(out=T.ident[:, :], in_=T.ident[:, :], compare_op=ALU.not_equal, fill=1.0,
                               base=0, pattern=[[-1, P]], channel_multiplier=1).then_inc(T.s_const, 1)
            pool.affine_select(out=T.tri[:, :], in_=T.ones[:, :], compare_op=ALU.is_gt, fill=0.0,
                               base=0, pattern=[[1, P]], channel_multiplier=-1).then_inc(T.s_const, 1)
            pool.iota(T.half_step[:, :], pattern=[[0, 1]], base=0x1FFFFF, channel_multiplier=0).then_inc(T.s_const, 1)
            pool.wait_ge(T.s_const, 3)



def embed(T, ids, table):
    nc = T.nc
    with ExitStack() as ctx:
        idx = ctx.enter_context(nc.sbuf_tensor("idx", [P, NT], I32))
        raw = ctx.enter_context(nc.sbuf_tensor("raw", [P, NT * D], F32))
        G = 4
        W = NT // G * D
        tmp = Fp4Scratch(T, lambda name, shape: ctx.enter_context(nc.sbuf_tensor(name, shape, F32)), "emb", W, 32)
        ids_in, chain = T.sem("emb_ids_in"), T.sem("emb_steps")
        rows_in = [T.sem(f"emb_rows_in{g}") for g in range(G)]
        with nc.Block() as block:
            @block.sync
            def _(sp):
                sp.dma_start(idx[:, :], ids).then_inc(ids_in, 16)

            @block.gpsimd
            def _(pool):
                pool.wait_ge(ids_in, 16)
                for t in range(NT):
                    pool.indirect_dma_start(out=raw[:, t * D:(t + 1) * D], out_offset=None, in_=table,
                                            in_offset=bass.IndirectOffsetOnAxis(ap=idx[:, t:t + 1], axis=0),
                                            ).then_inc(rows_in[t * G // NT], 16)

            @block.vector
            def _(dve):
                st = Steps(dve, chain)
                for g in range(G):
                    dve.wait_ge(rows_in[g], 16 * NT // G)
                    st.settled() if g else None
                    fp4_blocks(dve, st, raw[:, g * W:(g + 1) * W], T.H[:, g * W:(g + 1) * W], tmp, 32, True)



def norm(T, add_back=False, rms=None, col_scale=None, fp4=None, keep=None):
    nc = T.nc
    s_dve, s_var, s_std, s_xn, s_tr, s_ev = T.norm_sems
    first = T.norms == 0
    n0, r0, d0 = T.norms, T.norm_roots, T.norm_dve_steps
    roots = 2 if rms else 1
    T.norms += B
    T.norm_roots += B * roots
    T.norm_dve_steps += B * steps_of_norm(add_back, rms, fp4, keep)
    with nc.Block() as block:
        @block.vector
        def _(dve):
            def body(b, p, base):
                st = Steps(dve, s_dve, base)
                for t in range(TB):
                    st.step(dve.bn_stats(T.stats[:, p, t, :], token_tile(T, b * TB + t)))
                st.settled()
                st.step(dve.tensor_copy(T.ss[:, p, 0:1], T.ident[:, 0:1]))
                for t in range(TB):
                    st.step(dve.bn_aggr(T.mv[:, p, t, :], T.stats[:, p, t, :]))
                st.settled()
                dve.tensor_scalar(T.var[:, p, :], T.mv[:, p, :, 1], LN_EPS, None, ALU.add).then_inc(s_var, 1)
                dve.wait_ge(s_std, r0 + b * roots + 1)
                st.link(dve.reciprocal(T.rstd[:, p, :], T.std[:, p, :]))
                dve.wait_ge(s_tr, n0 + b + 1)
                for t in range(TB):
                    ins = dve.tensor_scalar(T.xn[:, p, t, :], token_tile(T, b * TB + t), T.mv[:, p, t, 0:1],
                                            T.rstd[:, p, t:t + 1], ALU.subtract, ALU.mult)
                    st.step(ins)
                st.settled()
                xn = T.xn[:, p, :, :].rearrange("p t d -> p (t d)")
                if add_back:
                    h = T.H[:, bass.ds(b * TB * D, TB * D)]
                    st.link(dve.tensor_tensor(h, h, xn, ALU.add))
                if rms:
                    for t in range(TB):
                        st.step(dve.tensor_tensor(T.sq[:, :], T.xn[:, p, t, :], T.xn[:, p, t, :], ALU.mult))
                        st.settled()
                        st.link(dve.tensor_reduce(T.ss[:, p, t:t + 1], T.sq[:, :], AX.X, ALU.add))
                    dve.tensor_scalar(T.var[:, p, :], T.ss[:, p, :], 1.0 / D, rms[0], ALU.mult, ALU.add)\
                       .then_inc(s_var, 1)
                    dve.wait_ge(s_std, r0 + b * roots + 2)
                    st.link(dve.tensor_scalar(T.std[:, p, :], T.std[:, p, :], rms[1], None, ALU.add))
                    st.link(dve.reciprocal(T.rstd[:, p, :], T.std[:, p, :]))
                    for t in range(TB):
                        st.step(dve.tensor_scalar(T.xn[:, p, t, :], T.xn[:, p, t, :], T.rstd[:, p, t:t + 1],
                                                  None, ALU.mult))
                    st.settled()
                if fp4:
                    fp4_blocks(dve, st, xn, xn, fp4, 16, False)
                if keep is not None:
                    st.link(dve.tensor_copy(keep[:, bass.ds(b * TB * D, TB * D)], xn))
                dve.nop().then_inc(s_xn, 1)
                return st.n

            with dve.Fori(0, B // 2) as i:
                k = steps_of_norm(add_back, rms, fp4, keep)
                for p in range(2):
                    n = body(i * 2 + p, p, d0 + (i * 2 + p) * k)
                    assert n == k, (n, k)

        @block.scalar
        def _(act):
            if first:
                act.sem_inc(s_ev, 2)
            with act.Fori(0, B // 2) as i:
                for p in range(2):
                    b = i * 2 + p
                    for r in range(roots):
                        act.wait_ge(s_var, r0 + b * roots + r + 1)
                        act.activation(T.std[:, p, :], T.var[:, p, :], ACT.Sqrt).then_inc(s_std, 1)
                    act.wait_ge(s_tr, n0 + b + 3)
                    for k in range(KD):
                        out, src = T.XT[:, k, bass.ds(b * S, S)], T.PS[:, 2 * p + k, :]
                        if col_scale is None:
                            ins = act.activation(out, src, ACT.Copy)
                        else:
                            ins = act.activation(out, src, ACT.Copy, scale=col_scale[:, k:k + 1])
                    ins.then_inc(s_ev, 1)

        @block.tensor
        def _(pe):
            pe.wait_ge(T.s_const, 2)
            if first:
                pe.sem_inc(s_tr, 2)
            with pe.Fori(0, B // 2) as i:
                for p in range(2):
                    b = i * 2 + p
                    pe.wait_ge(s_xn, n0 + b + 1)
                    pe.wait_ge(s_ev, n0 + b + 1)
                    for t in range(TB):
                        for k in range(KD):
                            ins = pe.transpose(T.PS[:, 2 * p + k, t * P:(t + 1) * P],
                                               T.xn[:, p, t, k * P:(k + 1) * P], T.ident[:, :])
                    ins.then_inc(s_tr, 1)


FP4_STEPS = 13


def steps_of_norm(add_back, rms, fp4, keep):
    n = 2 * TB + 2 + TB + (keep is not None)
    n += bool(add_back)
    n += (3 * TB + 2) if rms else 0
    n += FP4_STEPS if fp4 else 0
    return n



D1 = 512
TH = 8


def toeplitz_attention(T, w):
    nc = T.nc
    F = D1 // P
    JOBS = 2 * F
    with ExitStack() as ctx:
        def sb(name, shape):
            return ctx.enter_context(nc.sbuf_tensor("ta_" + name, shape, F32))

        uT = sb("uT", [P, 2, F, B, P])
        vT = sb("vT", [P, 2, F, B, P])
        y = sb("y", [P, 2, F, B, P])
        s_uv, s_act, s_y, s_out, s_h = (T.sem("ta_" + x) for x in (
            "uv_in_bank", "uv_evacuated", "y_steps", "out_in_bank", "h_added"))
        YS = 5 * F
        with nc.Block() as block:
            @block.tensor
            def _(pe):
                w.wait(pe, "l0_uv", "l0_o", "l0_ob")
                pe.sem_inc(s_out, 4)
                with pe.Fori(0, TB // 2) as i:
                    for p in range(2):
                        c = i * 2 + p
                        for n in range(JOBS):
                            f = n // 2 + (F if n % 2 == 0 else 0)
                            pe.wait_ge(s_act, c * JOBS + n + 1)
                            for k in range(KD):
                                x = T.XT[:, k, :].rearrange("p (b s) -> p b s", b=B)[:, :, bass.ds(c * P, P)]
                                ins = pe.matmul(T.PS[:, n % 4, :], w.l0_uv[:, k, f * P:(f + 1) * P], x,
                                                start=(k == 0), stop=(k == KD - 1))
                            ins.then_inc(s_uv, 1)
                        pe.wait_ge(s_y, c * YS + YS)
                        for g in range(2):
                            pe.wait_ge(s_h, c * 2 + g + 1)
                            for b in range(2 * g, 2 * g + 2):
                                bank = T.PS[:, 4 + 2 * p + g, (b % 2) * D:(b % 2 + 1) * D]
                                pe.matmul(bank, T.ones[0:1, :], w.l0_ob[0:1, :], start=True, stop=False)
                                for f in range(F):
                                    ins = pe.matmul(bank, y[:, p, f, b, :], w.l0_o[:, f, :],
                                                    start=False, stop=(f == F - 1))
                            ins.then_inc(s_out, 1)

            @block.scalar
            def _(act):
                w.wait(act, "l0_uvb")
                act.sem_inc(s_act, 4)
                with act.Fori(0, TB // 2) as i:
                    for p in range(2):
                        c = i * 2 + p
                        act.wait_ge(s_out, 2 * c + 2)
                        for n in range(JOBS):
                            f = n // 2
                            act.wait_ge(s_uv, c * JOBS + n + 1)
                            out = (uT if n % 2 else vT)[:, p, f, :, :]
                            act.activation(out, T.PS[:, n % 4, :].rearrange("p (b s) -> p b s", b=B), ACT.Silu,
                                           bias=w.l0_uvb[:, f + (0 if n % 2 else F):f + (1 if n % 2 else F + 1)])\
                               .then_inc(s_act, 1)

            @block.vector
            def _(dve):
                w.wait(dve, "l0_t")
                dve.sem_inc(s_h, 4)
                with dve.Fori(0, TB // 2) as i:
                    for p in range(2):
                        c = i * 2 + p
                        st = Steps(dve, s_y, c * YS)
                        dve.wait_ge(s_out, 2 * c + 2)
                        for f in range(F):
                            dve.wait_ge(s_act, c * JOBS + 2 * f + 5)
                            v, o = vT[:, p, f, :, :], y[:, p, f, :, :]
                            st.link(dve.tensor_scalar(o, v, w.l0_t[:, f, 0:1], None, ALU.mult))
                            for d in range(1, B):
                                st.link(dve.scalar_tensor_tensor(o[:, d:B, :], v[:, 0:B - d, :], w.l0_t[:, f, d:d + 1],
                                                                 o[:, d:B, :], ALU.mult, ALU.add))
                            dve.wait_ge(s_act, c * JOBS + 2 * f + 6)
                            st.step(dve.tensor_tensor(o, o, uT[:, p, f, :, :], ALU.mult))
                        for g in range(2):
                            dve.wait_ge(s_out, 4 + 2 * c + g + 1)
                            for b in range(2 * g, 2 * g + 2):
                                h = token_tile(T, c + b * TB)
                                ins = dve.tensor_tensor(h, h, T.PS[:, 4 + 2 * p + g, (b % 2) * D:(b % 2 + 1) * D],
                                                        ALU.add)
                            ins.then_inc(s_h, 1)



TOPK = 4
E1 = 32
CAP = int(1.25 * N * TOPK / E1)


def over(ap, n):
    return ap.unsqueeze(1).broadcast_to([ap.shape[0], n, ap.shape[1]])


def top4(dve, st, s, mask, code, m, c, sels, low):
    n, e = s.shape[1], s.shape[2]
    for r, sel in enumerate(sels):
        st.link(dve.tensor_reduce(m, s, AX.X, ALU.max))
        st.link(dve.tensor_tensor(c, s, spread(m, e), ALU.is_equal))
        st.link(dve.tensor_tensor(c, c, over(code, n), ALU.mult))
        st.link(dve.tensor_reduce(m, c, AX.X, ALU.max))
        st.link(dve.tensor_tensor(sel, c, spread(m, e), ALU.is_equal))
        st.step(dve.scalar_tensor_tensor(s, sel, -low, s, ALU.mult, ALU.add))
        if r == 0:
            st.link(dve.tensor_copy(mask, sel))
        else:
            st.link(dve.tensor_tensor(mask, mask, sel, ALU.add))


def code_row(T, pool, s_made, irow, row, e):
    pool.iota(irow, pattern=[[-1, e]], base=e, channel_multiplier=0).then_inc(s_made, 1)
    pool.wait_ge(s_made, 1)
    pool.tensor_copy(row, irow).then_inc(s_made, 1)


def router0(T, w, SC):
    nc = T.nc
    E = 16
    with ExitStack() as ctx:
        def sb(name, shape, dt=F32):
            return ctx.enter_context(nc.sbuf_tensor("r0_" + name, shape, dt))

        irow, code = sb("irow", [P, E], I32), sb("code", [P, E])
        m, m0, c, sel = sb("m", [P, NT]), sb("m0", [P, NT]), sb("c", [P, NT, E]), sb("sel", [P, NT, E])
        lg, s, mask = sb("lg", [P, NT, E]), sb("s", [P, NT, E]), sb("mask", [P, NT, E])
        scT = sb("scT", [E, N])
        s_code, s_lg, s_x, s_e, s_dve, s_t, s_tc, s_o, s_h = (T.sem("r0_" + x) for x in (
            "code_made", "logits_in_bank", "shifted", "exp_done", "dve_steps", "scores_transposed",
            "scores_copied", "bias_in_bank", "h_added"))
        with nc.Block() as block:
            @block.gpsimd
            def _(pool):
                code_row(T, pool, s_code, irow[:, :], code[:, :], E)

            @block.tensor
            def _(pe):
                w.wait(pe, "l0_rw", "l0_rb", "l0_db")
                for t in range(NT):
                    out = T.PS[:, 0, t * E:(t + 1) * E]
                    pe.matmul(out, T.ones[0:1, :], w.l0_rb[0:1, :], start=True, stop=False)
                    for k in range(KD):
                        ins = pe.matmul(out, T.XT[:, k, t * P:(t + 1) * P], w.l0_rw[:, k, :],
                                        start=False, stop=(k == KD - 1))
                ins.then_inc(s_lg, 1)
                pe.wait_ge(s_dve, 8 + 7 * TOPK)
                for t in range(NT):
                    ins = pe.transpose(T.PS[0:E, 4 + t // 4, (t % 4) * P:(t % 4 + 1) * P], SC[:, t, :], T.ident[:, :])
                ins.then_inc(s_t, 1)
                pe.wait_ge(s_tc, 1)
                for t in range(NT):
                    if t % 2 == 0 and t >= 8:
                        pe.wait_ge(s_h, t // 2 - 3)
                    ins = pe.matmul(T.PS[:, t // 2 % 4, (t % 2) * D:(t % 2 + 1) * D], scT[:, t * P:(t + 1) * P],
                                    w.l0_db[:, :], start=True, stop=True)
                    if t % 2:
                        ins.then_inc(s_o, 1)

            @block.scalar
            def _(act):
                act.wait_ge(s_x, 1)
                act.activation(lg[:, :, :], lg[:, :, :], ACT.Exp).then_inc(s_e, 1)
                act.wait_ge(s_t, 1)
                act.activation(scT[:, :], T.PS[0:E, 4:8, :].rearrange("p a b -> p (a b)"), ACT.Copy).then_inc(s_tc, 1)

            @block.vector
            def _(dve):
                st = Steps(dve, s_dve)
                dve.wait_ge(s_lg, 1)
                st.step(dve.tensor_copy(lg[:, :, :], T.PS[:, 0, 0:NT * E].rearrange("p (t e) -> p t e", e=E)))
                st.link(dve.tensor_copy(s[:, :, :], T.PS[:, 0, 0:NT * E].rearrange("p (t e) -> p t e", e=E)))
                st.link(dve.tensor_reduce(m0[:, :], s[:, :, :], AX.X, ALU.max))
                dve.wait_ge(s_code, 2)
                st.link(dve.tensor_tensor(lg[:, :, :], lg[:, :, :], spread(m0[:, :], E), ALU.subtract))
                dve.nop().then_inc(s_x, 1)
                top4(dve, st, s[:, :, :], mask[:, :, :], code[:, :], m[:, :], c[:, :, :], [sel[:, :, :]] * TOPK, 1e38)
                dve.wait_ge(s_e, 1)
                st.link(dve.tensor_tensor(lg[:, :, :], lg[:, :, :], mask[:, :, :], ALU.mult))
                st.link(dve.tensor_reduce(m[:, :], lg[:, :, :], AX.X, ALU.add))
                st.link(dve.reciprocal(m[:, :], m[:, :]))
                st.link(dve.tensor_tensor(SC, lg[:, :, :], spread(m[:, :], E), ALU.mult))
                assert st.n == 8 + 7 * TOPK
                for g in range(NT // 2):
                    dve.wait_ge(s_o, g + 1)
                    h = token_tile(T, 2 * g)
                    h = T.H[:, 2 * g * D:(2 * g + 2) * D]
                    dve.tensor_tensor(h, h, T.PS[:, g % 4, :], ALU.add).then_inc(s_h, 1)


def router1(T, w, weight, dest, index):
    nc = T.nc
    E, G = E1, 8
    with ExitStack() as ctx:
        def sb(name, shape, dt=F32):
            return ctx.enter_context(nc.sbuf_tensor("r1_" + name, shape, dt))

        irow, code = sb("irow", [P, E], I32), sb("code", [P, E])
        m, c, sel = sb("m", [P, NT]), sb("c", [P, NT, E]), sb("sel", [P, TOPK, NT, E])
        place, destf, offset = sb("place", [P, NT, E]), sb("destf", [P, TOPK * NT]), sb("offset", [P, E])
        pr, s, mask = sb("pr", [P, NT, E]), sb("s", [P, NT, E]), sb("mask", [P, NT, E])
        gs, keep, gc, gsel = (sb(x, [P, NT, G]) for x in ("gs", "keep", "gc", "gsel"))
        before = sb("before", [P, NT, E])
        s_code, s_lg, s_x, s_e, s_dve, s_p = (T.sem("r1_" + x) for x in (
            "code_made", "logits_in_bank", "shifted", "exp_done", "dve_steps", "places_in_bank"))
        PLACED = 3 + 2 + 1 + 7 * TOPK + 3 + 7 * TOPK + NT
        with nc.Block() as block:
            @block.gpsimd
            def _(pool):
                code_row(T, pool, s_code, irow[:, :], code[:, :], E)

            @block.tensor
            def _(pe):
                w.wait(pe, "l1_wg")
                for t in range(NT):
                    for k in range(KD):
                        ins = pe.matmul(T.PS[:, 0, t * E:(t + 1) * E], T.XT[:, k, t * P:(t + 1) * P],
                                        w.l1_wg[:, k, :], start=(k == 0), stop=(k == KD - 1))
                ins.then_inc(s_lg, 1)
                pe.wait_ge(s_dve, PLACED)
                for t in range(NT):
                    out = T.PS[:, 1, t * E:(t + 1) * E]
                    pe.matmul(out, T.ones[:, :], before[:, t, :], start=True, stop=False)
                    ins = pe.matmul(out, T.tri[:, :], mask[:, t, :], start=False, stop=True)
                ins.then_inc(s_p, 1)

            @block.scalar
            def _(act):
                act.wait_ge(s_x, 1)
                act.activation(pr[:, :, :], pr[:, :, :], ACT.Exp).then_inc(s_e, 1)

            @block.vector
            def _(dve):
                st = Steps(dve, s_dve)
                dve.wait_ge(s_lg, 1)
                lg = T.PS[:, 0, 0:NT * E].rearrange("p (t e) -> p t e", e=E)
                st.link(dve.tensor_reduce(m[:, :], lg, AX.X, ALU.max))
                st.link(dve.tensor_tensor(pr[:, :, :], lg, spread(m[:, :], E), ALU.subtract))
                dve.nop().then_inc(s_x, 1)
                dve.wait_ge(s_e, 1)
                st.link(dve.tensor_reduce(m[:, :], pr[:, :, :], AX.X, ALU.add))
                st.link(dve.reciprocal(m[:, :], m[:, :]))
                st.link(dve.tensor_tensor(pr[:, :, :], pr[:, :, :], spread(m[:, :], E), ALU.mult))
                groups = pr[:, :, :].rearrange("p t (g e) -> p (t g) e", g=G)
                st.link(dve.tensor_reduce(gs[:, :, :].rearrange("p t g -> p (t g)"), groups, AX.X, ALU.max))
                dve.wait_ge(s_code, 2)
                top4(dve, st, gs[:, :, :], keep[:, :, :], code[:, E - G:E], m[:, :], gc[:, :, :],
                     [gsel[:, :, :]] * TOPK, 3.0)
                kg = keep[:, :, :].rearrange("p t g -> p (t g)")
                s4 = s[:, :, :].rearrange("p t (g e) -> p (t g) e", g=G)
                st.link(dve.tensor_tensor(s4, groups, spread(kg, E // G), ALU.mult))
                st.link(dve.tensor_scalar(gc[:, :, :], keep[:, :, :], 1.0, None, ALU.subtract))
                st.link(dve.tensor_tensor(s4, s4, spread(gc[:, :, :].rearrange("p t g -> p (t g)"), E // G), ALU.add))
                top4(dve, st, s[:, :, :], mask[:, :, :], code[:, :], m[:, :], c[:, :, :],
                     [sel[:, r, :, :] for r in range(TOPK)], 3.0)
                st.link(dve.memset(before[:, 0, :], 0.0))
                for t in range(1, NT):
                    st.link(dve.tensor_tensor(before[:, t, :], before[:, t - 1, :], mask[:, t - 1, :], ALU.add))
                assert st.n == PLACED, st.n
                st.link(dve.tensor_tensor(pr[:, :, :], pr[:, :, :], mask[:, :, :], ALU.mult))
                st.link(dve.tensor_reduce(m[:, :], pr[:, :, :], AX.X, ALU.add))
                st.link(dve.tensor_scalar(m[:, :], m[:, :], 1e-9, None, ALU.add))
                st.link(dve.reciprocal(m[:, :], m[:, :]))
                st.link(dve.tensor_tensor(pr[:, :, :], pr[:, :, :], spread(m[:, :], E), ALU.mult))
                dve.wait_ge(s_p, 1)
                count = T.PS[:, 1, 0:NT * E].rearrange("p (t e) -> p t e", e=E)
                st.step(dve.tensor_scalar(offset[:, :], code[:, :], float(E), -float(CAP), ALU.subtract, ALU.mult))
                st.step(dve.scalar_tensor_tensor(pr[:, :, :], count, float(CAP), pr[:, :, :], ALU.is_lt, ALU.mult))
                st.link(dve.tensor_scalar(place[:, :, :], count, float(CAP), float(2 * E * CAP), ALU.is_ge, ALU.mult))
                st.link(dve.tensor_tensor(place[:, :, :], place[:, :, :], count, ALU.add))
                st.link(dve.tensor_tensor(place[:, :, :], place[:, :, :], over(offset[:, :], NT), ALU.add))
                for r in range(TOPK):
                    one_hot = sel[:, r, :, :]
                    st.step(dve.tensor_tensor(c[:, :, :], one_hot, place[:, :, :], ALU.mult))
                    st.link(dve.tensor_tensor(one_hot, one_hot, pr[:, :, :], ALU.mult))
                    st.step(dve.tensor_reduce(destf[:, r * NT:(r + 1) * NT], c[:, :, :], AX.X, ALU.add))
                    st.link(dve.tensor_reduce(weight[:, r, :], one_hot, AX.X, ALU.add))
                st.link(dve.tensor_copy(dest[:, :], destf[:, :]))
                st.link(dve.tensor_scalar(destf[:, :], destf[:, :], float(E * CAP - 1), None, ALU.min))
                st.link(dve.tensor_copy(index[:, :], destf[:, :]))



EI = 256
CH = N // S


def experts(T, w, name, SC, E, w13_dram, w2_dram, clipped_bias=None, on_pool=None):
    nc = T.nc
    F = EI // P
    LIMIT, ALPHA = 7.0, 1.702
    with ExitStack() as ctx:
        def sb(nm, shape):
            return ctx.enter_context(nc.sbuf_tensor(name + nm, shape, F32))

        w13, w2 = sb("w13", [P, 2, KD, 2 * EI]), sb("w2", [P, 2, F, D])
        g, u, sg = sb("g", [P, 2, S]), sb("u", [P, 2, S]), sb("sg", [P, 2, S])
        hT = sb("hT", [P, 2, F, S])
        s_w = [T.sem(f"{name}weights_in{q}") for q in range(2)]
        s_gu, s_free, s_sg, s_h, s_dn, s_add, s_pool = (T.sem(name + x) for x in (
            "gate_up_in_bank", "gate_up_read", "gate_activated", "h_ready", "down_in_bank", "h_added",
            "pool_steps"))
        UN = CH * F
        DN = CH * 2

        def all_experts(eng, body):
            if E > 1:
                with eng.Fori(0, E // 2) as i:
                    for q in range(2):
                        body(i * 2 + q, q, i)
            if E % 2:
                body(E - 1, 0, E // 2)

        with nc.Block() as block:
            @block.sync
            def _(sp):
                def body(e, q, i):
                    sp.wait_ge(s_dn, e * DN + DN + 1)
                    sp.dma_start(w13[:, q, :, :], w13_dram[bass.ds(e * P, P), :, :]).then_inc(s_w[q], 16)
                    sp.dma_start(w2[:, q, :, :], w2_dram[bass.ds(e * P, P), :, :]).then_inc(s_w[q], 16)
                all_experts(sp, body)

            @block.tensor
            def _(pe):
                pe.sem_inc(s_dn, 2 * DN + 1)

                def body(e, q, i):
                    pe.wait_ge(s_w[q], i * 32 + 32)

                    def gate_up(c):
                        for f in range(F):
                            n = e * UN + c * F + f
                            pe.wait_ge(s_h if clipped_bias is None else s_free, n + 1)
                            for a in range(2):
                                for k in range(KD):
                                    ins = pe.matmul(T.PS[:, 2 * f + a, :],
                                                    w13[:, q, k, a * EI + f * P:a * EI + (f + 1) * P],
                                                    T.XT[:, k, c * S:(c + 1) * S], start=(k == 0), stop=(k == KD - 1))
                            ins.then_inc(s_gu, 1)

                    def down(c):
                        pe.wait_ge(s_h, e * UN + c * F + F + 2)
                        for m in range(2):
                            pe.wait_ge(s_add, e * DN + c * 2 + m + 1)
                            for t in range(2 * m, 2 * m + 2):
                                out = T.PS[:, 4 + (2 * c + m) % 4, (t % 2) * D:(t % 2 + 1) * D]
                                for f in range(F):
                                    ins = pe.matmul(out, hT[:, c % 2, f, t * P:(t + 1) * P], w2[:, q, f, :],
                                                    start=(f == 0), stop=(f == F - 1))
                            ins.then_inc(s_dn, 1)

                    gate_up(0)
                    for c in range(1, CH):
                        gate_up(c)
                        down(c - 1)
                    down(CH - 1)
                all_experts(pe, body)

            @block.scalar
            def _(act):
                def body(e, q, i):
                    for c in range(CH):
                        for f in range(F):
                            n = e * UN + c * F + f
                            if clipped_bias is None:
                                act.wait_ge(s_gu, n + 1)
                                act.wait_ge(s_h, n + 1)
                                act.activation(sg[:, f, :], T.PS[:, 2 * f, :], ACT.Silu).then_inc(s_sg, 1)
                            else:
                                act.wait_ge(s_free, n + 3)
                                act.wait_ge(s_h, n + 1)
                                act.activation(sg[:, f, :], g[:, f, :], ACT.Sigmoid, scale=ALPHA).then_inc(s_sg, 1)
                all_experts(act, body)

            if on_pool:
                @block.gpsimd
                def _(pool):
                    on_pool(pool)

            if clipped_bias is not None:
                @block.gpsimd
                def _(pool):
                    pool.sem_inc(s_h, 2)

                    def body(e, q, i):
                        for c in range(CH):
                            for f in range(F):
                                n = e * UN + c * F + f
                                pool.wait_ge(s_sg, n + 1)
                                pool.tensor_tensor(g[:, f, :], g[:, f, :], sg[:, f, :], ALU.mult).then_inc(s_pool, 1)
                                pool.tensor_scalar(u[:, f, :], u[:, f, :], -LIMIT, 1.0, ALU.max, ALU.add)\
                                    .then_inc(s_pool, 1)
                                pool.wait_ge(s_pool, 2 * n + 2)
                                pool.wait_ge(s_dn, e * DN + 2 * c + 2 * DN - 1)
                                pool.tensor_tensor(hT[:, c % 2, f, :], g[:, f, :], u[:, f, :], ALU.mult)\
                                    .then_inc(s_h, 1)
                    all_experts(pool, body)

            @block.vector
            def _(dve):
                if clipped_bias is not None:
                    w.wait(dve, "l0_gub")
                dve.sem_inc(s_free, 2)
                dve.sem_inc(s_add, 4)
                if clipped_bias is None:
                    dve.sem_inc(s_h, 2)

                def body(e, q, i):
                    def unit(c):
                        for f in range(F):
                            n = e * UN + c * F + f
                            if clipped_bias is None:
                                dve.wait_ge(s_sg, n + 1)
                                dve.wait_ge(s_dn, e * DN + 2 * c + 2 * DN - 1)
                                dve.tensor_tensor(hT[:, c % 2, f, :], sg[:, f, :], T.PS[:, 2 * f + 1, :],
                                                  ALU.mult).then_inc(s_h, 1)
                            else:
                                dve.wait_ge(s_gu, n + 1)
                                dve.wait_ge(s_h, n + 1)
                                dve.tensor_scalar(g[:, f, :], T.PS[:, 2 * f, :], clipped_bias[:, one(e), f],
                                                  LIMIT, ALU.add, ALU.min)
                                dve.tensor_scalar(u[:, f, :], T.PS[:, 2 * f + 1, :], clipped_bias[:, one(e), 2 + f],
                                                  LIMIT, ALU.add, ALU.min).then_inc(s_free, 1)

                    def add(c):
                        for m in range(2):
                            dve.wait_ge(s_dn, e * DN + c * 2 + m + 2 * DN + 2)
                            for t in range(2 * m, 2 * m + 2):
                                h = token_tile(T, c * TB + t)
                                ins = dve.scalar_tensor_tensor(
                                    h, T.PS[:, 4 + (2 * c + m) % 4, (t % 2) * D:(t % 2 + 1) * D],
                                    SC[:, c * TB + t, one(e)], h, ALU.mult, ALU.add)
                            ins.then_inc(s_add, 1)

                    unit(0)
                    for c in range(1, CH):
                        unit(c)
                        add(c - 1)
                    add(CH - 1)
                all_experts(dve, body)


def one(e):
    return bass.ds(e, 1)



RING = 3


def dispatch(pool, xn, dest, rows, zeroed, s_scattered):
    pool.wait_ge(*zeroed)
    for t in range(NT):
        for r in range(TOPK):
            pool.indirect_dma_start(out=rows,
                                    out_offset=bass.IndirectOffsetOnAxis(ap=dest[:, r * NT + t:r * NT + t + 1], axis=0),
                                    in_=xn[:, t * D:(t + 1) * D], in_offset=None,
                                    bounds_check=E1 * CAP - 1, oob_is_err=False).then_inc(s_scattered, 16)


def routed_experts(T, w13_dram, w2_dram, rows, results, s_scattered):
    nc = T.nc
    F = EI // P
    TILES = [(c, min(P, CAP - c)) for c in range(0, CAP, P)]
    C = len(TILES)
    FULL = CAP // P
    with ExitStack() as ctx:
        def sb(nm, shape):
            return ctx.enter_context(nc.sbuf_tensor("re_" + nm, shape, F32))

        w13, w2 = sb("w13", [P, RING, KD, 2 * EI]), sb("w2", [P, RING, F, D])
        xe, xeT = sb("xe", [P, RING, C, D]), sb("xeT", [P, RING, KD, CAP])
        sg, hT, ot = sb("sg", [P, F, CAP]), sb("hT", [P, RING, F, CAP]), sb("ot", [P, RING, C, D])
        s_w, s_xe, s_st = ([T.sem(f"re_{x}{q}") for q in range(RING)] for x in ("weights_in", "rows_in", "stored"))
        s_t, s_xt, s_gu, s_sg, s_h, s_dn, s_ev = (T.sem("re_" + x) for x in (
            "rows_transposed", "xeT_ready", "gate_up_in_bank", "gate_activated", "h_ready", "down_in_bank",
            "results_copied"))

        def steps(eng, body):
            body(0, 0, 0, True, False)
            with eng.Fori(0, (E1 - 2) // RING) as i:
                for j in range(1, RING + 1):
                    body(i * RING + j, j % RING, i + j // RING, False, False)
            body(E1 - 1, (E1 - 1) % RING, (E1 - 1) // RING, False, True)

        with nc.Block() as block:
            @block.sync
            def _(sp):
                for q in range(RING):
                    sp.sem_inc(s_st[q], 1)

                def load(e, q, first=False):
                    sp.wait_ge(s_dn, e + 1)
                    sp.dma_start(w13[:, q, :, :], w13_dram[bass.ds(e * P, P), :, :]).then_inc(s_w[q], 16)
                    sp.dma_start(w2[:, q, :, :], w2_dram[bass.ds(e * P, P), :, :]).then_inc(s_w[q], 16)
                    if first:
                        sp.wait_ge(s_scattered, 16 * NT * TOPK)
                    move(e, q, xe, rows, s_xe, False)

                def move(e, q, buf, dram, sem, store):
                    full = buf[:, q, 0:FULL, :], dram[bass.ds(e * CAP, FULL * P), :].rearrange("(c p) d -> p c d", p=P)
                    rest = buf[0:CAP - FULL * P, q, FULL, :], dram[bass.ds(e * CAP + FULL * P, CAP - FULL * P), :]
                    for a, b in (full, rest):
                        if store:
                            a, b = b, a
                        sp.dma_start(a, b).then_inc(sem[q], 16)

                def body(e, q):
                    sp.wait_ge(s_ev, e + 2)
                    move(e, q, ot, results, s_st, True)
                    load(e + RING, q)

                for e in range(RING):
                    load(e, e, e == 0)
                for e in range(2):
                    body(e, e)
                with sp.Fori(0, (E1 - RING - 2) // RING) as i:
                    for j in range(2, RING + 2):
                        body(i * RING + j, j % RING)
                for e in range(E1 - RING, E1):
                    sp.wait_ge(s_ev, e + 2)
                    move(e, e % RING, ot, results, s_st, True)
                for q in range(RING):
                    sp.wait_ge(s_st[q], 32 * len(range(q, E1, RING)) + 1)

            @block.tensor
            def _(pe):
                pe.sem_inc(s_dn, RING)

                def turn(e, q, u):
                    pe.wait_ge(s_xe[q], u * 32 + 32)
                    pe.wait_ge(s_xt, e + 1)
                    for k in range(KD):
                        for c, (c0, m) in enumerate(TILES):
                            ins = pe.transpose(T.PS[:, k, c0:c0 + m], xe[0:m, q, c, k * P:(k + 1) * P],
                                               T.ident[0:m, 0:m])
                    ins.then_inc(s_t, 1)

                def gate_up(e, q, u):
                    pe.wait_ge(s_w[q], u * 32 + 32)
                    pe.wait_ge(s_xt, e + 2)
                    for f in range(F):
                        pe.wait_ge(s_h, e * F + f + 1)
                        for a in range(2):
                            for k in range(KD):
                                c = a * EI + f * P
                                ins = pe.matmul(T.PS[:, 2 + 2 * f + a, 0:CAP], w13[:, q, k, c:c + P],
                                                xeT[:, q, k, :], start=(k == 0), stop=(k == KD - 1))
                        ins.then_inc(s_gu, 1)

                def down(e, q):
                    pe.wait_ge(s_h, e * F + 2 * F)
                    pe.wait_ge(s_ev, e + 1)
                    for c, (c0, m) in enumerate(TILES):
                        for f in range(F):
                            ins = pe.matmul(T.PS[0:m, 6 + c // 2, c % 2 * D:(c % 2 + 1) * D], hT[:, q, f, c0:c0 + m],
                                            w2[:, q, f, :], start=(f == 0), stop=(f == F - 1))
                    ins.then_inc(s_dn, 1)

                def body(e, q, u, first, last):
                    gate_up(e, q, u)
                    if not last:
                        turn(e + 1, (q + 1) % RING, u + (q + 1) // RING)
                    if not first:
                        down(e - 1, (q - 1) % RING)
                turn(0, 0, 0)
                steps(pe, body)
                down(E1 - 1, (E1 - 1) % RING)

            @block.scalar
            def _(act):
                act.sem_inc(s_xt, 1)

                def transposed(e, q):
                    act.wait_ge(s_t, e + 1)
                    act.activation(xeT[:, q, :, :], T.PS[:, 0:KD, 0:CAP], ACT.Copy).then_inc(s_xt, 1)

                def body(e, q, u, first, last):
                    for f in range(F):
                        act.wait_ge(s_gu, e * F + f + 1)
                        act.wait_ge(s_h, e * F + f + 1)
                        act.activation(sg[:, f, :], T.PS[:, 2 + 2 * f, 0:CAP], ACT.Silu).then_inc(s_sg, 1)
                    if not last:
                        transposed(e + 1, (q + 1) % RING)
                transposed(0, 0)
                steps(act, body)

            @block.vector
            def _(dve):
                dve.sem_inc(s_h, F)
                dve.sem_inc(s_ev, 1)

                def results_out(e, q, u):
                    dve.wait_ge(s_st[q], u * 32 + 1)
                    dve.wait_ge(s_dn, e + RING + 1)
                    dve.tensor_copy(ot[:, q, 0:2, :].rearrange("p c d -> p (c d)"), T.PS[:, 6, :])
                    m = TILES[2][1]
                    dve.tensor_copy(ot[0:m, q, 2, :], T.PS[0:m, 7, 0:D]).then_inc(s_ev, 1)

                def body(e, q, u, first, last):
                    for f in range(F):
                        dve.wait_ge(s_sg, e * F + f + 1)
                        dve.tensor_tensor(hT[:, q, f, :], sg[:, f, :], T.PS[:, 3 + 2 * f, 0:CAP],
                                          ALU.mult).then_inc(s_h, 1)
                    if not first:
                        before = (q - 1) % RING
                        results_out(e - 1, before, u if before < q else u - 1)
                steps(dve, body)
                results_out(E1 - 1, (E1 - 1) % RING, (E1 - 1) // RING)


def zero_places(T, rows):
    nc = T.nc
    s_made, s_zeroed = T.sem("zeros_made"), T.sem("rows_zeroed")
    zeros = T.zeros = T.sb("zeros", [P, 8 * D])
    part = E1 * CAP // P * D // zeros.shape[1]
    view = rows.rearrange("(a p c) d -> a p (c d)", p=P, a=part)
    with nc.Block() as block:
        @block.vector
        def _(dve):
            dve.memset(zeros[:, :], 0.0).then_inc(s_made, 1)

        @block.scalar
        def _(act):
            act.wait_ge(s_made, 1)
            for a in range(part):
                act.dma_start(view[a], zeros[:, :]).then_inc(s_zeroed, 16)
    return s_zeroed, 16 * part


def routed_layer(T, w, w13_dram, w2_dram, rows, results, zeroed):
    nc = T.nc
    with ExitStack() as ctx:
        def sb(nm, shape, dt=F32):
            return ctx.enter_context(nc.sbuf_tensor("rl_" + nm, shape, dt))

        weight, dest, index = sb("weight", [P, TOPK, NT]), sb("dest", [P, TOPK * NT], I32), sb("index", [P, TOPK * NT], I32)
        s_scattered = T.sem("rl_rows_scattered")
        with nc.sbuf_tensor("rl_xn", [P, NT * D], F32) as xn:
            norm(T, keep=xn)
            router1(T, w, weight, dest, index)
            with nc.sbuf_tensor("rl_one", [P, NT, 1], F32) as shared_weight:
                with nc.Block() as block:
                    @block.vector
                    def _(dve):
                        s = T.sem("rl_one_made")
                        dve.memset(shared_weight[:, :, :], 1.0).then_inc(s, 1)
                        dve.wait_ge(s, 1)
                shared = slice(E1 * P, (E1 + 1) * P)
                experts(T, w, "e1_", shared_weight, 1, w13_dram[shared, :, :], w2_dram[shared, :, :],
                        on_pool=lambda pool: dispatch(pool, xn, dest, rows, zeroed, s_scattered))
            routed_experts(T, w13_dram, w2_dram, rows, results, s_scattered)
        combine(T, results, index, weight)


def combine(T, results, index, weight):
    nc = T.nc
    SLOTS = 4
    with nc.sbuf_tensor("cb_rows", [P, SLOTS, TOPK * D], F32) as rows:
        s_in = [T.sem(f"cb_rows_in{q}") for q in range(SLOTS)]
        s_add, s_sum = T.sem("cb_added"), T.sem("cb_steps")
        with nc.Block() as block:
            @block.gpsimd
            def _(pool):
                for t in range(NT):
                    if t >= SLOTS:
                        pool.wait_ge(s_add, t - SLOTS + 1)
                    for r in range(TOPK):
                        pool.indirect_dma_start(
                            out=rows[:, t % SLOTS, r * D:(r + 1) * D], out_offset=None, in_=results,
                            in_offset=bass.IndirectOffsetOnAxis(ap=index[:, r * NT + t:r * NT + t + 1], axis=0),
                        ).then_inc(s_in[t % SLOTS], 16)

            @block.vector
            def _(dve):
                st = Steps(dve, s_sum)
                for t in range(NT):
                    dve.wait_ge(s_in[t % SLOTS], 16 * TOPK * (t // SLOTS + 1))
                    h = token_tile(T, t)
                    for r in range(TOPK):
                        ins = dve.scalar_tensor_tensor(h, rows[:, t % SLOTS, r * D:(r + 1) * D],
                                                       weight[:, r, t:t + 1], h, ALU.mult, ALU.add)
                        if r < TOPK - 1:
                            st.link(ins)
                    ins.then_inc(s_add, 1)



HG = 4
GROUPS = 4


def attention(T, w, name, rope, dv, w_dram, kv=None, tables=None):
    nc = T.nc
    KK = 1 if kv is not None else KD
    UQ = 2 if rope else 1
    U = 2 * UQ
    QW = UQ * 2 * P
    WQ, WK, WV = KD * QW, KK * QW, KK * HG * dv
    KO = max(1, HG * dv // P)
    PO = min(P, HG * dv)
    NCH = TB * HG * dv // P
    WW = WQ + WK + WV + KO * D
    X = TB * HG
    PB = 8
    OB = X * dv // 512 if X * dv >= 512 else 1
    STEPS = B * GROUPS
    with ExitStack() as ctx:
        def sb(nm, shape):
            return ctx.enter_context(nc.sbuf_tensor(name + nm, shape, F32))

        ww = sb("ww", [P, 2, WW])
        xs = sb("xs", [P, KK, S])
        qk = sb("qk", [P, 2, 2, S])
        rt = sb("rt", [P, 2 * U, S]) if rope else None
        vs = sb("vs", [P, TB, HG * dv])
        nm, rs, rr = sb("nm", [P, X]), sb("rs", [P, X]), sb("rr", [P, X])
        pe_, pt = sb("p", [P, PB, S]), sb("pt", [P, 4, S])
        o, oT = sb("o", [P, X, dv]), sb("oT", [P, NCH, P])
        s_w = [T.sem(f"{name}weights_in{p}") for p in range(2)]
        (s_src, s_unit, s_v, s_read, s_vs, s_s, s_m, s_exp, s_pt, s_ped, s_pea, s_pv, s_on, s_otr, s_ot, s_o,
         s_add, s_chain) = (T.sem(name + x) for x in (
             "source_copied", "qk_unit_in_banks", "v_in_bank", "qk_unit_read", "v_ready", "scores_in_bank",
             "max_ready", "exp_done", "p_transposed", "pt_even_ready", "pt_odd_ready", "pv_done", "o_normalised",
             "o_transposed", "oT_ready", "out_in_bank", "h_added", "dve_steps"))
        s_qks = T.sem(name + "qk_turned") if rope else s_read
        READS = 2 if rope else 1

        def steps(eng, first, body):
            if first:
                first((0, 0, 0, 0))
            with eng.Fori(0, STEPS // 2 - 1) as i:
                a, b, c = (i * 2, 0, i, i // 2), (i * 2 + 1, 1, i, i // 2), (i * 2 + 2, 0, i + 1, (i + 1) // 2)
                body(a, b)
                body(b, c)
            i = STEPS // 2 - 1
            a, b = (i * 2, 0, i, i // 2), (i * 2 + 1, 1, i, i // 2)
            body(a, b)
            body(b, None)

        with nc.Block() as block:
            @block.sync
            def _(sp):
                def body(n, p, i, b):
                    sp.wait_ge(s_o, n + 1)
                    group = i % 2 * 2 + p
                    sp.dma_start(ww[:, p, :], w_dram[bass.ds(group * P, P), :]).then_inc(s_w[p], 16)
                    sp.wait_ge(s_v, n + 1)
                    src = T.XT[:, :, bass.ds(b * S, S)] if kv is None else kv[:, bass.ds(b * S, S)]
                    dst = xs[:, :, :] if kv is None else xs[:, 0, :]
                    sp.dma_start(dst, src).then_inc(s_src, 16)
                with sp.Fori(0, STEPS // 2) as i:
                    for p in range(2):
                        body(i * 2 + p, p, i, i // 2)

            if rope:
                @block.gpsimd
                def _(pool):
                    def turned(n):
                        for u in range(U):
                            pool.wait_ge(s_read, 2 * (U * n + u) + 2)
                            pool.tensor_tensor(qk[:, u // 2, u % 2, :], rt[:, 2 * u, :], rt[:, 2 * u + 1, :],
                                               ALU.add).then_inc(s_qks, 1)
                    with pool.Fori(0, STEPS) as n:
                        turned(n)

            @block.tensor
            def _(pe):
                pe.sem_inc(s_o, 2)
                pe.sem_inc(s_v, 1)
                pe.sem_inc(s_pt, PB)
                pe.sem_inc(s_pv, 4)

                def weights(p):
                    return (ww[:, p, 0:WQ].rearrange("p (k m) -> p k m", k=KD),
                            ww[:, p, WQ:WQ + WK].rearrange("p (k m) -> p k m", k=KK),
                            ww[:, p, WQ + WK:WQ + WK + WV].rearrange("p (k m) -> p k m", k=KK),
                            ww[:, p, WQ + WK + WV:WW].rearrange("p (k m) -> p k m", k=KO))

                def unit(step, u):
                    n, p, i, b = step
                    if u == 0:
                        pe.wait_ge(s_w[p], i * 16 + 16)
                    if u < 2:
                        pe.wait_ge(s_exp, X * n + X - 2 + 2 * u)
                    else:
                        pe.wait_ge(s_read, READS * (U * n + u - 1))
                    j = u // UQ
                    kk = KD if j == 0 else KK
                    for a in range(2):
                        for k in range(kk):
                            rhs = (T.XT[:, k, bass.ds(b * S, S)] if j == 0 or kv is None
                                   else kv[:, bass.ds(b * S, S)])
                            c = (u % UQ * 2 + a) * P
                            ins = pe.matmul(T.PS[:, 2 * (u % 2) + a, :], weights(p)[j][:, k, c:c + P],
                                            rhs, start=(k == 0), stop=(k == kk - 1))
                    ins.then_inc(s_unit, 1)

                def values(step):
                    n, p, i, b = step
                    wv = weights(p)[2]
                    pe.wait_ge(s_src, n * 16 + 16)
                    pe.wait_ge(s_read, READS * (U * n + U - 1))
                    for t in range(TB):
                        for k in range(KK):
                            c = t * HG * dv
                            ins = pe.matmul(T.PS[:, c // 512, c % 512:c % 512 + HG * dv],
                                            xs[:, k, t * P:(t + 1) * P], wv[:, k, :], start=(k == 0), stop=(k == KK - 1))
                    ins.then_inc(s_v, 1)

                def scores(n, x):
                    qt, h = x // HG, x % HG
                    if qt:
                        pe.wait_ge(s_exp, X * n + X + x - HG + 1)
                    r = slice(64 * (h % 2), 64 * (h % 2) + 64)
                    pe.matmul(T.PS[:, h, :], qk[r, 0, h // 2, qt * P:(qt + 1) * P], qk[r, 1, h // 2, :],
                              start=True, stop=True).then_inc(s_s, 1)

                def first_scores(n):
                    pe.wait_ge(s_qks, U * n + U)
                    pe.wait_ge(s_vs, n + 1)
                    for h in range(HG):
                        scores(n, h)

                def turn(n, x):
                    pe.wait_ge(s_exp, X * n + X + x + 1)
                    pe.wait_ge((s_ped, s_pea)[x % 2], X // 2 * n + x // 2 + 1)
                    for k in range(TB):
                        ins = pe.transpose(T.PS[:, 4 + x % 2, k * P:(k + 1) * P],
                                           pe_[:, x % PB, k * P:(k + 1) * P], T.ident[:, :])
                    ins.then_inc(s_pt, 1)

                def times_v(n, x):
                    h = x % HG
                    pe.wait_ge((s_ped, s_pea)[x % 2], X // 2 * n + x // 2 + 2)
                    if x == 0:
                        pe.wait_ge(s_add, n + 1)
                    c = x * dv
                    for k in range(TB):
                        ins = pe.matmul(T.PS[:, 6 + c // 512, c % 512:c % 512 + dv],
                                        pt[:, x % 4, k * P:(k + 1) * P], vs[:, k, h * dv:(h + 1) * dv],
                                        start=(k == 0), stop=(k == TB - 1))
                    ins.then_inc(s_pv, 1)

                def first(step):
                    for u in range(U):
                        unit(step, u)
                    values(step)
                    first_scores(0)

                def body(step, after):
                    n, p, i, b = step
                    wo = weights(p)[3]
                    for x in range(X):
                        turn(n, x)
                        if x + HG < X:
                            scores(n, x + HG)
                        if x:
                            times_v(n, x - 1)
                        if after and x in (X - 3, X - 1):
                            unit(after, (x - X + 3) // 2)
                    times_v(n, X - 1)
                    if after:
                        for u in range(2, U):
                            unit(after, u)
                        values(after)
                    pe.wait_ge(s_on, n + 1)
                    of = o[:, :, :].rearrange("p x d -> p (x d)")
                    for j in range(NCH):
                        ins = pe.transpose(T.PS[:, 4 + j // 4, j % 4 * P:(j % 4 + 1) * P],
                                           of[:, j * P:(j + 1) * P], T.ident[:, :])
                    ins.then_inc(s_otr, 1)
                    if after:
                        first_scores(after[0])
                    pe.wait_ge(s_ot, n + 1)
                    for t in range(TB):
                        for k in range(KO):
                            r = slice(0, P) if PO == P else slice(t % 2 * PO, (t % 2 + 1) * PO)
                            j = t * KO + k if PO == P else t // 2
                            bank, half = (t // 2, t % 2) if PO == P else (t % 2, t // 2)
                            ins = pe.matmul(T.PS[:, 6 + bank, half * D:(half + 1) * D],
                                            oT[r, j, :], wo[r, k, :], start=(k == 0), stop=(k == KO - 1))
                    ins.then_inc(s_o, 1)
                steps(pe, first, body)

            @block.scalar
            def _(act):
                act.sem_inc(s_exp, X)
                act.sem_inc(s_pea, 1)

                def values(n):
                    act.wait_ge(s_v, n + 2)
                    src = (T.PS[:, 0:2, :].rearrange("p a b -> p (a b)") if TB * HG * dv == 1024
                           else T.PS[:, 0, 0:TB * HG * dv])
                    act.activation(vs[:, :, :].rearrange("p t c -> p (t c)"), src, ACT.Copy).then_inc(s_vs, 1)

                def exp(n, x):
                    act.wait_ge(s_m, X * n + x + 1)
                    act.wait_ge(s_pt, X * n + x + 1)
                    act.activation(pe_[:, x % PB, :], T.PS[:, x % HG, :], ACT.Exp, bias=nm[:, x:x + 1],
                                   accum_out=rs[:, x:x + 1]).then_inc(s_exp, 1)

                def evacuate(n, x):
                    act.wait_ge(s_pt, X * n + PB + x + 1)
                    act.wait_ge(s_pv, X * n + x + 1)
                    act.activation(pt[:, x % 4, :], T.PS[:, 5, :], ACT.Copy).then_inc(s_pea, 1)

                def first(step):
                    values(0)
                    for h in range(HG):
                        exp(0, h)

                def body(step, after):
                    n = step[0]
                    for x in range(0, X, 2):
                        for h in range(HG, HG + 2):
                            if x + h < X:
                                exp(n, x + h)
                        evacuate(n, x + 1)
                    if after:
                        values(after[0])
                    act.wait_ge(s_otr, n + 1)
                    src = T.PS[:, 4:6, :].rearrange("p a b -> p (a b)") if NCH > 4 else T.PS[:, 4, 0:NCH * P]
                    act.activation(oT[:, :, :].rearrange("p j q -> p (j q)"), src, ACT.Copy).then_inc(s_ot, 1)
                    if after:
                        for h in range(HG):
                            exp(after[0], h)
                steps(act, first, body)

            @block.vector
            def _(dve):
                if tables is not None:
                    w.wait(dve, "l1_rope")
                dve.sem_inc(s_ped, 1)
                dve.sem_inc(s_add, 1)

                def unit(n, u):
                    dve.wait_ge(s_unit, U * n + u + 1)
                    if rope:
                        for a in range(2):
                            dve.tensor_tensor(rt[:, 2 * u + a, :], T.PS[:, 2 * (u % 2) + a, :],
                                              tables[:, u // 2 * 2 + a, :], ALU.mult).then_inc(s_read, 1)
                    else:
                        dve.tensor_scalar(qk[:, u, :, :], T.PS[:, 2 * u:2 * u + 2, :], (1.0, 0.25)[u], None,
                                          ALU.mult).then_inc(s_read, 1)

                def maximum(n, x):
                    dve.wait_ge(s_s, X * n + x + 1)
                    dve.tensor_reduce(nm[:, x:x + 1], T.PS[:, x % HG, :], AX.X, ALU.max, negate=True).then_inc(s_m, 1)

                def evacuate(n, x):
                    dve.wait_ge(s_pt, X * n + PB + x + 1)
                    dve.wait_ge(s_pv, X * n + x + 1)
                    dve.tensor_copy(pt[:, x % 4, :], T.PS[:, 4, :]).then_inc(s_ped, 1)

                def first(step):
                    for u in range(U):
                        unit(0, u)
                    for h in range(HG):
                        maximum(0, h)

                def body(step, after):
                    n, p, i, b = step
                    for x in range(0, X, 2):
                        evacuate(n, x)
                        for h in range(HG, HG + 2):
                            if x + h < X:
                                maximum(n, x + h)
                        if after and x == X - 4:
                            unit(after[0], 0)
                    dve.wait_ge(s_exp, X * n + 2 * X)
                    dve.reciprocal(rr[:, :], rs[:, :]).then_inc(s_chain, 1)
                    if after:
                        unit(after[0], 1)
                    dve.wait_ge(s_chain, n + 1)
                    dve.wait_ge(s_pv, X * n + X + 4)
                    XB = X // OB
                    for a in range(OB):
                        ins = dve.tensor_tensor(o[:, a * XB:(a + 1) * XB, :],
                                                T.PS[:, 6 + a, 0:XB * dv].rearrange("p (x d) -> p x d", d=dv),
                                                spread(rr[:, a * XB:(a + 1) * XB], dv), ALU.mult)
                    ins.then_inc(s_on, 1)
                    if after:
                        for u in range(2, U):
                            unit(after[0], u)
                        for h in range(HG):
                            maximum(after[0], h)
                    dve.wait_ge(s_o, n + 3)
                    h = T.H[:, bass.ds(b * TB * D, TB * D)]
                    if PO == P:
                        out = T.PS[:, 6:8, :].rearrange("p a b -> p (a b)")
                    else:
                        h = h.rearrange("p (t d) -> p t d", d=D)
                        out = T.PS[:, 6:8, :].rearrange("p a (b d) -> p b a d", d=D)
                        h = h.rearrange("p (b a) d -> p b a d", a=2)
                    dve.tensor_tensor(h, h, out, ALU.add).then_inc(s_add, 1)
                steps(dve, first, body)


def compress_kv(T, w, kv):
    nc = T.nc
    s_kv, s_done = T.sem("kv_in_bank"), T.sem("kv_ready")
    with nc.Block() as block:
        @block.tensor
        def _(pe):
            w.wait(pe, "l1_kvd")
            for c in range(CH):
                for k in range(KD):
                    ins = pe.matmul(T.PS[:, c, :], w.l1_kvd[:, k, :], T.XT[:, k, c * S:(c + 1) * S],
                                    start=(k == 0), stop=(k == KD - 1))
                ins.then_inc(s_kv, 1)

        @block.scalar
        def _(act):
            for c in range(CH):
                act.wait_ge(s_kv, c + 1)
                act.activation(kv[:, c * S:(c + 1) * S], T.PS[:, c, :], ACT.Copy).then_inc(s_done, 1)
            act.wait_ge(s_done, CH)



LM = 64


def landmark_attention(T, w):
    nc = T.nc
    with ExitStack() as ctx:
        def sb(nm, shape):
            return ctx.enter_context(nc.sbuf_tensor("la_" + nm, shape, F32))

        xs = sb("xs", [P, 2, KD, S])
        e = sb("e", [P, 2 * TB, D])
        k3 = sb("k3", [P, TB, D])
        nm, rs, rr = sb("nm", [P, 2 * TB]), sb("rs", [P, 2 * TB]), sb("rr", [P, 2 * TB])
        qT, kT, klT = sb("qT", [P, KD, S]), sb("kT", [P, KD, S]), sb("klT", [P, KD, LM])
        k2T, mid, k1T = sb("k2T", [P, TB, LM]), sb("mid", [LM, D]), sb("k1T", [LM, S])
        LT = LM // TB
        s_xs = [T.sem(f"la_x_arrived{p}") for p in range(2)]
        s_qk, s_v, s_m, s_e, s_n, s_k3, s_kl, s_tq, s_tk, s_klT, s_qT, s_kT, s_k2, s_k2T, s_k1, s_k1T, \
            s_mid, s_midT, s_o, s_add, s_steps = (T.sem("la_" + x) for x in (
                "qk_in_bank", "v_in_bank", "max_ready", "exp_done", "qk_normalised", "k3_ready",
                "landmarks_in_bank", "q_transposed", "k_transposed", "klT_ready", "qT_ready", "kT_ready",
                "k2_in_bank", "k2T_ready", "k1_in_bank", "k1T_ready", "mid_in_bank", "mid_ready", "out_in_bank",
                "h_added", "dve_steps"))

        def steps(eng, body):
            with eng.Fori(0, B // 2) as i:
                for p in range(2):
                    body(i * 2 + p, p, i)

        with nc.Block() as block:
            @block.sync
            def _(sp):
                def body(b, p, i):
                    sp.wait_ge(s_v, b + 1)
                    sp.dma_start(xs[:, p, :, :], T.XT[:, :, bass.ds(b * S, S)]).then_inc(s_xs[p], 16)
                steps(sp, body)

            @block.tensor
            def _(pe):
                w.wait(pe, "l2_w", "l2_b", "l2_avg")
                pe.sem_inc(s_v, 2)

                def body(b, p, i):
                    pe.wait_ge(s_xs[p], 16 * i + 16)
                    pe.wait_ge(s_qT, b + 1)
                    pe.wait_ge(s_kT, b + 1)
                    for t in range(TB):
                        out = T.PS[:, t, :]
                        pe.matmul(out, T.ones[0:1, :], w.l2_b[0:1, 0:2 * D], start=True, stop=False)
                        for k in range(KD):
                            ins = pe.matmul(out, xs[:, p, k, t * P:(t + 1) * P], w.l2_w[:, k, 0:2 * D],
                                            start=False, stop=(k == KD - 1))
                        ins.then_inc(s_qk, 1)
                    pe.wait_ge(s_add, b + 1)
                    for t in range(TB):
                        out = T.PS[:, 4 + t // 2, (t % 2) * D:(t % 2 + 1) * D]
                        pe.matmul(out, T.ones[0:1, :], w.l2_b[0:1, 2 * D:3 * D], start=True, stop=False)
                        for k in range(KD):
                            ins = pe.matmul(out, xs[:, p, k, t * P:(t + 1) * P], w.l2_w[:, k, 2 * D:3 * D],
                                            start=False, stop=(k == KD - 1))
                    ins.then_inc(s_v, 1)
                    pe.wait_ge(s_n, b + 1)
                    for t in range(TB):
                        for k in range(KD):
                            c = k * LM + t * LT
                            ins = pe.matmul(T.PS[:, 6, c:c + LT], e[:, 2 * t + 1, k * P:(k + 1) * P],
                                            w.l2_avg[:, :], start=True, stop=True)
                    ins.then_inc(s_kl, 1)
                    for j, s_t in ((1, s_tk), (0, s_tq)):
                        for t in range(TB):
                            for k in range(KD):
                                ins = pe.transpose(T.PS[:, 2 * j + k, t * P:(t + 1) * P],
                                                   e[:, 2 * t + j, k * P:(k + 1) * P], T.ident[:, :])
                        ins.then_inc(s_t, 1)
                    pe.wait_ge(s_kT, b + 2)
                    pe.wait_ge(s_klT, b + 1)
                    for t in range(TB):
                        for k in range(KD):
                            ins = pe.matmul(T.PS[:, 7, t * LM:(t + 1) * LM], kT[:, k, t * P:(t + 1) * P],
                                            klT[:, k, :], start=(k == 0), stop=(k == KD - 1))
                    ins.then_inc(s_k2, 1)
                    pe.wait_ge(s_qT, b + 2)
                    pe.wait_ge(s_k3, b + 1)
                    for k in range(KD):
                        ins = pe.matmul(T.PS[0:LM, 4, :], klT[:, k, :], qT[:, k, :],
                                        start=(k == 0), stop=(k == KD - 1))
                    ins.then_inc(s_k1, 1)
                    pe.wait_ge(s_k2T, b + 1)
                    for t in range(TB):
                        ins = pe.matmul(T.PS[0:LM, 6, D:2 * D], k2T[:, t, :], k3[:, t, :],
                                        start=(t == 0), stop=(t == TB - 1))
                    ins.then_inc(s_mid, 1)
                    pe.wait_ge(s_k1T, b + 1)
                    pe.wait_ge(s_midT, b + 1)
                    for t in range(TB):
                        ins = pe.matmul(T.PS[:, 4 + t // 2, (t % 2) * D:(t % 2 + 1) * D], k1T[:, t * P:(t + 1) * P],
                                        mid[:, :], start=True, stop=True)
                    ins.then_inc(s_o, 1)
                steps(pe, body)

            @block.scalar
            def _(act):
                act.sem_inc(s_qT, 1)

                def body(b, p, i):
                    for t in range(TB):
                        act.wait_ge(s_m, TB * b + t + 1)
                        for j in range(2):
                            ins = act.activation(e[:, 2 * t + j, :], T.PS[:, t, j * D:(j + 1) * D], ACT.Exp,
                                                 bias=nm[:, 2 * t + j:2 * t + j + 1],
                                                 accum_out=rs[:, 2 * t + j:2 * t + j + 1])
                            ins.then_inc(s_e, 1)
                    act.wait_ge(s_kl, b + 1)
                    act.activation(klT[:, :, :].rearrange("p k l -> p (k l)"), T.PS[:, 6, 0:KD * LM],
                                   ACT.Copy).then_inc(s_klT, 1)
                    act.wait_ge(s_tq, b + 1)
                    act.activation(qT[:, :, :], T.PS[:, 0:2, :], ACT.Copy).then_inc(s_qT, 1)
                    act.wait_ge(s_k2, b + 1)
                    act.activation(k2T[:, :, :].rearrange("p t l -> p (t l)"), T.PS[:, 7, 0:TB * LM],
                                   ACT.Copy).then_inc(s_k2T, 1)
                    act.wait_ge(s_mid, b + 1)
                    act.activation(mid[:, :], T.PS[0:LM, 6, D:2 * D], ACT.Copy).then_inc(s_midT, 1)
                steps(act, body)

            @block.vector
            def _(dve):
                dve.sem_inc(s_kT, 1)
                dve.sem_inc(s_add, 1)

                def body(b, p, i):
                    for t in range(TB):
                        dve.wait_ge(s_qk, TB * b + t + 1)
                        dve.tensor_reduce(nm[:, 2 * t:2 * t + 2], T.PS[:, t, :].rearrange("p (j d) -> p j d", j=2),
                                          AX.X, ALU.max, negate=True).then_inc(s_m, 1)
                    st = Steps(dve, s_steps, b * 1)
                    dve.wait_ge(s_e, 2 * TB * b + 2 * TB)
                    st.link(dve.reciprocal(rr[:, :], rs[:, :]))
                    dve.tensor_tensor(e[:, :, :], e[:, :, :], spread(rr[:, :], D), ALU.mult).then_inc(s_n, 1)
                    dve.wait_ge(s_v, b + 3)
                    dve.wait_ge(s_n, b + 1)
                    ke = e[:, :, :].rearrange("p (t j) d -> p t j d", j=2)[:, :, 1, :]
                    dve.tensor_tensor(k3[:, :, :], ke, T.PS[:, 4:6, :].rearrange("p a (b d) -> p (a b) d", d=D),
                                      ALU.mult).then_inc(s_k3, 1)
                    dve.wait_ge(s_tk, b + 1)
                    dve.tensor_copy(kT[:, :, :], T.PS[:, 2:4, :]).then_inc(s_kT, 1)
                    dve.wait_ge(s_k1, b + 1)
                    dve.tensor_copy(k1T[:, :], T.PS[0:LM, 4, :]).then_inc(s_k1T, 1)
                    dve.wait_ge(s_o, b + 1)
                    h = T.H[:, bass.ds(b * TB * D, TB * D)]
                    dve.tensor_tensor(h, h, T.PS[:, 4:6, :].rearrange("p a b -> p (a b)"), ALU.add).then_inc(s_add, 1)
                steps(dve, body)



FF = 4 * D
MAGIC = 1.5 * 2 ** 23


def ternary_ffn(T, w):
    nc = T.nc
    FT = FF // P
    with ExitStack() as ctx:
        def sb(nm, shape):
            return ctx.enter_context(nc.sbuf_tensor("tf_" + nm, shape, F32))

        WN = KD * FF
        part, sc, rc = sb("part", [P, 2]), sb("sc", [P, 2]), sb("rc", [P, 2])
        q = sb("q", [P, 2, WN])
        hT = sb("hT", [P, 2, FT, S])
        s_part, s_total, s_steps, s_t = (T.sem("tf_" + x) for x in (
            "sums_of_partitions", "totals_in_bank", "dve_steps", "ternary_ready"))
        s_h, s_g, s_o, s_add = (T.sem("tf_" + x) for x in ("h_in_bank", "gelu_done", "out_in_bank", "h_added"))
        with nc.Block() as block:
            @block.tensor
            def _(pe):
                pe.wait_ge(s_part, 1)
                pe.matmul(T.PS[:, 0, 0:2], T.ones[:, :], part[:, :], start=True, stop=True).then_inc(s_total, 1)
                w.wait(pe, "l2_b2")
                pe.wait_ge(s_t, 2)
                pe.sem_inc(s_o, 4)

                with pe.Fori(0, CH // 2) as i:
                    for p in range(2):
                        c = i * 2 + p
                        for f in range(FT):
                            pe.wait_ge(s_g, FT * c + f + 1)
                            for k in range(KD):
                                ins = pe.matmul(T.PS[:, f % 4, :], w.l2_w1[:, k, f * P:(f + 1) * P],
                                                T.XT[:, k, bass.ds(c * S, S)], start=(k == 0), stop=(k == KD - 1))
                            ins.then_inc(s_h, 1)
                        pe.wait_ge(s_g, FT * c + FT + 4)
                        for g in range(2):
                            pe.wait_ge(s_add, 2 * c + g + 1)
                            for t in range(2 * g, 2 * g + 2):
                                out = T.PS[:, 4 + 2 * p + g, (t % 2) * D:(t % 2 + 1) * D]
                                pe.matmul(out, T.ones[0:1, :], w.l2_b2[0:1, :], start=True, stop=False)
                                for f in range(FT):
                                    ins = pe.matmul(out, hT[:, p, f, t * P:(t + 1) * P], w.l2_w2[:, f, :],
                                                    start=False, stop=(f == FT - 1))
                            ins.then_inc(s_o, 1)

            @block.scalar
            def _(act):
                w.wait(act, "l2_b1")
                act.sem_inc(s_g, 4)
                with act.Fori(0, CH // 2) as i:
                    for p in range(2):
                        c = i * 2 + p
                        act.wait_ge(s_o, 2 * c + 2)
                        for f in range(FT):
                            act.wait_ge(s_h, FT * c + f + 1)
                            act.activation(hT[:, p, f, :], T.PS[:, f % 4, :], ACT.Gelu,
                                           bias=w.l2_b1[:, f:f + 1]).then_inc(s_g, 1)

            @block.vector
            def _(dve):
                w.wait(dve, "l2_w1", "l2_w2")
                st = Steps(dve, s_steps)
                flat = [w.l2_w1[:, :, :].rearrange("p k n -> p (k n)"), w.l2_w2[:, :, :].rearrange("p k n -> p (k n)")]
                for j in range(2):
                    st.step(dve.tensor_reduce(part[:, j:j + 1], flat[j], AX.X, ALU.add, apply_absolute_value=True))
                st.settled()
                st.link(dve.tensor_copy(sc[:, :], part[:, :]))
                dve.nop().then_inc(s_part, 1)
                dve.wait_ge(s_total, 1)
                st.link(dve.tensor_scalar(sc[:, :], T.PS[:, 0, 0:2], 1.0 / (FF * D), 1e-8, ALU.mult, ALU.max))
                st.link(dve.reciprocal(rc[:, :], sc[:, :]))
                for j in range(2):
                    st.link(dve.tensor_scalar(q[:, j, :], flat[j], rc[:, j:j + 1], MAGIC, ALU.mult, ALU.add))
                    st.link(dve.tensor_scalar(q[:, j, :], q[:, j, :], MAGIC, 1.0, ALU.subtract, ALU.min))
                    st.link(dve.tensor_scalar(q[:, j, :], q[:, j, :], -1.0, None, ALU.max))
                    st.link(dve.tensor_tensor(q[:, j, :], q[:, j, :], flat[j], ALU.subtract))
                    dve.tensor_tensor(flat[j], flat[j], q[:, j, :], ALU.add).then_inc(s_t, 1)
                dve.sem_inc(s_add, 4)
                with dve.Fori(0, CH // 2) as i:
                    for p in range(2):
                        c = i * 2 + p
                        for g in range(2):
                            dve.wait_ge(s_o, 4 + 2 * c + g + 1)
                            h = T.H[:, bass.ds((c * TB + 2 * g) * D, 2 * D)]
                            dve.tensor_tensor(h, h, T.PS[:, 4 + 2 * p + g, :], ALU.add).then_inc(s_add, 1)



I3 = 704
FT3 = -(-I3 // P)


def fp4_weights(T, w, tmp, wgT, wdT):
    nc = T.nc
    s_q, s_steps, s_tr, s_ev = (T.sem("q3_" + x) for x in ("quantised", "dve_steps", "transposed", "evacuated"))
    R = FT3 * D

    with nc.Block() as block:
        @block.vector
        def _(dve):
            w.wait(dve, "l3_wg", "l3_wu", "l3_wd")
            st = Steps(dve, s_steps)
            for m, n in ((w.l3_wg, R), (w.l3_wu, R), (w.l3_wd, KD * I3)):
                flat = m[:, :, :].rearrange("p k n -> p (k n)")
                for a in range(0, n, n // 2):
                    fp4_blocks(dve, st, flat[:, a:a + n // 2], flat[:, a:a + n // 2], tmp, 16, False)
                dve.nop().then_inc(s_q, 1)

        @block.tensor
        def _(pe):
            job = 0
            for j, m in enumerate((w.l3_wg, w.l3_wu)):
                pe.wait_ge(s_q, j + 1)
                for k in range(KD):
                    for half in range(2):
                        if job >= 4:
                            pe.wait_ge(s_ev, job - 3)
                        for r in range(3):
                            ins = pe.transpose(T.PS[:, job % 4, r * P:(r + 1) * P],
                                               m[:, half * 3 + r, k * P:(k + 1) * P], T.ident[:, :])
                        ins.then_inc(s_tr, 1)
                        job += 1
            pe.wait_ge(s_q, 3)
            for f in range(FT3):
                n = min(P, I3 - f * P)
                pe.wait_ge(s_ev, job - 3)
                for k in range(KD):
                    ins = pe.transpose(T.PS[0:n, job % 4, k * P:(k + 1) * P], w.l3_wd[:, k, f * P:f * P + n],
                                       T.ident[:, :])
                ins.then_inc(s_tr, 1)
                job += 1

        @block.scalar
        def _(act):
            job = 0
            for j in range(2):
                for k in range(KD):
                    for half in range(2):
                        act.wait_ge(s_tr, job + 1)
                        act.activation(wgT[:, k, j, half * 3 * P:(half + 1) * 3 * P], T.PS[:, job % 4, 0:3 * P],
                                       ACT.Copy).then_inc(s_ev, 1)
                        job += 1
            for f in range(FT3):
                n = min(P, I3 - f * P)
                act.wait_ge(s_tr, job + 1)
                act.activation(wdT[0:n, f, :], T.PS[0:n, job % 4, 0:D], ACT.Copy).then_inc(s_ev, 1)
                job += 1


def fp4_ffn(T, w, tmp, wgT, wdT, out):
    nc = T.nc
    HI = I3 // 2
    with ExitStack() as ctx:
        def sb(nm, shape):
            return ctx.enter_context(nc.sbuf_tensor("f3_" + nm, shape, F32))

        xs = sb("xs", [P, 2, KD, P])
        sg, h, hT = sb("sg", [P, 2, I3]), sb("h", [P, 2, I3]), sb("hT", [P, 2, FT3, P])
        s_xs = [T.sem(f"f3_x_arrived{p}") for p in range(2)]
        s_gu, s_sg, s_hm, s_q, s_steps, s_tr, s_ev, s_o, s_add, s_out = (T.sem("f3_" + x) for x in (
            "gate_up_in_bank", "silu_done", "product_done", "quantised", "dve_steps", "h_transposed",
            "hT_ready", "out_in_bank", "h_added", "out_written"))
        ST = FP4_STEPS

        def steps(eng, body, last=None):
            with eng.Fori(0, NT // 2 - 1) as i:
                for p in range(2):
                    body(i * 2 + p, p, i)
            body(NT - 2, 0, NT // 2 - 1)
            (last or body)(NT - 1, 1, NT // 2 - 1)

        with nc.Block() as block:
            @block.sync
            def _(sp):
                def body(n, p, i):
                    sp.wait_ge(s_gu, n + 1)
                    sp.dma_start(xs[:, p, :, :], T.XT[:, :, bass.ds(n * P, P)]).then_inc(s_xs[p], 16)
                steps(sp, body)

            @block.tensor
            def _(pe):
                pe.sem_inc(s_gu, 2)

                def gate_up(n, p, i):
                    pe.wait_ge(s_xs[p], 16 * i + 16)
                    pe.wait_ge(s_hm, n + 1)
                    for j in range(2):
                        for a in range(2):
                            for k in range(KD):
                                ins = pe.matmul(T.PS[:, 2 * j + a, 0:HI], xs[:, p, k, :],
                                                wgT[:, k, j, a * HI:(a + 1) * HI], start=(k == 0), stop=(k == KD - 1))
                    ins.then_inc(s_gu, 1)

                def rest(n, p, i=None):
                    pe.wait_ge(s_q, n + 1)
                    pe.wait_ge(s_ev, n + 1)
                    for f in range(FT3):
                        m = min(P, I3 - f * P)
                        ins = pe.transpose(T.PS[0:m, 4 + f // 4, f % 4 * P:(f % 4 + 1) * P],
                                           h[:, p, f * P:f * P + m], T.ident[:, :])
                    ins.then_inc(s_tr, 1)
                    pe.wait_ge(s_ev, n + 2)
                    pe.wait_ge(s_add, n + 1)
                    for f in range(FT3):
                        m = min(P, I3 - f * P)
                        ins = pe.matmul(T.PS[:, 6 + p, 0:D], hT[0:m, p, f, :], wdT[0:m, f, :],
                                        start=(f == 0), stop=(f == FT3 - 1))
                    ins.then_inc(s_o, 1)

                def body(n, p, i):
                    gate_up(n + 1, 1 - p, i + p)
                    rest(n, p)
                gate_up(0, 0, 0)
                steps(pe, body, rest)

            @block.scalar
            def _(act):
                act.sem_inc(s_ev, 1)

                def silu(n, p):
                    act.wait_ge(s_gu, n + 3)
                    act.wait_ge(s_hm, n + 1)
                    act.activation(sg[:, p, :].rearrange("p (a n) -> p a n", a=2), T.PS[:, 0:2, 0:HI],
                                   ACT.Silu).then_inc(s_sg, 1)

                def rest(n, p, i=None):
                    act.wait_ge(s_tr, n + 1)
                    act.activation(hT[:, p, 0:5, :].rearrange("p f q -> p (f q)")[:, 0:512], T.PS[:, 4, :], ACT.Copy)
                    act.activation(hT[:, p, 4, :], T.PS[:, 5, 0:P], ACT.Copy)
                    act.activation(hT[0:64, p, 5, :], T.PS[0:64, 5, P:2 * P], ACT.Copy).then_inc(s_ev, 1)

                def body(n, p, i):
                    silu(n + 1, 1 - p)
                    rest(n, p)
                silu(0, 0)
                steps(act, body, rest)

            @block.vector
            def _(dve):
                dve.sem_inc(s_hm, 1)
                dve.sem_inc(s_add, 2)

                def product(n, p):
                    dve.wait_ge(s_sg, n + 1)
                    dve.tensor_tensor(h[:, p, :].rearrange("p (a n) -> p a n", a=2),
                                      sg[:, p, :].rearrange("p (a n) -> p a n", a=2), T.PS[:, 2:4, 0:HI],
                                      ALU.mult).then_inc(s_hm, 1)

                def rest(n, p, i=None):
                    st = Steps(dve, s_steps, n * ST)
                    dve.wait_ge(s_hm, n + 2)
                    fp4_blocks(dve, st, h[:, p, :], h[:, p, :], tmp, 16, False)
                    dve.nop().then_inc(s_q, 1)
                    assert st.n == ST

                def add(n, p, i=None):
                    dve.wait_ge(s_o, n + 1)
                    ht = token_tile(T, n)
                    dve.tensor_tensor(ht, ht, T.PS[:, 6 + p, 0:D], ALU.add).then_inc(s_add, 1)

                product(0, 0)
                rest(0, 0)

                def body(n, p, i):
                    product(n + 1, 1 - p)
                    rest(n + 1, 1 - p)
                    add(n, p)
                steps(dve, body, add)

            @block.gpsimd
            def _(pool):
                def body(n, p, i):
                    pool.wait_ge(s_add, n + 3)
                    pool.dma_start(out[bass.ds(n * P, P), :], token_tile(T, n)).then_inc(s_out, 16)
                steps(pool, body)
                pool.wait_ge(s_out, 16 * NT)



class Weights:

    def __init__(self, T, only=None):
        self.T, self.only, self.tensors = T, only, {}
        self.l0_uv = self.place("l0_uv", [P, KD, 2 * D1])
        self.l0_uvb = self.place("l0_uvb", [P, 2 * D1 // P])
        self.l0_t = self.place("l0_t", [P, D1 // P, B])
        self.l0_o = self.place("l0_o", [P, D1 // P, D])
        self.l0_ob = self.place("l0_ob", [1, D])
        self.l0_rw = self.place("l0_rw", [P, KD, 16])
        self.l0_rb = self.place("l0_rb", [1, 16])
        self.l0_db = self.place("l0_db", [16, D])
        self.l0_gub = self.place("l0_gub", [P, 16, 4])
        self.l1_wg = self.place("l1_wg", [P, KD, 32])
        self.l1_kvd = self.place("l1_kvd", [P, KD, P])
        self.l1_rope = self.place("l1_rope", [P, 4, S])
        self.l1_nw = self.place("l1_nw", [P, KD])
        self.l2_w = self.place("l2_w", [P, KD, 3 * D])
        self.l2_b = self.place("l2_b", [1, 3 * D])
        self.l2_avg = self.place("l2_avg", [P, P * LM // S])
        self.l2_w1 = self.place("l2_w1", [P, KD, FF])
        self.l2_b1 = self.place("l2_b1", [P, FF // P])
        self.l2_w2 = self.place("l2_w2", [P, FF // P, D])
        self.l2_b2 = self.place("l2_b2", [1, D])
        self.l3_wg = self.place("l3_wg", [P, FT3, D])
        self.l3_wu = self.place("l3_wu", [P, FT3, D])
        self.l3_wd = self.place("l3_wd", [P, KD, I3])
        self.loaded = {x: T.sem("loaded_" + x) for x in sorted({n[0:2] for n in self.tensors})}

    def place(self, name, shape):
        if self.only is not None and name not in self.only:
            return None
        self.tensors[name] = self.T.sb("w_" + name, shape)
        return self.tensors[name]

    def load(self, eng, name, src):
        t = self.tensors[name]
        eng.dma_start(t[:, :] if len(t.shape) == 2 else t[:, :, :], src).then_inc(self.loaded[name[0:2]], 16)

    def wait(self, eng, *names):
        for x in sorted({n[0:2] for n in names}):
            eng.wait_ge(self.loaded[x], 16 * sum(n[0:2] == x for n in self.tensors))


def load_weights(T, w, dram):
    with T.nc.Block() as block:
        @block.sync
        def _(sp):
            for name in w.tensors:
                w.load(sp, name, dram[name])




def by_partition(a, k):
    return a.reshape(k, a.shape[0] // k, a.shape[1]).transpose(1, 0, 2)


def lay_out(inp):
    import numpy as np
    f = {k: np.asarray(v) for k, v in inp.items()}
    cat = np.concatenate
    a = {}
    a["ids"] = f["x"].reshape(NT, P).T
    a["table"] = f["L0_tok_embedding"]
    a["l0_uv"] = by_partition(cat([f["L0_attn_u_w"], f["L0_attn_v_w"]]).T, KD)
    a["l0_uvb"] = cat([f["L0_attn_u_b"], f["L0_attn_v_b"]]).reshape(2 * D1 // P, P).T
    t = cat([f["L0_attn_t_zero"], f["L0_attn_t_pos"][:, :B - 1]], 1)
    a["l0_t"] = by_partition(np.repeat(t, D1 // TH, axis=0), D1 // P)
    a["l0_o"] = by_partition(f["L0_attn_o_w"].T, D1 // P)
    a["l0_ob"] = f["L0_attn_o_b"][None]
    a["l0_rw"] = by_partition(f["L0_ffn_router_w"], KD)
    a["l0_rb"] = f["L0_ffn_router_b"][None]
    a["l0_db"] = f["L0_ffn_down_bias"]

    def experts_by_partition(x):
        x = x.reshape(x.shape[0], x.shape[1] // P, P, x.shape[2]).transpose(0, 2, 1, 3)
        return x.reshape(x.shape[0] * P, x.shape[2], x.shape[3])

    gu, gub = f["L0_ffn_gate_up_proj"], f["L0_ffn_gate_up_bias"]
    a["l0_w13"] = experts_by_partition(cat([gu[:, :, 0::2], gu[:, :, 1::2]], 2))
    a["l0_w2"] = experts_by_partition(f["L0_ffn_down_proj"])
    a["l0_gub"] = cat([gub[:, 0::2], gub[:, 1::2]], 1).reshape(16, 4, P).transpose(2, 0, 1)
    a["l1_wg"] = by_partition(f["L1_ffn_wg"].T, KD)
    w1, w3, w2 = (cat([f["L1_ffn_w" + n], f["L1_ffn_sw" + n][None]]) for n in "132")
    a["l1_w13"] = experts_by_partition(cat([w1, w3], 2))
    a["l1_w2"] = experts_by_partition(w2)
    def turned(x):
        x = x.reshape(x.shape[0], GROUPS, 2, 1, 2, 2, 32)
        x = cat([x, x[:, :, :, :, :, ::-1]], 3)
        return x.reshape(x.shape[0], GROUPS, 4 * P).transpose(1, 0, 2)

    def side_by_side(*xs):
        out = []
        for x in xs:
            if x.shape[1] < P:
                x = cat([x, x], 1)
            k = x.shape[1] // P
            out.append(x.reshape(GROUPS, k, P, x.shape[2]).transpose(0, 2, 1, 3).reshape(GROUPS * P, -1))
        return cat(out, 1)

    def columns(x, n):
        return x.reshape(x.shape[0], GROUPS, n).transpose(1, 0, 2)

    a["l1_kvd"] = by_partition(f["L1_attn_kv_down"], KD)
    a["l1_nw"] = f["L1_attn_norm_w"].reshape(KD, P).T
    a["l1_aw"] = side_by_side(turned(f["L1_attn_wq"]), turned(f["L1_attn_wk"]), columns(f["L1_attn_wv"], 256),
                              f["L1_attn_wo"].reshape(GROUPS, 256, D))
    inv = (1.0 / (10000.0 ** (np.arange(0, 64, 2, dtype=np.float32) / np.float32(64)))).astype(np.float32)
    ang = np.arange(S, dtype=np.float32)[:, None] * inv[None, :]
    cos, sin = np.cos(ang).T, np.sin(ang).T
    cs = np.stack([cat([cos, cos]), cat([-sin, sin])], 1)
    a["l1_rope"] = np.tile(cat([cs, cs / np.float32(8)], 1), (2, 1, 1)).astype(np.float32)
    a["l2_w"] = by_partition(cat([f["L2_attn_Wq"], f["L2_attn_Wk"], f["L2_attn_Wv"]], 1), KD)
    a["l2_b"] = cat([f["L2_attn_bq"], f["L2_attn_bk"], f["L2_attn_bv"]])[None]
    a["l2_avg"] = (np.arange(P)[:, None] // (S // LM) == np.arange(P * LM // S)[None]).astype(np.float32) / (S // LM)
    a["l2_w1"] = by_partition(f["L2_ffn_W1"].T, KD)
    a["l2_b1"] = f["L2_ffn_b1"].reshape(FF // P, P).T
    a["l2_w2"] = by_partition(f["L2_ffn_W2"].T, FF // P)
    a["l2_b2"] = f["L2_ffn_b2"][None]
    rows = np.zeros((FT3 * P - I3, D), np.float32)
    a["l3_wg"], a["l3_wu"] = (by_partition(cat([f["L3_ffn_w_" + n], rows]), FT3) for n in ("gate", "up"))
    a["l3_wd"] = by_partition(f["L3_ffn_w_down"], KD)
    def padded(x):
        x = x.reshape(D, GROUPS, HG, 16)
        return cat([x] + [np.zeros_like(x)] * 3, 3).reshape(D, GROUPS, 2 * P).transpose(1, 0, 2)

    qkv = f["L3_attn_w_qkv"]
    a["l3_aw"] = side_by_side(padded(qkv[:, 0:D]), padded(qkv[:, D:2 * D]), columns(qkv[:, 2 * D:], 64),
                              f["L3_attn_w_out"].reshape(GROUPS, 64, D))
    return {k: np.ascontiguousarray(v) for k, v in a.items()}



def tower(nc, dram, out):
    with ExitStack() as ctx:
        T = places(nc, ctx)
        w = Weights(T)
        rows, results = (nc.dram_tensor("l1_" + n, (E1 * CAP, D), F32).ap() for n in ("rows", "results"))
        constants(T)
        s_zeroed = zero_places(T, rows)
        load_weights(T, w, dram)
        embed(T, dram["ids"], dram["table"])

        norm(T, add_back=True, rms=(0.0, 1e-8))
        toeplitz_attention(T, w)
        norm(T)
        with nc.sbuf_tensor("scores0", [P, NT, 16], F32) as SC:
            router0(T, w, SC[:, :, :])
            experts(T, w, "e0_", SC, 16, dram["l0_w13"], dram["l0_w2"], w.l0_gub)

        norm(T, add_back=True, rms=(1e-6, 0.0), col_scale=w.l1_nw)
        with nc.sbuf_tensor("kv", [P, N], F32) as kv:
            compress_kv(T, w, kv[:, :])
            with layers_semaphores(T):
                attention(T, w, "a1_", True, 64, dram["l1_aw"], kv[:, :], w.l1_rope)
        routed_layer(T, w, dram["l1_w13"], dram["l1_w2"], rows, results, s_zeroed)

        norm(T)
        landmark_attention(T, w)
        norm(T)
        ternary_ffn(T, w)

        norm(T)
        attention(T, w, "a3_", False, 16, dram["l3_aw"])
        with ExitStack() as last:
            def sb(name, shape):
                return last.enter_context(nc.sbuf_tensor(name, shape, F32))

            wgT, wdT = sb("wgT", [P, KD, 2, FT3 * P]), sb("wdT", [P, FT3, D])
            tmp = Fp4Scratch(T, sb, "q3", 1024, 16)
            norm(T, fp4=tmp)
            fp4_weights(T, w, tmp, wgT, wdT)
            fp4_ffn(T, w, tmp, wgT, wdT, out)


def kernel(**inputs):
    import numpy as np
    import concourse.bacc as bacc
    from concourse.bass_utils import run_bass_kernel_spmd

    arrays = lay_out(inputs)
    nc = bacc.Bacc("TRN2", target_bir_lowering=False, num_devices=1)
    dram = {n: nc.dram_tensor("in_" + n, a.shape, mybir.dt.from_np(a.dtype), kind="ExternalInput").ap()
            for n, a in arrays.items()}
    out = nc.dram_tensor("out", (N, D), F32, kind="ExternalOutput").ap()
    tower(nc, dram, out)
    got = run_bass_kernel_spmd(nc, [{"in_" + n: a for n, a in arrays.items()}], core_ids=[0])
    return np.asarray(got.results[0]["out"]).reshape(B, S, D)
```

```python
import concourse.bass as bass
from concourse import mybir
from contextlib import ExitStack, contextmanager

F32 = mybir.dt.float32
I32 = mybir.dt.int32
ALU = mybir.AluOpType
ACT = mybir.ActivationFunctionType
AX = mybir.AxisListType

P = 128
B, S, D = 4, 512, 256
N = B * S
NT = N // P
TB = S // P
KD = D // P
LN_EPS = 1e-5
SIGN_BIT = -(1 << 31)


class Steps:

    def __init__(self, eng, sem, base=0):
        self.eng, self.sem, self.base, self.n = eng, sem, base, 0

    def step(self, ins):
        self.n += 1
        ins.then_inc(self.sem, 1)

    def settled(self):
        self.eng.wait_ge(self.sem, self.base + self.n)

    def link(self, ins):
        self.step(ins)
        self.settled()


def spread(ap, n):
    return ap.unsqueeze(2).broadcast_to([ap.shape[0], ap.shape[1], n])



class Fp4Scratch:

    def __init__(self, T, sb, name, n, block):
        self.half_step = T.half_step
        self.a, self.m, self.t = (sb(f"{name}_{k}", [P, n]) for k in "amt")
        self.sc, self.rc = (sb(f"{name}_{k}", [P, n // block]) for k in ("sc", "rc"))


def fp4_blocks(dve, st, x, out, tmp, block, table):
    n = x.shape[1]
    nb = n // block
    sc, rc = tmp.sc[:, 0:nb], tmp.rc[:, 0:nb]
    a, m, t = tmp.a[:, 0:n], tmp.m[:, 0:n], tmp.t[:, 0:n]

    def v(ap):
        return ap.rearrange("p (g e) -> p g e", e=block)

    st.link(dve.tensor_reduce(sc, v(x), AX.X, ALU.max, apply_absolute_value=True))
    if table:
        st.link(dve.tensor_scalar(rc, sc, 0.0, None, ALU.is_equal))
        st.link(dve.scalar_tensor_tensor(sc, sc, 1.0 / 6.0, rc, ALU.mult, ALU.add))
    else:
        st.link(dve.tensor_scalar(sc, sc, 1.0 / 6.0, 1e-12, ALU.mult, ALU.max))
    st.link(dve.reciprocal(rc, sc))
    st.link(dve.tensor_tensor(v(a), v(x), spread(rc, block), ALU.mult))
    st.link(dve.tensor_scalar(a.bitcast(I32), a.bitcast(I32), 0x7FFFFFFF, None, ALU.bitwise_and))
    st.step(dve.tensor_scalar(m, a, 1.0, None, ALU.max))
    st.link(dve.tensor_scalar(t, a, 0.25, None, ALU.is_gt))
    st.step(dve.scalar_tensor_tensor(t, a, 0.75, t, ALU.is_gt, ALU.add))
    st.link(dve.tensor_tensor(m.bitcast(I32), m.bitcast(I32), tmp.half_step[:, 0:1].broadcast_to([P, n]), ALU.add))
    st.link(dve.tensor_scalar(m.bitcast(I32), m.bitcast(I32), -0x400000, None, ALU.bitwise_and))
    st.link(dve.scalar_tensor_tensor(m, t, 0.5, m, ALU.mult, ALU.add))
    st.link(dve.scalar_tensor_tensor(v(m), v(m), -1.0, spread(sc, block), ALU.add, ALU.mult))
    st.link(dve.scalar_tensor_tensor(out.bitcast(I32), x.bitcast(I32), SIGN_BIT, m.bitcast(I32),
                                     ALU.bitwise_and, ALU.bitwise_or))



class Places:
    pass


def places(nc, ctx):
    T = Places()
    T.nc = nc
    T.sb = lambda name, shape, dt=F32: ctx.enter_context(nc.sbuf_tensor(name, shape, dt))
    T.sem = lambda name: ctx.enter_context(nc.semaphore(name))
    T.PS = ctx.enter_context(nc.psum_tensor("PS", [P, 8, 512], F32))
    T.H = T.sb("H", [P, NT * D])
    T.XT = T.sb("XT", [P, KD, N])
    T.stats = T.sb("stats", [P, NT * 6])
    T.mv = T.sb("mv", [P, NT, 2])
    T.var, T.std, T.rstd = (T.sb(x, [P, NT]) for x in ("var", "std", "rstd"))
    T.ss, T.ms, T.root = (T.sb(x, [P, 2, TB]) for x in ("ss", "ms", "root"))
    T.sq = T.sb("sq", [P, TB * D])
    T.xn = T.sb("xn", [P, 2, TB, D])
    T.ident = T.sb("ident", [P, P])
    T.tri = T.sb("tri", [P, P])
    T.ones = T.sb("ones", [P, P])
    T.half_step = T.sb("half_step", [P, 1], I32)
    T.norm_sems = [T.sem("norm_" + x) for x in ("dve_steps", "var_ready", "std_ready", "xn_ready", "transposed",
                                                "evacuated")]
    T.norms = T.norm_roots = T.norm_dve_steps = 0
    T.s_const = T.sem("s_const")
    return T


@contextmanager
def layers_semaphores(T):
    of_program, taken = T.sem, []

    def sem(name):
        taken.append(T.nc.alloc_semaphore(name=name))
        return taken[-1]
    T.sem = sem
    yield
    T.sem = of_program
    with T.nc.Block() as block:
        @block.gpsimd
        def _(pool):
            T.nc.clear_and_free_semaphores(taken)


def token_tile(T, t):
    return T.H[:, bass.ds(t * D, D)]


def constants(T):
    nc = T.nc
    made = T.sem("s_const_made")
    with nc.Block() as block:
        @block.gpsimd
        def _(pool):
            pool.memset(T.ones[:, :], 1.0).then_inc(made, 1)
            pool.memset(T.ident[:, :], 0.0).then_inc(made, 1)
            pool.wait_ge(made, 2)
            pool.affine_select(out=T.ident[:, :], in_=T.ident[:, :], compare_op=ALU.not_equal, fill=1.0,
                               base=0, pattern=[[-1, P]], channel_multiplier=1).then_inc(T.s_const, 1)
            pool.affine_select(out=T.tri[:, :], in_=T.ones[:, :], compare_op=ALU.is_gt, fill=0.0,
                               base=0, pattern=[[1, P]], channel_multiplier=-1).then_inc(T.s_const, 1)
            pool.iota(T.half_step[:, :], pattern=[[0, 1]], base=0x1FFFFF, channel_multiplier=0).then_inc(T.s_const, 1)
            pool.wait_ge(T.s_const, 3)



def embed(T, ids, table):
    nc = T.nc
    with ExitStack() as ctx:
        idx = ctx.enter_context(nc.sbuf_tensor("idx", [P, NT], I32))
        raw = ctx.enter_context(nc.sbuf_tensor("raw", [P, NT * D], F32))
        G = 4
        W = NT // G * D
        tmp = Fp4Scratch(T, lambda name, shape: ctx.enter_context(nc.sbuf_tensor(name, shape, F32)), "emb", W, 32)
        ids_in, chain = T.sem("emb_ids_in"), T.sem("emb_steps")
        rows_in = [T.sem(f"emb_rows_in{g}") for g in range(G)]
        with nc.Block() as block:
            @block.sync
            def _(sp):
                sp.dma_start(idx[:, :], ids).then_inc(ids_in, 16)

            @block.gpsimd
            def _(pool):
                pool.wait_ge(ids_in, 16)
                for t in range(NT):
                    pool.indirect_dma_start(out=raw[:, t * D:(t + 1) * D], out_offset=None, in_=table,
                                            in_offset=bass.IndirectOffsetOnAxis(ap=idx[:, t:t + 1], axis=0),
                                            ).then_inc(rows_in[t * G // NT], 16)

            @block.vector
            def _(dve):
                st = Steps(dve, chain)
                for g in range(G):
                    dve.wait_ge(rows_in[g], 16 * NT // G)
                    st.settled() if g else None
                    fp4_blocks(dve, st, raw[:, g * W:(g + 1) * W], T.H[:, g * W:(g + 1) * W], tmp, 32, True)



def norm(T, add_back=False, rms=None, col_scale=None, fp4=None, keep=None, arrivals=None):
    nc = T.nc
    s_dve, s_var, s_std, s_xn, s_tr, s_ev = T.norm_sems
    first = T.norms == 0
    n0, r0, d0 = T.norms, T.norm_roots, T.norm_dve_steps
    summed = TB + (TB * (TOPK - 1) if arrivals else 0)
    applied = TB + bool(add_back) + (TB + 4 if rms else 0) + (FP4_STEPS if fp4 else 0) + (keep is not None)
    d1 = d0 + B * summed
    d2 = d1 + NT + (B if arrivals else 1)
    first_roots, batch_roots = (0, 1 + bool(rms)) if arrivals else (1, int(bool(rms)))
    T.norms += B
    T.norm_roots += first_roots + B * batch_roots
    T.norm_dve_steps = d2 + B * applied
    with nc.Block() as block:
        if arrivals:
            @block.gpsimd
            def _(pool):
                arrivals.gather(pool)

        @block.vector
        def _(dve):
            def statistics(b, base):
                st = Steps(dve, s_dve, base)
                if arrivals:
                    arrivals.add(dve, st, b)
                for t in range(TB):
                    st.step(dve.bn_stats(T.stats[:, bass.ds((b * TB + t) * 6, 6)], token_tile(T, b * TB + t)))

            def reciprocal_roots(tiles, base, root):
                st = Steps(dve, s_dve, base)
                st.settled()
                for t in tiles:
                    st.step(dve.bn_aggr(T.mv[:, t, :], T.stats[:, t * 6:(t + 1) * 6]))
                st.settled()
                these = slice(tiles[0], tiles[-1] + 1)
                dve.tensor_scalar(T.var[:, these], T.mv[:, these, 1], LN_EPS, None, ALU.add).then_inc(s_var, 1)
                dve.wait_ge(s_std, root)
                st.link(dve.reciprocal(T.rstd[:, these], T.std[:, these]))

            def body(b, p, base):
                st = Steps(dve, s_dve, base)
                dve.wait_ge(s_tr, n0 + b + 1)
                for t in range(TB):
                    ins = dve.tensor_scalar(T.xn[:, p, t, :], token_tile(T, b * TB + t), T.mv[:, one(b * TB + t), 0],
                                            T.rstd[:, one(b * TB + t)], ALU.subtract, ALU.mult)
                    st.step(ins)
                st.settled()
                xn = T.xn[:, p, :, :].rearrange("p t d -> p (t d)")
                if add_back:
                    h = T.H[:, bass.ds(b * TB * D, TB * D)]
                    st.link(dve.tensor_tensor(h, h, xn, ALU.add))
                if rms:
                    st.link(dve.tensor_tensor(T.sq[:, :], xn, xn, ALU.mult))
                    st.link(dve.tensor_reduce(T.ss[:, p, :], T.sq[:, :].rearrange("p (t d) -> p t d", t=TB), AX.X,
                                              ALU.add))
                    dve.tensor_scalar(T.ms[:, p, :], T.ss[:, p, :], 1.0 / D, rms[0], ALU.mult, ALU.add)\
                       .then_inc(s_var, 1)
                    dve.wait_ge(s_std, r0 + first_roots + b * batch_roots + batch_roots)
                    st.link(dve.tensor_scalar(T.ss[:, p, :], T.root[:, p, :], rms[1], None, ALU.add))
                    st.link(dve.reciprocal(T.ss[:, p, :], T.ss[:, p, :]))
                    for t in range(TB):
                        st.step(dve.tensor_scalar(T.xn[:, p, t, :], T.xn[:, p, t, :], T.ss[:, p, t:t + 1],
                                                  None, ALU.mult))
                    st.settled()
                if fp4:
                    fp4_blocks(dve, st, xn, xn, fp4, 16, False)
                if keep is not None:
                    st.link(dve.tensor_copy(keep[:, bass.ds(b * TB * D, TB * D)], xn))
                dve.nop().then_inc(s_xn, 1)
                assert st.n == applied, (st.n, applied)

            if arrivals:
                all_steps = summed + TB + 1 + applied
                for b in range(B):
                    base = d0 + b * all_steps
                    statistics(b, base)
                    reciprocal_roots(range(b * TB, b * TB + TB), base + summed, r0 + b * batch_roots + 1)
                    body(b, b % 2, base + summed + TB + 1)
            else:
                with dve.Fori(0, B) as b:
                    statistics(b, d0 + b * summed)
                reciprocal_roots(range(NT), d1, r0 + 1)
                with dve.Fori(0, B // 2) as i:
                    for p in range(2):
                        body(i * 2 + p, p, d2 + (i * 2 + p) * applied)

        @block.scalar
        def _(act):
            if first:
                act.sem_inc(s_ev, 2)

            def roots(n, tiles):
                act.wait_ge(s_var, n)
                act.activation(T.std[:, tiles], T.var[:, tiles], ACT.Sqrt).then_inc(s_std, 1)

            def batch(b, p):
                if rms:
                    act.wait_ge(s_var, r0 + first_roots + b * batch_roots + batch_roots)
                    act.activation(T.root[:, p, :], T.ms[:, p, :], ACT.Sqrt).then_inc(s_std, 1)
                act.wait_ge(s_tr, n0 + b + 3)
                for k in range(KD):
                    out, src = T.XT[:, k, bass.ds(b * S, S)], T.PS[:, 2 * p + k, :]
                    if col_scale is None:
                        ins = act.activation(out, src, ACT.Copy)
                    else:
                        ins = act.activation(out, src, ACT.Copy, scale=col_scale[:, k:k + 1])
                ins.then_inc(s_ev, 1)

            if arrivals:
                for b in range(B):
                    roots(r0 + b * batch_roots + 1, slice(b * TB, b * TB + TB))
                    batch(b, b % 2)
            else:
                roots(r0 + 1, slice(0, NT))
                with act.Fori(0, B // 2) as i:
                    for p in range(2):
                        batch(i * 2 + p, p)

        @block.tensor
        def _(pe):
            pe.wait_ge(T.s_const, 2)
            if first:
                pe.sem_inc(s_tr, 2)
            with pe.Fori(0, B // 2) as i:
                for p in range(2):
                    b = i * 2 + p
                    pe.wait_ge(s_xn, n0 + b + 1)
                    pe.wait_ge(s_ev, n0 + b + 1)
                    for t in range(TB):
                        for k in range(KD):
                            ins = pe.transpose(T.PS[:, 2 * p + k, t * P:(t + 1) * P],
                                               T.xn[:, p, t, k * P:(k + 1) * P], T.ident[:, :])
                    ins.then_inc(s_tr, 1)


FP4_STEPS = 13



D1 = 512
TH = 8


def toeplitz_attention(T, w):
    nc = T.nc
    F = D1 // P
    JOBS = 2 * F
    with ExitStack() as ctx:
        def sb(name, shape):
            return ctx.enter_context(nc.sbuf_tensor("ta_" + name, shape, F32))

        uT = sb("uT", [P, 2, F, B, P])
        vT = sb("vT", [P, 2, F, B, P])
        y = sb("y", [P, 2, F, B, P])
        s_uv, s_act, s_y, s_out, s_h = (T.sem("ta_" + x) for x in (
            "uv_in_bank", "uv_evacuated", "y_steps", "out_in_bank", "h_added"))
        YS = 5 * F

        def steps(eng, ahead, body):
            ahead(0, 0)
            with eng.Fori(0, TB // 2 - 1) as i:
                for p in range(2):
                    ahead(i * 2 + p + 1, 1 - p)
                    body(i * 2 + p, p)
            ahead(TB - 1, 1)
            body(TB - 2, 0)
            body(TB - 1, 1)

        with nc.Block() as block:
            @block.tensor
            def _(pe):
                w.wait(pe, "l0_uv", "l0_o", "l0_ob")
                pe.sem_inc(s_out, 4)

                def products(c, p):
                    for n in range(JOBS):
                        f = n // 2 + (F if n % 2 == 0 else 0)
                        pe.wait_ge(s_act, c * JOBS + n + 1)
                        for k in range(KD):
                            x = T.XT[:, k, :].rearrange("p (b s) -> p b s", b=B)[:, :, bass.ds(c * P, P)]
                            ins = pe.matmul(T.PS[:, n % 4, :], w.l0_uv[:, k, f * P:(f + 1) * P], x,
                                            start=(k == 0), stop=(k == KD - 1))
                        ins.then_inc(s_uv, 1)

                def output(c, p):
                    pe.wait_ge(s_y, c * YS + YS)
                    for g in range(2):
                        pe.wait_ge(s_h, c * 2 + g + 1)
                        for b in range(2 * g, 2 * g + 2):
                            bank = T.PS[:, 4 + 2 * p + g, (b % 2) * D:(b % 2 + 1) * D]
                            pe.matmul(bank, T.ones[0:1, :], w.l0_ob[0:1, :], start=True, stop=False)
                            for f in range(F):
                                ins = pe.matmul(bank, y[:, p, f, b, :], w.l0_o[:, f, :],
                                                start=False, stop=(f == F - 1))
                        ins.then_inc(s_out, 1)
                steps(pe, products, output)

            @block.scalar
            def _(act):
                w.wait(act, "l0_uvb")
                act.sem_inc(s_act, 4)
                with act.Fori(0, TB // 2) as i:
                    for p in range(2):
                        c = i * 2 + p
                        act.wait_ge(s_out, 2 * c + 2)
                        for n in range(JOBS):
                            f = n // 2
                            act.wait_ge(s_uv, c * JOBS + n + 1)
                            out = (uT if n % 2 else vT)[:, p, f, :, :]
                            act.activation(out, T.PS[:, n % 4, :].rearrange("p (b s) -> p b s", b=B), ACT.Silu,
                                           bias=w.l0_uvb[:, f + (0 if n % 2 else F):f + (1 if n % 2 else F + 1)])\
                               .then_inc(s_act, 1)

            @block.vector
            def _(dve):
                w.wait(dve, "l0_t")
                dve.sem_inc(s_h, 4)

                def mix(c, p):
                    st = Steps(dve, s_y, c * YS)
                    dve.wait_ge(s_out, 2 * c + 2)
                    for f in range(F):
                        dve.wait_ge(s_act, c * JOBS + 2 * f + 5)
                        v, o = vT[:, p, f, :, :], y[:, p, f, :, :]
                        st.link(dve.tensor_scalar(o, v, w.l0_t[:, f, 0:1], None, ALU.mult))
                        for d in range(1, B):
                            st.link(dve.scalar_tensor_tensor(o[:, d:B, :], v[:, 0:B - d, :], w.l0_t[:, f, d:d + 1],
                                                             o[:, d:B, :], ALU.mult, ALU.add))
                        dve.wait_ge(s_act, c * JOBS + 2 * f + 6)
                        st.step(dve.tensor_tensor(o, o, uT[:, p, f, :, :], ALU.mult))

                def add(c, p):
                    for g in range(2):
                        dve.wait_ge(s_out, 4 + 2 * c + g + 1)
                        for b in range(2 * g, 2 * g + 2):
                            h = token_tile(T, c + b * TB)
                            ins = dve.tensor_tensor(h, h, T.PS[:, 4 + 2 * p + g, (b % 2) * D:(b % 2 + 1) * D],
                                                    ALU.add)
                        ins.then_inc(s_h, 1)
                steps(dve, mix, add)



TOPK = 4
E1 = 32
CAP = int(1.25 * N * TOPK / E1)


def over(ap, n):
    return ap.unsqueeze(1).broadcast_to([ap.shape[0], n, ap.shape[1]])


TOP4_STEPS = 6 * TOPK + 1


def top4(dve, st, s, mask, code, m, c, sels, low):
    n, e = s.shape[1], s.shape[2]
    for sel in sels:
        st.link(dve.tensor_reduce(m, s, AX.X, ALU.max))
        st.link(dve.tensor_tensor(c, s, spread(m, e), ALU.is_equal))
        st.link(dve.tensor_tensor(c, c, over(code, n), ALU.mult))
        st.link(dve.tensor_reduce(m, c, AX.X, ALU.max))
        st.link(dve.tensor_tensor(sel, c, spread(m, e), ALU.is_equal))
        st.link(dve.scalar_tensor_tensor(s, sel, -low, s, ALU.mult, ALU.add))
    st.link(dve.tensor_scalar(mask, s, -low / 2, None, ALU.is_lt))


def code_row(T, pool, s_made, irow, row, e):
    pool.iota(irow, pattern=[[-1, e]], base=e, channel_multiplier=0).then_inc(s_made, 1)
    pool.wait_ge(s_made, 1)
    pool.tensor_copy(row, irow).then_inc(s_made, 1)


def choices(dve, st, sel, place, score, c, destf, weight):
    for r in range(TOPK):
        one_hot = sel[:, r, :, :]
        st.step(dve.tensor_tensor(c, one_hot, place, ALU.mult))
        st.link(dve.tensor_tensor(one_hot, one_hot, score, ALU.mult))
        st.step(dve.tensor_reduce(destf[:, r * NT:(r + 1) * NT], c, AX.X, ALU.add))
        st.link(dve.tensor_reduce(weight[:, r * NT:(r + 1) * NT], one_hot, AX.X, ALU.add))


def router0(T, w, weight, dest, which, on_pool):
    nc = T.nc
    E = E0
    with ExitStack() as ctx:
        def sb(name, shape, dt=F32):
            return ctx.enter_context(nc.sbuf_tensor("r0_" + name, shape, dt))

        irow, code = sb("irow", [P, E], I32), sb("code", [P, E])
        m, m0, c, sel = sb("m", [P, NT]), sb("m0", [P, NT]), sb("c", [P, NT, E]), sb("sel", [P, TOPK, NT, E])
        SC, before = sb("SC", [P, NT, E]), sb("before", [P, NT + 1, E])
        total, segs = sb("total", [P, E]), sb("segs", [P, E])
        ends = sb("ends", [P, E + 1])
        inumbers, numbers = sb("inumbers", [P, SEGS], I32), sb("numbers", [P, SEGS])
        ipart, part = sb("ipart", [P, 1], I32), sb("part", [P, 1])
        filled, of = sb("filled", [P, E, N // SEG]), sb("of", [P, SEGS, E])
        destf, whichf = sb("destf", [P, TOPK * NT]), sb("whichf", [P, SEGS])
        lg, s, mask = sb("lg", [P, NT, E]), sb("s", [P, NT, E]), sb("mask", [P, NT, E])
        scT = sb("scT", [E, N])
        s_code, s_lg, s_x, s_e, s_dve, s_t, s_tc, s_o, s_h = (T.sem("r0_" + x) for x in (
            "code_made", "logits_in_bank", "shifted", "exp_done", "dve_steps", "scores_transposed",
            "scores_copied", "bias_in_bank", "h_added"))
        s_place, s_known = T.sem("r0_counts_in_bank"), T.sem("r0_places_known")
        SCORED = 8 + TOP4_STEPS
        COUNTED = SCORED + 1 + NT
        with nc.Block() as block:
            @block.gpsimd
            def _(pool):
                code_row(T, pool, s_code, irow[:, :], code[:, :], E)
                pool.iota(inumbers[:, :], pattern=[[1, SEGS]], base=0, channel_multiplier=0).then_inc(s_code, 1)
                pool.iota(ipart[:, :], pattern=[[0, 1]], base=0, channel_multiplier=1).then_inc(s_code, 1)
                pool.wait_ge(s_code, 4)
                pool.tensor_copy(numbers[:, :], inumbers[:, :]).then_inc(s_code, 1)
                pool.tensor_copy(part[:, :], ipart[:, :]).then_inc(s_code, 1)
                pool.wait_ge(s_known, 1)
                on_pool(pool)

            @block.tensor
            def _(pe):
                w.wait(pe, "l0_rw", "l0_rb", "l0_db")
                for t in range(NT):
                    out = T.PS[:, 0, t * E:(t + 1) * E]
                    pe.matmul(out, T.ones[0:1, :], w.l0_rb[0:1, :], start=True, stop=False)
                    for k in range(KD):
                        ins = pe.matmul(out, T.XT[:, k, t * P:(t + 1) * P], w.l0_rw[:, k, :],
                                        start=False, stop=(k == KD - 1))
                ins.then_inc(s_lg, 1)
                pe.wait_ge(s_dve, SCORED)
                for t in range(NT):
                    ins = pe.transpose(T.PS[0:E, 4 + t // 4, (t % 4) * P:(t % 4 + 1) * P], SC[:, t, :], T.ident[:, :])
                ins.then_inc(s_t, 1)
                pe.wait_ge(s_tc, 1)
                pe.wait_ge(s_dve, COUNTED)
                for t in range(NT):
                    out = T.PS[:, 4, t * E:(t + 1) * E]
                    pe.matmul(out, T.ones[:, :], before[:, t, :], start=True, stop=False)
                    pe.matmul(out, T.tri[:, :], mask[:, t, :], start=False, stop=True)
                pe.matmul(T.PS[:, 5, 0:E], T.ones[:, :], before[:, NT, :], start=True, stop=True).then_inc(s_place, 1)
                for t in range(NT):
                    if t % 2 == 0 and t >= 8:
                        pe.wait_ge(s_h, t // 2 - 3)
                    ins = pe.matmul(T.PS[:, t // 2 % 4, (t % 2) * D:(t % 2 + 1) * D], scT[:, t * P:(t + 1) * P],
                                    w.l0_db[:, :], start=True, stop=True)
                    if t % 2:
                        ins.then_inc(s_o, 1)

            @block.scalar
            def _(act):
                act.wait_ge(s_x, 1)
                act.activation(lg[:, :, :], lg[:, :, :], ACT.Exp).then_inc(s_e, 1)
                act.wait_ge(s_t, 1)
                act.activation(scT[:, :], T.PS[0:E, 4:8, :].rearrange("p a b -> p (a b)"), ACT.Copy).then_inc(s_tc, 1)

            @block.vector
            def _(dve):
                st = Steps(dve, s_dve)
                dve.wait_ge(s_lg, 1)
                st.step(dve.tensor_copy(lg[:, :, :], T.PS[:, 0, 0:NT * E].rearrange("p (t e) -> p t e", e=E)))
                st.link(dve.tensor_copy(s[:, :, :], T.PS[:, 0, 0:NT * E].rearrange("p (t e) -> p t e", e=E)))
                st.link(dve.tensor_reduce(m0[:, :], s[:, :, :], AX.X, ALU.max))
                dve.wait_ge(s_code, 2)
                st.link(dve.tensor_tensor(lg[:, :, :], lg[:, :, :], spread(m0[:, :], E), ALU.subtract))
                dve.nop().then_inc(s_x, 1)
                top4(dve, st, s[:, :, :], mask[:, :, :], code[:, :], m[:, :], c[:, :, :], [sel[:, r, :, :] for r in range(TOPK)], 1e38)
                dve.wait_ge(s_e, 1)
                st.link(dve.tensor_tensor(lg[:, :, :], lg[:, :, :], mask[:, :, :], ALU.mult))
                st.link(dve.tensor_reduce(m[:, :], lg[:, :, :], AX.X, ALU.add))
                st.link(dve.reciprocal(m[:, :], m[:, :]))
                st.link(dve.tensor_tensor(SC[:, :, :], lg[:, :, :], spread(m[:, :], E), ALU.mult))
                assert st.n == SCORED
                st.link(dve.memset(before[:, 0, :], 0.0))
                for t in range(NT):
                    st.link(dve.tensor_tensor(before[:, t + 1, :], before[:, t, :], mask[:, t, :], ALU.add))
                assert st.n == COUNTED
                dve.wait_ge(s_code, 6)
                dve.wait_ge(s_place, 1)
                st.step(dve.tensor_copy(total[:, :], T.PS[:, 5, 0:E]))
                st.link(dve.tensor_scalar(whichf[:, 0:N // SEG], numbers[:, 0:N // SEG], float(SEG), None, ALU.mult))
                st.link(dve.tensor_tensor(filled[:, :, :], spread(total[:, :], N // SEG),
                                          over(whichf[:, 0:N // SEG], E), ALU.is_gt))
                st.step(dve.memset(ends[:, 0:1], 0.0))
                st.link(dve.tensor_reduce(segs[:, :], filled[:, :, :], AX.X, ALU.add))
                for e in range(E):
                    st.link(dve.tensor_tensor(ends[:, e + 1:e + 2], ends[:, e:e + 1], segs[:, e:e + 1], ALU.add))
                st.link(dve.tensor_tensor(of[:, :, :], spread(numbers[:, :], E), over(ends[:, 1:E + 1], SEGS),
                                          ALU.is_ge))
                st.link(dve.tensor_reduce(whichf[:, :], of[:, :, :], AX.X, ALU.add))
                st.link(dve.tensor_scalar(whichf[:, :], whichf[:, :], float(E - 1), float(P), ALU.min, ALU.mult))
                st.link(dve.tensor_scalar(whichf[:, :], whichf[:, :], part[:, 0:1], None, ALU.add))
                st.step(dve.tensor_copy(which[:, :], whichf[:, :]))
                st.link(dve.tensor_scalar(segs[:, :], ends[:, 0:E], float(SEG), None, ALU.mult))
                st.link(dve.tensor_tensor(mask[:, :, :], T.PS[:, 4, 0:NT * E].rearrange("p (t e) -> p t e", e=E),
                                          over(segs[:, :], NT), ALU.add))
                choices(dve, st, sel, mask[:, :, :], SC[:, :, :], c[:, :, :], destf, weight)
                dve.tensor_copy(dest[:, :], destf[:, :]).then_inc(s_known, 1)
                for g in range(NT // 2):
                    dve.wait_ge(s_o, g + 1)
                    h = T.H[:, 2 * g * D:(2 * g + 2) * D]
                    dve.tensor_tensor(h, h, T.PS[:, g % 4, :], ALU.add).then_inc(s_h, 1)


def router1(T, w, weight, dest, index):
    nc = T.nc
    E, G = E1, 8
    with ExitStack() as ctx:
        def sb(name, shape, dt=F32):
            return ctx.enter_context(nc.sbuf_tensor("r1_" + name, shape, dt))

        irow, code = sb("irow", [P, E], I32), sb("code", [P, E])
        m, c, sel = sb("m", [P, NT]), sb("c", [P, NT, E]), sb("sel", [P, TOPK, NT, E])
        place, destf, offset = sb("place", [P, NT, E]), sb("destf", [P, TOPK * NT]), sb("offset", [P, E])
        pr, s, mask = sb("pr", [P, NT, E]), sb("s", [P, NT, E]), sb("mask", [P, NT, E])
        gs, keep, gc, gsel = (sb(x, [P, NT, G]) for x in ("gs", "keep", "gc", "gsel"))
        before = sb("before", [P, NT, E])
        s_code, s_lg, s_x, s_e, s_dve, s_p = (T.sem("r1_" + x) for x in (
            "code_made", "logits_in_bank", "shifted", "exp_done", "dve_steps", "places_in_bank"))
        PLACED = 3 + 2 + 1 + TOP4_STEPS + 3 + TOP4_STEPS + NT
        with nc.Block() as block:
            @block.gpsimd
            def _(pool):
                code_row(T, pool, s_code, irow[:, :], code[:, :], E)

            @block.tensor
            def _(pe):
                w.wait(pe, "l1_wg")
                for t in range(NT):
                    for k in range(KD):
                        ins = pe.matmul(T.PS[:, 0, t * E:(t + 1) * E], T.XT[:, k, t * P:(t + 1) * P],
                                        w.l1_wg[:, k, :], start=(k == 0), stop=(k == KD - 1))
                ins.then_inc(s_lg, 1)
                pe.wait_ge(s_dve, PLACED)
                for t in range(NT):
                    out = T.PS[:, 1, t * E:(t + 1) * E]
                    pe.matmul(out, T.ones[:, :], before[:, t, :], start=True, stop=False)
                    ins = pe.matmul(out, T.tri[:, :], mask[:, t, :], start=False, stop=True)
                ins.then_inc(s_p, 1)

            @block.scalar
            def _(act):
                act.wait_ge(s_x, 1)
                act.activation(pr[:, :, :], pr[:, :, :], ACT.Exp).then_inc(s_e, 1)

            @block.vector
            def _(dve):
                st = Steps(dve, s_dve)
                dve.wait_ge(s_lg, 1)
                lg = T.PS[:, 0, 0:NT * E].rearrange("p (t e) -> p t e", e=E)
                st.link(dve.tensor_reduce(m[:, :], lg, AX.X, ALU.max))
                st.link(dve.tensor_tensor(pr[:, :, :], lg, spread(m[:, :], E), ALU.subtract))
                dve.nop().then_inc(s_x, 1)
                dve.wait_ge(s_e, 1)
                st.link(dve.tensor_reduce(m[:, :], pr[:, :, :], AX.X, ALU.add))
                st.link(dve.reciprocal(m[:, :], m[:, :]))
                st.link(dve.tensor_tensor(pr[:, :, :], pr[:, :, :], spread(m[:, :], E), ALU.mult))
                groups = pr[:, :, :].rearrange("p t (g e) -> p (t g) e", g=G)
                st.link(dve.tensor_reduce(gs[:, :, :].rearrange("p t g -> p (t g)"), groups, AX.X, ALU.max))
                dve.wait_ge(s_code, 2)
                top4(dve, st, gs[:, :, :], keep[:, :, :], code[:, E - G:E], m[:, :], gc[:, :, :],
                     [gsel[:, :, :]] * TOPK, 3.0)
                kg = keep[:, :, :].rearrange("p t g -> p (t g)")
                s4 = s[:, :, :].rearrange("p t (g e) -> p (t g) e", g=G)
                st.link(dve.tensor_tensor(s4, groups, spread(kg, E // G), ALU.mult))
                st.link(dve.tensor_scalar(gc[:, :, :], keep[:, :, :], 1.0, None, ALU.subtract))
                st.link(dve.tensor_tensor(s4, s4, spread(gc[:, :, :].rearrange("p t g -> p (t g)"), E // G), ALU.add))
                top4(dve, st, s[:, :, :], mask[:, :, :], code[:, :], m[:, :], c[:, :, :],
                     [sel[:, r, :, :] for r in range(TOPK)], 3.0)
                st.link(dve.memset(before[:, 0, :], 0.0))
                for t in range(1, NT):
                    st.link(dve.tensor_tensor(before[:, t, :], before[:, t - 1, :], mask[:, t - 1, :], ALU.add))
                assert st.n == PLACED, st.n
                st.link(dve.tensor_tensor(pr[:, :, :], pr[:, :, :], mask[:, :, :], ALU.mult))
                st.link(dve.tensor_reduce(m[:, :], pr[:, :, :], AX.X, ALU.add))
                st.link(dve.tensor_scalar(m[:, :], m[:, :], 1e-9, None, ALU.add))
                st.link(dve.reciprocal(m[:, :], m[:, :]))
                st.link(dve.tensor_tensor(pr[:, :, :], pr[:, :, :], spread(m[:, :], E), ALU.mult))
                dve.wait_ge(s_p, 1)
                count = T.PS[:, 1, 0:NT * E].rearrange("p (t e) -> p t e", e=E)
                st.step(dve.tensor_scalar(offset[:, :], code[:, :], float(E), -float(CAP), ALU.subtract, ALU.mult))
                st.step(dve.scalar_tensor_tensor(pr[:, :, :], count, float(CAP), pr[:, :, :], ALU.is_lt, ALU.mult))
                st.link(dve.tensor_scalar(place[:, :, :], count, float(CAP), float(2 * E * CAP), ALU.is_ge, ALU.mult))
                st.link(dve.tensor_tensor(place[:, :, :], place[:, :, :], count, ALU.add))
                st.link(dve.tensor_tensor(place[:, :, :], place[:, :, :], over(offset[:, :], NT), ALU.add))
                choices(dve, st, sel, place[:, :, :], pr[:, :, :], c[:, :, :], destf, weight)
                st.link(dve.tensor_copy(dest[:, :], destf[:, :]))
                st.link(dve.tensor_scalar(destf[:, :], destf[:, :], float(E * CAP - 1), None, ALU.min))
                st.link(dve.tensor_copy(index[:, :], destf[:, :]))



EI = 256
CH = N // S


def experts(T, w, name, SC, E, w13_dram, w2_dram, clipped_bias=None, on_pool=None):
    nc = T.nc
    F = EI // P
    LIMIT, ALPHA = 7.0, 1.702
    with ExitStack() as ctx:
        def sb(nm, shape):
            return ctx.enter_context(nc.sbuf_tensor(name + nm, shape, F32))

        w13, w2 = sb("w13", [P, 2, KD, 2 * EI]), sb("w2", [P, 2, F, D])
        g, u, sg = sb("g", [P, 2, S]), sb("u", [P, 2, S]), sb("sg", [P, 2, S])
        hT = sb("hT", [P, 2, F, S])
        s_w = [T.sem(f"{name}weights_in{q}") for q in range(2)]
        s_gu, s_free, s_sg, s_h, s_dn, s_add, s_pool = (T.sem(name + x) for x in (
            "gate_up_in_bank", "gate_up_read", "gate_activated", "h_ready", "down_in_bank", "h_added",
            "pool_steps"))
        UN = CH * F
        DN = CH * 2

        def all_experts(eng, body):
            if E > 1:
                with eng.Fori(0, E // 2) as i:
                    for q in range(2):
                        body(i * 2 + q, q, i)
            if E % 2:
                body(E - 1, 0, E // 2)

        with nc.Block() as block:
            @block.sync
            def _(sp):
                def body(e, q, i):
                    sp.wait_ge(s_dn, e * DN + DN + 1)
                    sp.dma_start(w13[:, q, :, :], w13_dram[bass.ds(e * P, P), :, :]).then_inc(s_w[q], 16)
                    sp.dma_start(w2[:, q, :, :], w2_dram[bass.ds(e * P, P), :, :]).then_inc(s_w[q], 16)
                all_experts(sp, body)

            @block.tensor
            def _(pe):
                pe.sem_inc(s_dn, 2 * DN + 1)

                def body(e, q, i):
                    pe.wait_ge(s_w[q], i * 32 + 32)

                    def gate_up(c):
                        for f in range(F):
                            n = e * UN + c * F + f
                            pe.wait_ge(s_h if clipped_bias is None else s_free, n + 1)
                            for a in range(2):
                                for k in range(KD):
                                    ins = pe.matmul(T.PS[:, 2 * f + a, :],
                                                    w13[:, q, k, a * EI + f * P:a * EI + (f + 1) * P],
                                                    T.XT[:, k, c * S:(c + 1) * S], start=(k == 0), stop=(k == KD - 1))
                            ins.then_inc(s_gu, 1)

                    def down(c):
                        pe.wait_ge(s_h, e * UN + c * F + F + 2)
                        for m in range(2):
                            pe.wait_ge(s_add, e * DN + c * 2 + m + 1)
                            for t in range(2 * m, 2 * m + 2):
                                out = T.PS[:, 4 + (2 * c + m) % 4, (t % 2) * D:(t % 2 + 1) * D]
                                for f in range(F):
                                    ins = pe.matmul(out, hT[:, c % 2, f, t * P:(t + 1) * P], w2[:, q, f, :],
                                                    start=(f == 0), stop=(f == F - 1))
                            ins.then_inc(s_dn, 1)

                    gate_up(0)
                    for c in range(1, CH):
                        gate_up(c)
                        down(c - 1)
                    down(CH - 1)
                all_experts(pe, body)

            @block.scalar
            def _(act):
                def body(e, q, i):
                    for c in range(CH):
                        for f in range(F):
                            n = e * UN + c * F + f
                            if clipped_bias is None:
                                act.wait_ge(s_gu, n + 1)
                                act.wait_ge(s_h, n + 1)
                                act.activation(sg[:, f, :], T.PS[:, 2 * f, :], ACT.Silu).then_inc(s_sg, 1)
                            else:
                                act.wait_ge(s_free, n + 3)
                                act.wait_ge(s_h, n + 1)
                                act.activation(sg[:, f, :], g[:, f, :], ACT.Sigmoid, scale=ALPHA).then_inc(s_sg, 1)
                all_experts(act, body)

            if on_pool:
                @block.gpsimd
                def _(pool):
                    on_pool(pool)

            if clipped_bias is not None:
                @block.gpsimd
                def _(pool):
                    pool.sem_inc(s_h, 2)

                    def body(e, q, i):
                        for c in range(CH):
                            for f in range(F):
                                n = e * UN + c * F + f
                                pool.wait_ge(s_sg, n + 1)
                                pool.tensor_tensor(g[:, f, :], g[:, f, :], sg[:, f, :], ALU.mult).then_inc(s_pool, 1)
                                pool.tensor_scalar(u[:, f, :], u[:, f, :], -LIMIT, 1.0, ALU.max, ALU.add)\
                                    .then_inc(s_pool, 1)
                                pool.wait_ge(s_pool, 2 * n + 2)
                                pool.wait_ge(s_dn, e * DN + 2 * c + 2 * DN - 1)
                                pool.tensor_tensor(hT[:, c % 2, f, :], g[:, f, :], u[:, f, :], ALU.mult)\
                                    .then_inc(s_h, 1)
                    all_experts(pool, body)

            @block.vector
            def _(dve):
                if clipped_bias is not None:
                    w.wait(dve, "l0_gub")
                dve.sem_inc(s_free, 2)
                dve.sem_inc(s_add, 4)
                if clipped_bias is None:
                    dve.sem_inc(s_h, 2)

                def body(e, q, i):
                    def unit(c):
                        for f in range(F):
                            n = e * UN + c * F + f
                            if clipped_bias is None:
                                dve.wait_ge(s_sg, n + 1)
                                dve.wait_ge(s_dn, e * DN + 2 * c + 2 * DN - 1)
                                dve.tensor_tensor(hT[:, c % 2, f, :], sg[:, f, :], T.PS[:, 2 * f + 1, :],
                                                  ALU.mult).then_inc(s_h, 1)
                            else:
                                dve.wait_ge(s_gu, n + 1)
                                dve.wait_ge(s_h, n + 1)
                                dve.tensor_scalar(g[:, f, :], T.PS[:, 2 * f, :], clipped_bias[:, one(e), f],
                                                  LIMIT, ALU.add, ALU.min)
                                dve.tensor_scalar(u[:, f, :], T.PS[:, 2 * f + 1, :], clipped_bias[:, one(e), 2 + f],
                                                  LIMIT, ALU.add, ALU.min).then_inc(s_free, 1)

                    def add(c):
                        for m in range(2):
                            dve.wait_ge(s_dn, e * DN + c * 2 + m + 2 * DN + 2)
                            for t in range(2 * m, 2 * m + 2):
                                h = token_tile(T, c * TB + t)
                                ins = dve.scalar_tensor_tensor(
                                    h, T.PS[:, 4 + (2 * c + m) % 4, (t % 2) * D:(t % 2 + 1) * D],
                                    SC[:, c * TB + t, one(e)], h, ALU.mult, ALU.add)
                            ins.then_inc(s_add, 1)

                    unit(0)
                    for c in range(1, CH):
                        unit(c)
                        add(c - 1)
                    add(CH - 1)
                all_experts(dve, body)


def one(e):
    return bass.ds(e, 1)



RING = 3


def dispatch(pool, xn, dest, rows, zeroed, s_scattered, places, tiles=range(NT)):
    pool.wait_ge(*zeroed)
    for t in tiles:
        for r in range(TOPK):
            pool.indirect_dma_start(out=rows,
                                    out_offset=bass.IndirectOffsetOnAxis(ap=dest[:, r * NT + t:r * NT + t + 1], axis=0),
                                    in_=xn[:, t * D:(t + 1) * D], in_offset=None,
                                    bounds_check=places - 1, oob_is_err=False).then_inc(s_scattered, 16)


def routed_experts(T, w13_dram, w2_dram, rows, results, s_scattered):
    nc = T.nc
    F = EI // P
    TILES = [(c, min(P, CAP - c)) for c in range(0, CAP, P)]
    C = len(TILES)
    FULL = CAP // P
    with ExitStack() as ctx:
        def sb(nm, shape):
            return ctx.enter_context(nc.sbuf_tensor("re_" + nm, shape, F32))

        w13, w2 = sb("w13", [P, RING, KD, 2 * EI]), sb("w2", [P, RING, F, D])
        xe, xeT = sb("xe", [P, RING, C, D]), sb("xeT", [P, RING, KD, CAP])
        sg, hT, ot = sb("sg", [P, F, CAP]), sb("hT", [P, RING, F, CAP]), sb("ot", [P, RING, C, D])
        s_w13, s_w2, s_xe, s_st = ([T.sem(f"re_{x}{q}") for q in range(RING)] for x in (
            "w13_in", "w2_in", "rows_in", "stored"))
        s_t, s_xt, s_gu, s_sg, s_h, s_dn, s_ev = (T.sem("re_" + x) for x in (
            "rows_transposed", "xeT_ready", "gate_up_in_bank", "gate_activated", "h_ready", "down_in_bank",
            "results_copied"))

        def before(q, u):
            return (q - 1, u) if q else (RING - 1, u - 1)

        def steps(eng, body):
            body(0, 0, 0, True, False)
            with eng.Fori(0, (E1 - 2) // RING) as i:
                for j in range(1, RING + 1):
                    body(i * RING + j, j % RING, i + j // RING, False, False)
            body(E1 - 1, (E1 - 1) % RING, (E1 - 1) // RING, False, True)

        with nc.Block() as block:
            @block.sync
            def _(sp):
                for q in range(RING):
                    sp.sem_inc(s_st[q], 1)

                def move(e, q, buf, dram, sem, store):
                    full = buf[:, q, 0:FULL, :], dram[bass.ds(e * CAP, FULL * P), :].rearrange("(c p) d -> p c d", p=P)
                    rest = buf[0:CAP - FULL * P, q, FULL, :], dram[bass.ds(e * CAP + FULL * P, CAP - FULL * P), :]
                    for a, b in (full, rest):
                        if store:
                            a, b = b, a
                        sp.dma_start(a, b).then_inc(sem[q], 16)

                def load_w13(e, q):
                    sp.dma_start(w13[:, q, :, :], w13_dram[bass.ds(e * P, P), :, :]).then_inc(s_w13[q], 16)

                def load_w2(e, q):
                    sp.dma_start(w2[:, q, :, :], w2_dram[bass.ds(e * P, P), :, :]).then_inc(s_w2[q], 16)

                def load_first(e, q):
                    sp.wait_ge(s_gu, F * e + F)
                    move(e + RING, q, xe, rows, s_xe, False)
                    load_w13(e + RING, q)

                def store(e, q):
                    sp.wait_ge(s_ev, e + 2)
                    move(e, q, ot, results, s_st, True)

                def body(e, q, before):
                    load_first(e, q)
                    store(e - 1, before)
                    load_w2(e - 1 + RING, before)

                for e in range(RING):
                    load_w13(e, e)
                    load_w2(e, e)
                sp.wait_ge(s_scattered, 16 * NT * TOPK)
                for e in range(RING):
                    move(e, e, xe, rows, s_xe, False)
                load_first(0, 0)
                body(1, 1, 0)
                with sp.Fori(0, (E1 - RING - 2) // RING) as i:
                    for j in range(2, RING + 2):
                        body(i * RING + j, j % RING, (j - 1) % RING)
                for e in range(E1 - RING - 1, E1):
                    store(e, e % RING)
                    if e == E1 - RING - 1:
                        load_w2(e + RING, e % RING)
                for q in range(RING):
                    sp.wait_ge(s_st[q], 32 * len(range(q, E1, RING)) + 1)

            @block.tensor
            def _(pe):
                def turn(e, q, u):
                    pe.wait_ge(s_xe[q], u * 32 + 32)
                    pe.wait_ge(s_xt, e + 1)
                    for k in range(KD):
                        for c, (c0, m) in enumerate(TILES):
                            ins = pe.transpose(T.PS[:, k, c0:c0 + m], xe[0:m, q, c, k * P:(k + 1) * P],
                                               T.ident[0:m, 0:m])
                    ins.then_inc(s_t, 1)

                def gate_up(e, q, u):
                    pe.wait_ge(s_w13[q], u * 16 + 16)
                    pe.wait_ge(s_xt, e + 2)
                    for f in range(F):
                        pe.wait_ge(s_h, e * F + f + 1)
                        for a in range(2):
                            for k in range(KD):
                                c = a * EI + f * P
                                ins = pe.matmul(T.PS[:, 2 + 2 * f + a, 0:CAP], w13[:, q, k, c:c + P],
                                                xeT[:, q, k, :], start=(k == 0), stop=(k == KD - 1))
                        ins.then_inc(s_gu, 1)

                def down(e, q, u):
                    pe.wait_ge(s_w2[q], u * 16 + 16)
                    pe.wait_ge(s_h, e * F + 2 * F)
                    pe.wait_ge(s_ev, e + 1)
                    for c, (c0, m) in enumerate(TILES):
                        for f in range(F):
                            ins = pe.matmul(T.PS[0:m, 6 + c // 2, c % 2 * D:(c % 2 + 1) * D], hT[:, q, f, c0:c0 + m],
                                            w2[:, q, f, :], start=(f == 0), stop=(f == F - 1))
                    ins.then_inc(s_dn, 1)

                def body(e, q, u, first, last):
                    gate_up(e, q, u)
                    if not last:
                        turn(e + 1, (q + 1) % RING, u + (q + 1) // RING)
                    if not first:
                        down(e - 1, *before(q, u))
                turn(0, 0, 0)
                steps(pe, body)
                down(E1 - 1, (E1 - 1) % RING, (E1 - 1) // RING)

            @block.scalar
            def _(act):
                act.sem_inc(s_xt, 1)

                def transposed(e, q):
                    act.wait_ge(s_t, e + 1)
                    act.activation(xeT[:, q, :, :], T.PS[:, 0:KD, 0:CAP], ACT.Copy).then_inc(s_xt, 1)

                def body(e, q, u, first, last):
                    for f in range(F):
                        act.wait_ge(s_gu, e * F + f + 1)
                        act.wait_ge(s_h, e * F + f + 1)
                        act.activation(sg[:, f, :], T.PS[:, 2 + 2 * f, 0:CAP], ACT.Silu).then_inc(s_sg, 1)
                    if not last:
                        transposed(e + 1, (q + 1) % RING)
                transposed(0, 0)
                steps(act, body)

            @block.vector
            def _(dve):
                dve.sem_inc(s_h, F)
                dve.sem_inc(s_ev, 1)

                def results_out(e, q, u):
                    dve.wait_ge(s_st[q], u * 32 + 1)
                    dve.wait_ge(s_dn, e + 1)
                    dve.tensor_copy(ot[:, q, 0:2, :].rearrange("p c d -> p (c d)"), T.PS[:, 6, :])
                    m = TILES[2][1]
                    dve.tensor_copy(ot[0:m, q, 2, :], T.PS[0:m, 7, 0:D]).then_inc(s_ev, 1)

                def body(e, q, u, first, last):
                    for f in range(F):
                        dve.wait_ge(s_sg, e * F + f + 1)
                        dve.tensor_tensor(hT[:, q, f, :], sg[:, f, :], T.PS[:, 3 + 2 * f, 0:CAP],
                                          ALU.mult).then_inc(s_h, 1)
                    if not first:
                        results_out(e - 1, *before(q, u))
                steps(dve, body)
                results_out(E1 - 1, (E1 - 1) % RING, (E1 - 1) // RING)


E0 = 16
SEG = 256
SEGS = -(-(N * TOPK + E0 * (SEG - 1)) // (SEG * RING)) * RING
EW = KD * 2 * EI + EI // P * D + 4


def segmented_experts(T, w_dram, which, rows, results, s_scattered):
    nc = T.nc
    F = EI // P
    C = SEG // P
    LIMIT, ALPHA = 7.0, 1.702
    with ExitStack() as ctx:
        def sb(nm, shape):
            return ctx.enter_context(nc.sbuf_tensor("se_" + nm, shape, F32))

        ww = sb("ww", [P, RING, EW])
        xe, xeT = sb("xe", [P, RING, C, D]), sb("xeT", [P, RING, KD, SEG])
        g, u_, sg = sb("g", [P, F, SEG]), sb("u", [P, F, SEG]), sb("sg", [P, F, SEG])
        hT, ot = sb("hT", [P, RING, F, SEG]), sb("ot", [P, RING, C, D])
        s_w, s_xe, s_st = ([T.sem(f"se_{x}{q}") for q in range(RING)] for x in ("weights_in", "rows_in", "stored"))
        s_t, s_xt, s_gu, s_clip, s_sg, s_gate, s_h, s_dn, s_ev = (T.sem("se_" + x) for x in (
            "rows_transposed", "xeT_ready", "gate_up_in_bank", "clipped", "gate_activated",
            "factors_ready", "h_ready", "down_in_bank", "results_copied"))

        def before(q, u):
            return (q - 1, u) if q else (RING - 1, u - 1)

        def steps(eng, body):
            body(0, 0, 0, True, False)
            with eng.Fori(0, (SEGS - RING) // RING) as i:
                for j in range(1, RING + 1):
                    body(i * RING + j, j % RING, i + j // RING, False, False)
            for e in range(SEGS - RING + 1, SEGS):
                body(e, e % RING, e // RING, False, e == SEGS - 1)

        with nc.Block() as block:
            @block.gpsimd
            def _(pool):
                def weights(e):
                    if e >= RING:
                        pool.wait_ge(s_dn, e - RING + 1)
                    pool.indirect_dma_start(out=ww[:, e % RING, :], out_offset=None, in_=w_dram,
                                            in_offset=bass.IndirectOffsetOnAxis(ap=which[:, e:e + 1], axis=0),
                                            ).then_inc(s_w[e % RING], 16)
                for e in range(SEGS):
                    weights(e)

            @block.sync
            def _(sp):
                for q in range(RING):
                    sp.sem_inc(s_st[q], 1)

                def at(dram, e):
                    return dram[bass.ds(e * SEG, SEG), :].rearrange("(c p) d -> p c d", p=P)

                def load(e, q):
                    sp.dma_start(xe[:, q, :, :], at(rows, e)).then_inc(s_xe[q], 16)

                def store(e, q):
                    sp.wait_ge(s_ev, e + 2)
                    sp.dma_start(at(results, e), ot[:, q, :, :]).then_inc(s_st[q], 16)

                def body(e, q):
                    sp.wait_ge(s_gu, e + 1)
                    load(e + RING, q)
                    store(e - 1, (q - 1) % RING)

                sp.wait_ge(s_scattered, 16 * NT * TOPK)
                for e in range(RING):
                    load(e, e)
                sp.wait_ge(s_gu, 1)
                load(RING, 0)
                for e in range(1, RING):
                    body(e, e)
                with sp.Fori(0, (SEGS - 2 * RING) // RING) as i:
                    for j in range(RING):
                        body(i * RING + RING + j, j)
                for e in range(SEGS - RING - 1, SEGS):
                    store(e, e % RING)
                for q in range(RING):
                    sp.wait_ge(s_st[q], 16 * (SEGS // RING) + 1)

            @block.tensor
            def _(pe):
                def turn(e, q, u):
                    pe.wait_ge(s_xe[q], u * 16 + 16)
                    pe.wait_ge(s_xt, e + 1)
                    for k in range(KD):
                        for c in range(C):
                            ins = pe.transpose(T.PS[:, 0, k * SEG + c * P:k * SEG + (c + 1) * P],
                                               xe[:, q, c, k * P:(k + 1) * P], T.ident[:, :])
                    ins.then_inc(s_t, 1)

                def gate_up(e, q, u):
                    pe.wait_ge(s_w[q], u * 16 + 16)
                    pe.wait_ge(s_xt, e + 2)
                    pe.wait_ge(s_clip, e * 2 * F + 2 * F)
                    for a in range(2):
                        for f in range(F):
                            for k in range(KD):
                                c = k * 2 * EI + a * EI + f * P
                                ins = pe.matmul(T.PS[:, 1 + a, f * SEG:(f + 1) * SEG], ww[:, q, c:c + P],
                                                xeT[:, q, k, :], start=(k == 0), stop=(k == KD - 1))
                    ins.then_inc(s_gu, 1)

                def down(e, q):
                    pe.wait_ge(s_h, e + 1)
                    pe.wait_ge(s_ev, e + 1)
                    for c in range(C):
                        for f in range(F):
                            w2 = ww[:, q, KD * 2 * EI + f * D:KD * 2 * EI + (f + 1) * D]
                            ins = pe.matmul(T.PS[:, 3, c * D:(c + 1) * D], hT[:, q, f, c * P:(c + 1) * P], w2,
                                            start=(f == 0), stop=(f == F - 1))
                    ins.then_inc(s_dn, 1)

                def body(e, q, u, first, last):
                    gate_up(e, q, u)
                    if not last:
                        turn(e + 1, (q + 1) % RING, u + (q + 1) // RING)
                    if not first:
                        down(e - 1, (q - 1) % RING)
                turn(0, 0, 0)
                steps(pe, body)
                down(SEGS - 1, (SEGS - 1) % RING)

            @block.scalar
            def _(act):
                act.sem_inc(s_xt, 1)
                act.sem_inc(s_ev, 1)

                def transposed(e, q):
                    act.wait_ge(s_t, e + 1)
                    act.activation(xeT[:, q, :, :].rearrange("p k s -> p (k s)"), T.PS[:, 0, :], ACT.Copy)\
                       .then_inc(s_xt, 1)

                def results_out(e, q, u):
                    act.wait_ge(s_st[q], u * 16 + 1)
                    act.wait_ge(s_dn, e + 1)
                    act.activation(ot[:, q, :, :].rearrange("p c d -> p (c d)"), T.PS[:, 3, :], ACT.Copy)\
                       .then_inc(s_ev, 1)

                def body(e, q, u, first, last):
                    if not last:
                        transposed(e + 1, (q + 1) % RING)
                    act.wait_ge(s_clip, e * 2 * F + 2 * F + F)
                    act.activation(sg[:, :, :], g[:, :, :], ACT.Sigmoid, scale=ALPHA).then_inc(s_sg, 1)
                    if not first:
                        results_out(e - 1, *before(q, u))
                transposed(0, 0)
                steps(act, body)
                results_out(SEGS - 1, (SEGS - 1) % RING, (SEGS - 1) // RING)

            @block.vector
            def _(dve):
                dve.sem_inc(s_clip, 2 * F)

                def body(e, q, u, first, last):
                    if not first:
                        dve.wait_ge(s_h, e)
                    dve.wait_ge(s_gu, e + 1)
                    for a, to in enumerate((g, u_)):
                        for f in range(F):
                            bias = KD * 2 * EI + F * D + a * F + f
                            dve.tensor_scalar(to[:, f, :], T.PS[:, 1 + a, f * SEG:(f + 1) * SEG],
                                              ww[:, q, bias:bias + 1], LIMIT, ALU.add, ALU.min).then_inc(s_clip, 1)
                    dve.wait_ge(s_clip, e * 2 * F + 4 * F)
                    dve.tensor_scalar(u_[:, :, :], u_[:, :, :], -LIMIT, 1.0, ALU.max, ALU.add).then_inc(s_gate, 1)
                    dve.wait_ge(s_sg, e + 1)
                    dve.tensor_tensor(g[:, :, :], g[:, :, :], sg[:, :, :], ALU.mult).then_inc(s_gate, 1)
                    dve.wait_ge(s_gate, e * 2 + 2)
                    dve.tensor_tensor(hT[:, q, :, :], g[:, :, :], u_[:, :, :], ALU.mult).then_inc(s_h, 1)
                steps(dve, body)


def clipped_layer(T, w, w_dram, rows, results, zeroed, arrivals, tmp, wgT, wdT):
    nc = T.nc
    with ExitStack() as ctx:
        which = ctx.enter_context(nc.sbuf_tensor("cl_which", [P, SEGS], I32))
        s_scattered = T.sem("cl_rows_scattered")
        with nc.sbuf_tensor("cl_xn", [P, NT * D], F32) as xn:
            norm(T, keep=xn)

            def send(tiles):
                return lambda pool: dispatch(pool, xn, arrivals.index, rows, zeroed, s_scattered, SEGS * SEG, tiles)

            some = NT // 8
            router0(T, w, arrivals.weight, arrivals.index, which, on_pool=send(range(some)))
            fp4_weights(T, w, tmp, wgT, wdT, on_pool=send(range(some, NT)))
        segmented_experts(T, w_dram, which, rows, results, s_scattered)


def zero_places(T, rows, zeros):
    nc = T.nc
    s_made, s_zeroed = T.sem("zeros_made"), T.sem("rows_zeroed")
    part = rows.shape[0] // P * D // zeros.shape[1]
    view = rows.rearrange("(a p c) d -> a p (c d)", p=P, a=part)
    with nc.Block() as block:
        @block.vector
        def _(dve):
            dve.memset(zeros[:, :], 0.0).then_inc(s_made, 1)

        @block.scalar
        def _(act):
            act.wait_ge(s_made, 1)
            for a in range(part):
                act.dma_start(view[a], zeros[:, :]).then_inc(s_zeroed, 16)
    return s_zeroed, 16 * part


def routed_layer(T, w, w13_dram, w2_dram, rows, results, zeroed, arrivals):
    nc = T.nc
    with ExitStack() as ctx:
        def sb(nm, shape, dt=F32):
            return ctx.enter_context(nc.sbuf_tensor("rl_" + nm, shape, dt))

        dest, shared_weight = sb("dest", [P, TOPK * NT], I32), sb("one", [P, NT, 1])
        s_scattered, s_one = T.sem("rl_rows_scattered"), T.sem("rl_one_made")
        with nc.sbuf_tensor("rl_xn", [P, NT * D], F32) as xn:
            norm(T, keep=xn)
            router1(T, w, arrivals.weight, dest, arrivals.index)
            with nc.Block() as block:
                @block.vector
                def _(dve):
                    dve.memset(shared_weight[:, :, :], 1.0).then_inc(s_one, 1)
                    dve.wait_ge(s_one, 1)

            def send(tiles):
                return lambda pool: dispatch(pool, xn, dest, rows, zeroed, s_scattered, E1 * CAP, tiles)

            shared, some = slice(E1 * P, (E1 + 1) * P), NT * 11 // 16
            experts(T, w, "e1_", shared_weight, 1, w13_dram[shared, :, :], w2_dram[shared, :, :],
                    on_pool=send(range(some)))
            ternary_weights(T, w, on_pool=send(range(some, NT)))
        routed_experts(T, w13_dram, w2_dram, rows, results, s_scattered)


class Arrivals:

    def __init__(self, T, sb, name, results):
        self.T, self.results = T, results
        self.index = sb(name + "index", [P, TOPK * NT], I32)
        self.weight = sb(name + "weight", [P, TOPK * NT], F32)
        self.rows = None
        self.s_in = [T.sem(f"{name}rows_in{q}") for q in range(TB)]
        self.s_add = T.sem(name + "added")

    def take_place(self, rows):
        self.rows = rows

    def gather(self, pool):
        for t in range(NT):
            if t >= TB:
                pool.wait_ge(self.s_add, t - TB + 1)
            for r in range(TOPK):
                pool.indirect_dma_start(
                    out=self.rows[:, t % TB, r * D:(r + 1) * D], out_offset=None, in_=self.results,
                    in_offset=bass.IndirectOffsetOnAxis(ap=self.index[:, r * NT + t:r * NT + t + 1], axis=0),
                ).then_inc(self.s_in[t % TB], 16)

    def add(self, dve, st, b):
        for t in range(TB):
            dve.wait_ge(self.s_in[t], 16 * TOPK * b + 16 * TOPK)
            h = token_tile(self.T, b * TB + t)
            for r in range(TOPK):
                ins = dve.scalar_tensor_tensor(h, self.rows[:, t, r * D:(r + 1) * D],
                                               self.weight[:, one(r * NT + b * TB + t)], h, ALU.mult, ALU.add)
                if r < TOPK - 1:
                    st.link(ins)
            ins.then_inc(self.s_add, 1)
        dve.wait_ge(self.s_add, b * TB + TB)



HG = 4
GROUPS = 4


def attention(T, w, name, rope, dv, w_dram, tables, kv=None):
    nc = T.nc
    KK = 1 if kv is not None else KD
    UQ = 2 if rope else 1
    U = 2 * UQ
    QW = UQ * P
    WQ, WK, WV = KD * QW, KK * QW, KK * HG * dv
    KO = max(1, HG * dv // P)
    PO = min(P, HG * dv)
    NCH = TB * HG * dv // P
    WW = WQ + WK + WV + KO * D
    X = TB * HG
    PB = 8
    BANK = [u * HG // U for u in range(U)]
    OB = X * dv // 512 if X * dv >= 512 else 1
    STEPS = B * GROUPS
    with ExitStack() as ctx:
        def sb(nm, shape):
            return ctx.enter_context(nc.sbuf_tensor(name + nm, shape, F32))

        ww = sb("ww", [P, 2, WW])
        xs = sb("xs", [P, KK, S])
        qs = sb("q", [P, 2 if rope else HG, S])
        ks = sb("k", [P, 2 if rope else 1, S])
        rt = sb("rt", [P, 2 * U, S]) if rope else None
        sw = sb("sw", [P, 2, S]) if rope else None
        vs = sb("vs", [P, TB, HG * dv])
        nm, rs, rr = sb("nm", [P, X]), sb("rs", [P, X]), sb("rr", [P, X])
        pe_, pt = sb("p", [P, PB, S]), sb("pt", [P, 4, S])
        o, oT = sb("o", [P, X, dv]), sb("oT", [P, NCH, P])
        s_w = [T.sem(f"{name}weights_in{p}") for p in range(2)]
        (s_src, s_unit, s_v, s_read, s_vs, s_s, s_m, s_exp, s_pt, s_ped, s_pea, s_pv, s_on, s_otr, s_ot, s_o,
         s_add, s_chain) = (T.sem(name + x) for x in (
             "source_copied", "qk_unit_in_banks", "v_in_bank", "qk_unit_read", "v_ready", "scores_in_bank",
             "max_ready", "exp_done", "p_transposed", "pt_even_ready", "pt_odd_ready", "pv_done", "o_normalised",
             "o_transposed", "oT_ready", "out_in_bank", "h_added", "dve_steps"))
        s_qks = T.sem(name + "qk_turned") if rope else s_read
        s_sw = T.sem(name + "halves_swapped") if rope else None
        FREE = 2 if rope else 0

        def steps(eng, first, body):
            if first:
                first((0, 0, 0, 0))
            with eng.Fori(0, STEPS // 2 - 1) as i:
                a, b, c = (i * 2, 0, i, i // 2), (i * 2 + 1, 1, i, i // 2), (i * 2 + 2, 0, i + 1, (i + 1) // 2)
                body(a, b)
                body(b, c)
            i = STEPS // 2 - 1
            a, b = (i * 2, 0, i, i // 2), (i * 2 + 1, 1, i, i // 2)
            body(a, b)
            body(b, None)

        with nc.Block() as block:
            @block.sync
            def _(sp):
                def body(n, p, i, b):
                    sp.wait_ge(s_o, n + 1)
                    group = i % 2 * 2 + p
                    sp.dma_start(ww[:, p, :], w_dram[bass.ds(group * P, P), :]).then_inc(s_w[p], 16)
                    sp.wait_ge(s_v, n + 1)
                    src = T.XT[:, :, bass.ds(b * S, S)] if kv is None else kv[:, bass.ds(b * S, S)]
                    dst = xs[:, :, :] if kv is None else xs[:, 0, :]
                    sp.dma_start(dst, src).then_inc(s_src, 16)
                with sp.Fori(0, STEPS // 2) as i:
                    for p in range(2):
                        body(i * 2 + p, p, i, i // 2)

            if rope:
                @block.gpsimd
                def _(pool):
                    def turned(n):
                        for u in range(U):
                            pool.wait_ge(s_read, FREE + U * n + u + 1)
                            pool.tensor_tensor((qs, ks)[u % 2][:, u // 2, :], rt[:, 2 * u, :], rt[:, 2 * u + 1, :],
                                               ALU.add).then_inc(s_qks, 1)
                    with pool.Fori(0, STEPS) as n:
                        turned(n)

            @block.tensor
            def _(pe):
                pe.sem_inc(s_o, 2)
                pe.sem_inc(s_v, 1)
                pe.sem_inc(s_pt, PB)
                pe.sem_inc(s_pv, 4)

                def weights(p):
                    return (ww[:, p, 0:WQ].rearrange("p (k m) -> p k m", k=KD),
                            ww[:, p, WQ:WQ + WK].rearrange("p (k m) -> p k m", k=KK),
                            ww[:, p, WQ + WK:WQ + WK + WV].rearrange("p (k m) -> p k m", k=KK),
                            ww[:, p, WQ + WK + WV:WW].rearrange("p (k m) -> p k m", k=KO))

                def unit(step, u):
                    n, p, i, b = step
                    if u == 0:
                        pe.wait_ge(s_w[p], i * 16 + 16)
                    pe.wait_ge(s_exp, X * n + X - HG + BANK[u] + 1)
                    j = u % 2
                    kk = KD if j == 0 else KK
                    for k in range(kk):
                        rhs = T.XT[:, k, bass.ds(b * S, S)] if j == 0 or kv is None else kv[:, bass.ds(b * S, S)]
                        c = u // 2 * P
                        ins = pe.matmul(T.PS[:, BANK[u], :], weights(p)[j][:, k, c:c + P], rhs,
                                        start=(k == 0), stop=(k == kk - 1))
                    ins.then_inc(s_unit, 1)

                def values(step):
                    n, p, i, b = step
                    wv = weights(p)[2]
                    pe.wait_ge(s_src, n * 16 + 16)
                    pe.wait_ge(s_read, FREE + U * n + UQ)
                    for t in range(TB):
                        for k in range(KK):
                            c = t * HG * dv
                            ins = pe.matmul(T.PS[:, c // 512, c % 512:c % 512 + HG * dv],
                                            xs[:, k, t * P:(t + 1) * P], wv[:, k, :], start=(k == 0), stop=(k == KK - 1))
                    ins.then_inc(s_v, 1)

                def scores(n, x):
                    qt, h = x // HG, x % HG
                    if qt:
                        pe.wait_ge(s_exp, X * n + X + x - HG + 1)
                    r, q, k = (slice(64 * (h % 2), 64 * (h % 2) + 64), h // 2, h // 2) if rope else (slice(0, P), h, 0)
                    pe.matmul(T.PS[:, h, :], qs[r, q, qt * P:(qt + 1) * P], ks[r, k, :],
                              start=True, stop=True).then_inc(s_s, 1)

                def first_scores(n):
                    pe.wait_ge(s_vs, n + 1)
                    for h in range(HG):
                        if h == 0 or rope and h == 2:
                            pe.wait_ge(s_qks, U * n + (h + 2 if rope else U))
                        scores(n, h)

                def turn(n, x):
                    pe.wait_ge(s_exp, X * n + X + x + 1)
                    pe.wait_ge((s_ped, s_pea)[x % 2], X // 2 * n + x // 2 + 1)
                    for k in range(TB):
                        ins = pe.transpose(T.PS[:, 4 + x % 2, k * P:(k + 1) * P],
                                           pe_[:, x % PB, k * P:(k + 1) * P], T.ident[:, :])
                    ins.then_inc(s_pt, 1)

                def times_v(n, x):
                    h = x % HG
                    pe.wait_ge((s_ped, s_pea)[x % 2], X // 2 * n + x // 2 + 2)
                    if x == 0:
                        pe.wait_ge(s_add, n + 1)
                    c = x * dv
                    for k in range(TB):
                        ins = pe.matmul(T.PS[:, 6 + c // 512, c % 512:c % 512 + dv],
                                        pt[:, x % 4, k * P:(k + 1) * P], vs[:, k, h * dv:(h + 1) * dv],
                                        start=(k == 0), stop=(k == TB - 1))
                    ins.then_inc(s_pv, 1)

                def first(step):
                    for u in range(U):
                        unit(step, u)
                    values(step)
                    first_scores(0)

                def body(step, after):
                    n, p, i, b = step
                    wo = weights(p)[3]
                    for x in range(X):
                        turn(n, x)
                        if x + HG < X:
                            scores(n, x + HG)
                        if x:
                            times_v(n, x - 1)
                        if after and x - X + HG in BANK:
                            unit(after, BANK.index(x - X + HG))
                    times_v(n, X - 1)
                    if after:
                        values(after)
                    pe.wait_ge(s_on, n + 1)
                    of = o[:, :, :].rearrange("p x d -> p (x d)")
                    for j in range(NCH):
                        ins = pe.transpose(T.PS[:, 4 + j // 4, j % 4 * P:(j % 4 + 1) * P],
                                           of[:, j * P:(j + 1) * P], T.ident[:, :])
                    ins.then_inc(s_otr, 1)
                    if after:
                        first_scores(after[0])
                    pe.wait_ge(s_ot, n + 1)
                    for t in range(TB):
                        for k in range(KO):
                            r = slice(0, P) if PO == P else slice(t % 2 * PO, (t % 2 + 1) * PO)
                            j = t * KO + k if PO == P else t // 2
                            bank, half = (t // 2, t % 2) if PO == P else (t % 2, t // 2)
                            ins = pe.matmul(T.PS[:, 6 + bank, half * D:(half + 1) * D],
                                            oT[r, j, :], wo[r, k, :], start=(k == 0), stop=(k == KO - 1))
                    ins.then_inc(s_o, 1)
                steps(pe, first, body)

            @block.scalar
            def _(act):
                act.sem_inc(s_exp, X)
                act.sem_inc(s_pea, 1)

                def values(n):
                    act.wait_ge(s_v, n + 2)
                    src = (T.PS[:, 0:2, :].rearrange("p a b -> p (a b)") if TB * HG * dv == 1024
                           else T.PS[:, 0, 0:TB * HG * dv])
                    act.activation(vs[:, :, :].rearrange("p t c -> p (t c)"), src, ACT.Copy).then_inc(s_vs, 1)

                def exp(n, x):
                    act.wait_ge(s_m, X * n + x + 1)
                    act.wait_ge(s_pt, X * n + x + 1)
                    act.activation(pe_[:, x % PB, :], T.PS[:, x % HG, :], ACT.Exp, bias=nm[:, x:x + 1],
                                   accum_out=rs[:, x:x + 1]).then_inc(s_exp, 1)

                def evacuate(n, x):
                    act.wait_ge(s_pt, X * n + PB + x + 1)
                    act.wait_ge(s_pv, X * n + x + 1)
                    act.activation(pt[:, x % 4, :], T.PS[:, 5, :], ACT.Copy).then_inc(s_pea, 1)

                def swap(n, u):
                    if rope:
                        act.wait_ge(s_unit, U * n + u + 1)
                        act.wait_ge(s_read, U * n + u + 1)
                        for a in range(0, P, 64):
                            for half in (0, 32):
                                ins = act.activation(sw[a + 32 - half:a + 64 - half, u % 2, :],
                                                     T.PS[a + half:a + half + 32, BANK[u], :], ACT.Copy)
                        ins.then_inc(s_sw, 1)

                def first(step):
                    for u in range(U):
                        swap(0, u)
                    values(0)
                    for h in range(HG):
                        exp(0, h)

                def body(step, after):
                    n = step[0]
                    for x in range(0, X, 2):
                        if x + HG < X:
                            exp(n, x + HG)
                        evacuate(n, x + 1)
                        if x + HG < X:
                            exp(n, x + HG + 1)
                        if after and x >= X - HG:
                            for u in range(U // 2):
                                swap(after[0], (x - X + HG) // 2 * (U // 2) + u)
                    if after:
                        values(after[0])
                    act.wait_ge(s_otr, n + 1)
                    src = T.PS[:, 4:6, :].rearrange("p a b -> p (a b)") if NCH > 4 else T.PS[:, 4, 0:NCH * P]
                    act.activation(oT[:, :, :].rearrange("p j q -> p (j q)"), src, ACT.Copy).then_inc(s_ot, 1)
                    if after:
                        for h in range(HG):
                            exp(after[0], h)
                steps(act, first, body)

            @block.vector
            def _(dve):
                w.wait(dve, "l1_rope" if rope else "l3_head")
                dve.sem_inc(s_ped, 1)
                if rope:
                    dve.sem_inc(s_read, FREE)
                dve.sem_inc(s_add, 1)

                def unit(n, u):
                    dve.wait_ge(s_unit, U * n + u + 1)
                    j = u % 2
                    if rope:
                        dve.wait_ge(s_sw, U * n + u + 1)
                        dve.tensor_tensor(rt[:, 2 * u, :], T.PS[:, BANK[u], :], tables[:, 2 * j, :], ALU.mult)
                        ins = dve.tensor_tensor(rt[:, 2 * u + 1, :], sw[:, u % 2, :], tables[:, 2 * j + 1, :], ALU.mult)
                    elif j == 0:
                        for h in range(HG):
                            ins = dve.tensor_scalar(qs[:, h, :], T.PS[:, BANK[u], :], tables[:, h:h + 1], None,
                                                    ALU.mult)
                    else:
                        ins = dve.tensor_scalar(ks[:, 0, :], T.PS[:, BANK[u], :], 0.25, None, ALU.mult)
                    ins.then_inc(s_read, 1)

                def maximum(n, x):
                    dve.wait_ge(s_s, X * n + x + 1)
                    dve.tensor_reduce(nm[:, x:x + 1], T.PS[:, x % HG, :], AX.X, ALU.max, negate=True).then_inc(s_m, 1)

                def evacuate(n, x):
                    dve.wait_ge(s_pt, X * n + PB + x + 1)
                    dve.wait_ge(s_pv, X * n + x + 1)
                    dve.tensor_copy(pt[:, x % 4, :], T.PS[:, 4, :]).then_inc(s_ped, 1)

                def first(step):
                    for u in range(U):
                        unit(0, u)
                    for h in range(HG):
                        maximum(0, h)

                def body(step, after):
                    n, p, i, b = step
                    for x in range(0, X, 2):
                        evacuate(n, x)
                        for h in range(HG, HG + 2):
                            if x + h < X:
                                maximum(n, x + h)
                        if after and x == X - HG:
                            unit(after[0], 0)
                    dve.wait_ge(s_exp, X * n + 2 * X)
                    dve.reciprocal(rr[:, :], rs[:, :]).then_inc(s_chain, 1)
                    if after:
                        unit(after[0], 1)
                    dve.wait_ge(s_chain, n + 1)
                    dve.wait_ge(s_pv, X * n + X + 4)
                    XB = X // OB
                    for a in range(OB):
                        ins = dve.tensor_tensor(o[:, a * XB:(a + 1) * XB, :],
                                                T.PS[:, 6 + a, 0:XB * dv].rearrange("p (x d) -> p x d", d=dv),
                                                spread(rr[:, a * XB:(a + 1) * XB], dv), ALU.mult)
                    ins.then_inc(s_on, 1)
                    if after:
                        for u in range(2, U):
                            unit(after[0], u)
                        for h in range(HG):
                            maximum(after[0], h)
                    dve.wait_ge(s_o, n + 3)
                    h = T.H[:, bass.ds(b * TB * D, TB * D)]
                    if PO == P:
                        out = T.PS[:, 6:8, :].rearrange("p a b -> p (a b)")
                    else:
                        h = h.rearrange("p (t d) -> p t d", d=D)
                        out = T.PS[:, 6:8, :].rearrange("p a (b d) -> p b a d", d=D)
                        h = h.rearrange("p (b a) d -> p b a d", a=2)
                    dve.tensor_tensor(h, h, out, ALU.add).then_inc(s_add, 1)
                steps(dve, first, body)


def compress_kv(T, w, kv):
    nc = T.nc
    s_kv, s_done = T.sem("kv_in_bank"), T.sem("kv_ready")
    with nc.Block() as block:
        @block.tensor
        def _(pe):
            w.wait(pe, "l1_kvd")
            for c in range(CH):
                for k in range(KD):
                    ins = pe.matmul(T.PS[:, c, :], w.l1_kvd[:, k, :], T.XT[:, k, c * S:(c + 1) * S],
                                    start=(k == 0), stop=(k == KD - 1))
                ins.then_inc(s_kv, 1)

        @block.scalar
        def _(act):
            for c in range(CH):
                act.wait_ge(s_kv, c + 1)
                act.activation(kv[:, c * S:(c + 1) * S], T.PS[:, c, :], ACT.Copy).then_inc(s_done, 1)
            act.wait_ge(s_done, CH)



LM = 64


def landmark_attention(T, w):
    nc = T.nc
    with ExitStack() as ctx:
        def sb(nm, shape):
            return ctx.enter_context(nc.sbuf_tensor("la_" + nm, shape, F32))

        xs = sb("xs", [P, 2, KD, S])
        e = sb("e", [P, 2 * TB, D])
        k3 = sb("k3", [P, TB, D])
        nm, rs, rr = sb("nm", [P, 2 * TB]), sb("rs", [P, 2 * TB]), sb("rr", [P, 2 * TB])
        qT, kT, klT = sb("qT", [P, KD, S]), sb("kT", [P, KD, S]), sb("klT", [P, KD, LM])
        k2T, mid, k1T = sb("k2T", [P, TB, LM]), sb("mid", [LM, D]), sb("k1T", [LM, S])
        LT = LM // TB
        s_xs = [T.sem(f"la_x_arrived{p}") for p in range(2)]
        s_qk, s_v, s_m, s_e, s_n, s_k3, s_kl, s_tq, s_tk, s_klT, s_qT, s_kT, s_k2, s_k2T, s_k1, s_k1T, \
            s_mid, s_midT, s_o, s_add, s_steps = (T.sem("la_" + x) for x in (
                "qk_in_bank", "v_in_bank", "max_ready", "exp_done", "qk_normalised", "k3_ready",
                "landmarks_in_bank", "q_transposed", "k_transposed", "klT_ready", "qT_ready", "kT_ready",
                "k2_in_bank", "k2T_ready", "k1_in_bank", "k1T_ready", "mid_in_bank", "mid_ready", "out_in_bank",
                "h_added", "dve_steps"))

        def steps(eng, body):
            with eng.Fori(0, B // 2) as i:
                for p in range(2):
                    body(i * 2 + p, p, i)

        with nc.Block() as block:
            @block.sync
            def _(sp):
                def body(b, p, i):
                    sp.wait_ge(s_v, b + 1)
                    sp.dma_start(xs[:, p, :, :], T.XT[:, :, bass.ds(b * S, S)]).then_inc(s_xs[p], 16)
                steps(sp, body)

            @block.tensor
            def _(pe):
                w.wait(pe, "l2_w", "l2_b", "l2_avg")
                pe.sem_inc(s_v, 2)

                def body(b, p, i):
                    pe.wait_ge(s_xs[p], 16 * i + 16)
                    pe.wait_ge(s_qT, b + 1)
                    pe.wait_ge(s_kT, b + 1)
                    for t in range(TB):
                        out = T.PS[:, t, :]
                        pe.matmul(out, T.ones[0:1, :], w.l2_b[0:1, 0:2 * D], start=True, stop=False)
                        for k in range(KD):
                            ins = pe.matmul(out, xs[:, p, k, t * P:(t + 1) * P], w.l2_w[:, k, 0:2 * D],
                                            start=False, stop=(k == KD - 1))
                        ins.then_inc(s_qk, 1)
                    pe.wait_ge(s_add, b + 1)
                    for t in range(TB):
                        out = T.PS[:, 4 + t // 2, (t % 2) * D:(t % 2 + 1) * D]
                        pe.matmul(out, T.ones[0:1, :], w.l2_b[0:1, 2 * D:3 * D], start=True, stop=False)
                        for k in range(KD):
                            ins = pe.matmul(out, xs[:, p, k, t * P:(t + 1) * P], w.l2_w[:, k, 2 * D:3 * D],
                                            start=False, stop=(k == KD - 1))
                    ins.then_inc(s_v, 1)
                    pe.wait_ge(s_n, b + 1)
                    for t in range(TB):
                        for k in range(KD):
                            c = k * LM + t * LT
                            ins = pe.matmul(T.PS[:, 6, c:c + LT], e[:, 2 * t + 1, k * P:(k + 1) * P],
                                            w.l2_avg[:, :], start=True, stop=True)
                    ins.then_inc(s_kl, 1)
                    for j, s_t in ((1, s_tk), (0, s_tq)):
                        for t in range(TB):
                            for k in range(KD):
                                ins = pe.transpose(T.PS[:, 2 * j + k, t * P:(t + 1) * P],
                                                   e[:, 2 * t + j, k * P:(k + 1) * P], T.ident[:, :])
                        ins.then_inc(s_t, 1)
                    pe.wait_ge(s_kT, b + 2)
                    pe.wait_ge(s_klT, b + 1)
                    for t in range(TB):
                        for k in range(KD):
                            ins = pe.matmul(T.PS[:, 7, t * LM:(t + 1) * LM], kT[:, k, t * P:(t + 1) * P],
                                            klT[:, k, :], start=(k == 0), stop=(k == KD - 1))
                    ins.then_inc(s_k2, 1)
                    pe.wait_ge(s_qT, b + 2)
                    pe.wait_ge(s_k3, b + 1)
                    for k in range(KD):
                        ins = pe.matmul(T.PS[0:LM, 4, :], klT[:, k, :], qT[:, k, :],
                                        start=(k == 0), stop=(k == KD - 1))
                    ins.then_inc(s_k1, 1)
                    pe.wait_ge(s_k2T, b + 1)
                    for t in range(TB):
                        ins = pe.matmul(T.PS[0:LM, 6, D:2 * D], k2T[:, t, :], k3[:, t, :],
                                        start=(t == 0), stop=(t == TB - 1))
                    ins.then_inc(s_mid, 1)
                    pe.wait_ge(s_k1T, b + 1)
                    pe.wait_ge(s_midT, b + 1)
                    for t in range(TB):
                        ins = pe.matmul(T.PS[:, 4 + t // 2, (t % 2) * D:(t % 2 + 1) * D], k1T[:, t * P:(t + 1) * P],
                                        mid[:, :], start=True, stop=True)
                    ins.then_inc(s_o, 1)
                steps(pe, body)

            @block.scalar
            def _(act):
                act.sem_inc(s_qT, 1)

                def body(b, p, i):
                    for t in range(TB):
                        act.wait_ge(s_m, TB * b + t + 1)
                        for j in range(2):
                            ins = act.activation(e[:, 2 * t + j, :], T.PS[:, t, j * D:(j + 1) * D], ACT.Exp,
                                                 bias=nm[:, 2 * t + j:2 * t + j + 1],
                                                 accum_out=rs[:, 2 * t + j:2 * t + j + 1])
                            ins.then_inc(s_e, 1)
                    act.wait_ge(s_kl, b + 1)
                    act.activation(klT[:, :, :].rearrange("p k l -> p (k l)"), T.PS[:, 6, 0:KD * LM],
                                   ACT.Copy).then_inc(s_klT, 1)
                    act.wait_ge(s_tq, b + 1)
                    act.activation(qT[:, :, :], T.PS[:, 0:2, :], ACT.Copy).then_inc(s_qT, 1)
                    act.wait_ge(s_k2, b + 1)
                    act.activation(k2T[:, :, :].rearrange("p t l -> p (t l)"), T.PS[:, 7, 0:TB * LM],
                                   ACT.Copy).then_inc(s_k2T, 1)
                    act.wait_ge(s_mid, b + 1)
                    act.activation(mid[:, :], T.PS[0:LM, 6, D:2 * D], ACT.Copy).then_inc(s_midT, 1)
                steps(act, body)

            @block.vector
            def _(dve):
                dve.sem_inc(s_kT, 1)
                dve.sem_inc(s_add, 1)

                def body(b, p, i):
                    for t in range(TB):
                        dve.wait_ge(s_qk, TB * b + t + 1)
                        dve.tensor_reduce(nm[:, 2 * t:2 * t + 2], T.PS[:, t, :].rearrange("p (j d) -> p j d", j=2),
                                          AX.X, ALU.max, negate=True).then_inc(s_m, 1)
                    st = Steps(dve, s_steps, b * 1)
                    dve.wait_ge(s_e, 2 * TB * b + 2 * TB)
                    st.link(dve.reciprocal(rr[:, :], rs[:, :]))
                    dve.tensor_tensor(e[:, :, :], e[:, :, :], spread(rr[:, :], D), ALU.mult).then_inc(s_n, 1)
                    dve.wait_ge(s_v, b + 3)
                    dve.wait_ge(s_n, b + 1)
                    ke = e[:, :, :].rearrange("p (t j) d -> p t j d", j=2)[:, :, 1, :]
                    dve.tensor_tensor(k3[:, :, :], ke, T.PS[:, 4:6, :].rearrange("p a (b d) -> p (a b) d", d=D),
                                      ALU.mult).then_inc(s_k3, 1)
                    dve.wait_ge(s_tk, b + 1)
                    dve.tensor_copy(kT[:, :, :], T.PS[:, 2:4, :]).then_inc(s_kT, 1)
                    dve.wait_ge(s_k1, b + 1)
                    dve.tensor_copy(k1T[:, :], T.PS[0:LM, 4, :]).then_inc(s_k1T, 1)
                    dve.wait_ge(s_o, b + 1)
                    h = T.H[:, bass.ds(b * TB * D, TB * D)]
                    dve.tensor_tensor(h, h, T.PS[:, 4:6, :].rearrange("p a b -> p (a b)"), ALU.add).then_inc(s_add, 1)
                steps(dve, body)



FF = 4 * D
MAGIC = 1.5 * 2 ** 23


def ternary_weights(T, w, on_pool):
    nc = T.nc
    with ExitStack() as ctx:
        def sb(nm, shape):
            return ctx.enter_context(nc.sbuf_tensor("tw_" + nm, shape, F32))

        part, sc, rc = sb("part", [P, 2]), sb("sc", [P, 2]), sb("rc", [P, 2])
        q = sb("q", [P, KD * FF])
        s_part, s_total, s_steps = (T.sem("tw_" + x) for x in ("sums_of_partitions", "totals_in_bank", "dve_steps"))
        with nc.Block() as block:
            @block.gpsimd
            def _(pool):
                on_pool(pool)

            @block.tensor
            def _(pe):
                pe.wait_ge(s_part, 1)
                pe.matmul(T.PS[:, 0, 0:2], T.ones[:, :], part[:, :], start=True, stop=True).then_inc(s_total, 1)

            @block.vector
            def _(dve):
                w.wait(dve, "l2_w1", "l2_w2")
                st = Steps(dve, s_steps)
                flat = [w.l2_w1[:, :, :].rearrange("p k n -> p (k n)"), w.l2_w2[:, :, :].rearrange("p k n -> p (k n)")]
                for j in range(2):
                    st.step(dve.tensor_reduce(part[:, j:j + 1], flat[j], AX.X, ALU.add, apply_absolute_value=True))
                st.settled()
                st.link(dve.tensor_copy(sc[:, :], part[:, :]))
                dve.nop().then_inc(s_part, 1)
                dve.wait_ge(s_total, 1)
                st.link(dve.tensor_scalar(sc[:, :], T.PS[:, 0, 0:2], 1.0 / (FF * D), 1e-8, ALU.mult, ALU.max))
                st.link(dve.reciprocal(rc[:, :], sc[:, :]))
                for j in range(2):
                    st.link(dve.tensor_scalar(q[:, :], flat[j], rc[:, j:j + 1], MAGIC, ALU.mult, ALU.add))
                    st.link(dve.tensor_scalar(q[:, :], q[:, :], MAGIC, 1.0, ALU.subtract, ALU.min))
                    st.link(dve.tensor_scalar(q[:, :], q[:, :], -1.0, None, ALU.max))
                    st.link(dve.tensor_tensor(q[:, :], q[:, :], flat[j], ALU.subtract))
                    st.link(dve.tensor_tensor(flat[j], flat[j], q[:, :], ALU.add))


def ternary_ffn(T, w):
    nc = T.nc
    FT = FF // P
    with ExitStack() as ctx:
        def sb(nm, shape):
            return ctx.enter_context(nc.sbuf_tensor("tf_" + nm, shape, F32))

        hT = sb("hT", [P, 2, FT, S])
        s_h, s_g, s_o, s_add = (T.sem("tf_" + x) for x in ("h_in_bank", "gelu_done", "out_in_bank", "h_added"))
        with nc.Block() as block:
            @block.tensor
            def _(pe):
                w.wait(pe, "l2_b2")
                pe.sem_inc(s_o, 4)

                with pe.Fori(0, CH // 2) as i:
                    for p in range(2):
                        c = i * 2 + p
                        for f in range(FT):
                            pe.wait_ge(s_g, FT * c + f + 1)
                            for k in range(KD):
                                ins = pe.matmul(T.PS[:, f % 4, :], w.l2_w1[:, k, f * P:(f + 1) * P],
                                                T.XT[:, k, bass.ds(c * S, S)], start=(k == 0), stop=(k == KD - 1))
                            ins.then_inc(s_h, 1)
                        pe.wait_ge(s_g, FT * c + FT + 4)
                        for g in range(2):
                            pe.wait_ge(s_add, 2 * c + g + 1)
                            for t in range(2 * g, 2 * g + 2):
                                out = T.PS[:, 4 + 2 * p + g, (t % 2) * D:(t % 2 + 1) * D]
                                pe.matmul(out, T.ones[0:1, :], w.l2_b2[0:1, :], start=True, stop=False)
                                for f in range(FT):
                                    ins = pe.matmul(out, hT[:, p, f, t * P:(t + 1) * P], w.l2_w2[:, f, :],
                                                    start=False, stop=(f == FT - 1))
                            ins.then_inc(s_o, 1)

            @block.scalar
            def _(act):
                w.wait(act, "l2_b1")
                act.sem_inc(s_g, 4)
                with act.Fori(0, CH // 2) as i:
                    for p in range(2):
                        c = i * 2 + p
                        act.wait_ge(s_o, 2 * c + 2)
                        for f in range(FT):
                            act.wait_ge(s_h, FT * c + f + 1)
                            act.activation(hT[:, p, f, :], T.PS[:, f % 4, :], ACT.Gelu,
                                           bias=w.l2_b1[:, f:f + 1]).then_inc(s_g, 1)

            @block.vector
            def _(dve):
                dve.sem_inc(s_add, 4)
                with dve.Fori(0, CH // 2) as i:
                    for p in range(2):
                        c = i * 2 + p
                        for g in range(2):
                            dve.wait_ge(s_o, 4 + 2 * c + g + 1)
                            h = T.H[:, bass.ds((c * TB + 2 * g) * D, 2 * D)]
                            dve.tensor_tensor(h, h, T.PS[:, 4 + 2 * p + g, :], ALU.add).then_inc(s_add, 1)



I3 = 704
FT3 = -(-I3 // P)


def fp4_weights(T, w, tmp, wgT, wdT, on_pool=None):
    nc = T.nc
    s_q, s_steps, s_tr, s_ev = (T.sem("q3_" + x) for x in ("quantised", "dve_steps", "transposed", "evacuated"))
    R = FT3 * D

    with nc.Block() as block:
        if on_pool:
            @block.gpsimd
            def _(pool):
                on_pool(pool)

        @block.vector
        def _(dve):
            w.wait(dve, "l3_wg", "l3_wu", "l3_wd")
            st = Steps(dve, s_steps)
            for m, n in ((w.l3_wg, R), (w.l3_wu, R), (w.l3_wd, KD * I3)):
                flat = m[:, :, :].rearrange("p k n -> p (k n)")
                for a in range(0, n, n // 2):
                    fp4_blocks(dve, st, flat[:, a:a + n // 2], flat[:, a:a + n // 2], tmp, 16, False)
                dve.nop().then_inc(s_q, 1)

        @block.tensor
        def _(pe):
            job = 0
            for j, m in enumerate((w.l3_wg, w.l3_wu)):
                pe.wait_ge(s_q, j + 1)
                for k in range(KD):
                    for half in range(2):
                        if job >= 4:
                            pe.wait_ge(s_ev, job - 3)
                        for r in range(3):
                            ins = pe.transpose(T.PS[:, job % 4, r * P:(r + 1) * P],
                                               m[:, half * 3 + r, k * P:(k + 1) * P], T.ident[:, :])
                        ins.then_inc(s_tr, 1)
                        job += 1
            pe.wait_ge(s_q, 3)
            for f in range(FT3):
                n = min(P, I3 - f * P)
                pe.wait_ge(s_ev, job - 3)
                for k in range(KD):
                    ins = pe.transpose(T.PS[0:n, job % 4, k * P:(k + 1) * P], w.l3_wd[:, k, f * P:f * P + n],
                                       T.ident[:, :])
                ins.then_inc(s_tr, 1)
                job += 1

        @block.scalar
        def _(act):
            job = 0
            for j in range(2):
                for k in range(KD):
                    for half in range(2):
                        act.wait_ge(s_tr, job + 1)
                        act.activation(wgT[:, k, j, half * 3 * P:(half + 1) * 3 * P], T.PS[:, job % 4, 0:3 * P],
                                       ACT.Copy).then_inc(s_ev, 1)
                        job += 1
            for f in range(FT3):
                n = min(P, I3 - f * P)
                act.wait_ge(s_tr, job + 1)
                act.activation(wdT[0:n, f, :], T.PS[0:n, job % 4, 0:D], ACT.Copy).then_inc(s_ev, 1)
                job += 1


def fp4_ffn(T, w, tmp, wgT, wdT, out):
    nc = T.nc
    HI = I3 // 2
    with ExitStack() as ctx:
        def sb(nm, shape):
            return ctx.enter_context(nc.sbuf_tensor("f3_" + nm, shape, F32))

        xs = sb("xs", [P, 2, KD, P])
        sg, h, hT = sb("sg", [P, 2, I3]), sb("h", [P, 2, I3]), sb("hT", [P, 2, FT3, P])
        s_xs = [T.sem(f"f3_x_arrived{p}") for p in range(2)]
        s_gu, s_sg, s_hm, s_q, s_steps, s_tr, s_ev, s_o, s_add, s_out = (T.sem("f3_" + x) for x in (
            "gate_up_in_bank", "silu_done", "product_done", "quantised", "dve_steps", "h_transposed",
            "hT_ready", "out_in_bank", "h_added", "out_written"))
        ST = FP4_STEPS

        def steps(eng, body, last=None):
            with eng.Fori(0, NT // 2 - 1) as i:
                for p in range(2):
                    body(i * 2 + p, p, i)
            body(NT - 2, 0, NT // 2 - 1)
            (last or body)(NT - 1, 1, NT // 2 - 1)

        with nc.Block() as block:
            @block.sync
            def _(sp):
                def body(n, p, i):
                    sp.wait_ge(s_gu, n + 1)
                    sp.dma_start(xs[:, p, :, :], T.XT[:, :, bass.ds(n * P, P)]).then_inc(s_xs[p], 16)
                steps(sp, body)

            @block.tensor
            def _(pe):
                pe.sem_inc(s_gu, 2)

                def gate_up(n, p, i):
                    pe.wait_ge(s_xs[p], 16 * i + 16)
                    pe.wait_ge(s_hm, n + 1)
                    for j in range(2):
                        for a in range(2):
                            for k in range(KD):
                                ins = pe.matmul(T.PS[:, 2 * j + a, 0:HI], xs[:, p, k, :],
                                                wgT[:, k, j, a * HI:(a + 1) * HI], start=(k == 0), stop=(k == KD - 1))
                    ins.then_inc(s_gu, 1)

                def rest(n, p, i=None):
                    pe.wait_ge(s_q, n + 1)
                    pe.wait_ge(s_ev, n + 1)
                    for f in range(FT3):
                        m = min(P, I3 - f * P)
                        ins = pe.transpose(T.PS[0:m, 4 + f // 4, f % 4 * P:(f % 4 + 1) * P],
                                           h[:, p, f * P:f * P + m], T.ident[:, :])
                    ins.then_inc(s_tr, 1)
                    pe.wait_ge(s_ev, n + 2)
                    pe.wait_ge(s_add, n + 1)
                    for f in range(FT3):
                        m = min(P, I3 - f * P)
                        ins = pe.matmul(T.PS[:, 6 + p, 0:D], hT[0:m, p, f, :], wdT[0:m, f, :],
                                        start=(f == 0), stop=(f == FT3 - 1))
                    ins.then_inc(s_o, 1)

                def body(n, p, i):
                    gate_up(n + 1, 1 - p, i + p)
                    rest(n, p)
                gate_up(0, 0, 0)
                steps(pe, body, rest)

            @block.scalar
            def _(act):
                act.sem_inc(s_ev, 1)

                def silu(n, p):
                    act.wait_ge(s_gu, n + 3)
                    act.wait_ge(s_hm, n + 1)
                    act.activation(sg[:, p, :].rearrange("p (a n) -> p a n", a=2), T.PS[:, 0:2, 0:HI],
                                   ACT.Silu).then_inc(s_sg, 1)

                def rest(n, p, i=None):
                    act.wait_ge(s_tr, n + 1)
                    act.activation(hT[:, p, 0:5, :].rearrange("p f q -> p (f q)")[:, 0:512], T.PS[:, 4, :], ACT.Copy)
                    act.activation(hT[:, p, 4, :], T.PS[:, 5, 0:P], ACT.Copy)
                    act.activation(hT[0:64, p, 5, :], T.PS[0:64, 5, P:2 * P], ACT.Copy).then_inc(s_ev, 1)

                def body(n, p, i):
                    silu(n + 1, 1 - p)
                    rest(n, p)
                silu(0, 0)
                steps(act, body, rest)

            @block.vector
            def _(dve):
                dve.sem_inc(s_hm, 1)
                dve.sem_inc(s_add, 2)

                def product(n, p):
                    dve.wait_ge(s_sg, n + 1)
                    dve.tensor_tensor(h[:, p, :].rearrange("p (a n) -> p a n", a=2),
                                      sg[:, p, :].rearrange("p (a n) -> p a n", a=2), T.PS[:, 2:4, 0:HI],
                                      ALU.mult).then_inc(s_hm, 1)

                def rest(n, p, i=None):
                    st = Steps(dve, s_steps, n * ST)
                    dve.wait_ge(s_hm, n + 2)
                    fp4_blocks(dve, st, h[:, p, :], h[:, p, :], tmp, 16, False)
                    dve.nop().then_inc(s_q, 1)
                    assert st.n == ST

                def add(n, p, i=None):
                    dve.wait_ge(s_o, n + 1)
                    ht = token_tile(T, n)
                    dve.tensor_tensor(ht, ht, T.PS[:, 6 + p, 0:D], ALU.add).then_inc(s_add, 1)

                product(0, 0)
                rest(0, 0)

                def body(n, p, i):
                    product(n + 1, 1 - p)
                    rest(n + 1, 1 - p)
                    add(n, p)
                steps(dve, body, add)

            @block.gpsimd
            def _(pool):
                def body(n, p, i):
                    pool.wait_ge(s_add, n + 3)
                    pool.dma_start(out[bass.ds(n * P, P), :], token_tile(T, n)).then_inc(s_out, 16)
                steps(pool, body)
                pool.wait_ge(s_out, 16 * NT)



class Weights:

    def __init__(self, T, only, sb=None):
        self.T, self.only, self.tensors = T, tuple(only), {}
        self.sb = sb or T.sb
        self.l0_uv = self.place("l0_uv", [P, KD, 2 * D1])
        self.l0_uvb = self.place("l0_uvb", [P, 2 * D1 // P])
        self.l0_t = self.place("l0_t", [P, D1 // P, B])
        self.l0_o = self.place("l0_o", [P, D1 // P, D])
        self.l0_ob = self.place("l0_ob", [1, D])
        self.l0_rw = self.place("l0_rw", [P, KD, 16])
        self.l0_rb = self.place("l0_rb", [1, 16])
        self.l0_db = self.place("l0_db", [16, D])
        self.l1_wg = self.place("l1_wg", [P, KD, 32])
        self.l1_kvd = self.place("l1_kvd", [P, KD, P])
        self.l1_rope = self.place("l1_rope", [P, 4, S])
        self.l1_nw = self.place("l1_nw", [P, KD])
        self.l2_w = self.place("l2_w", [P, KD, 3 * D])
        self.l2_b = self.place("l2_b", [1, 3 * D])
        self.l2_avg = self.place("l2_avg", [P, P * LM // S])
        self.l2_w1 = self.place("l2_w1", [P, KD, FF])
        self.l2_b1 = self.place("l2_b1", [P, FF // P])
        self.l2_w2 = self.place("l2_w2", [P, FF // P, D])
        self.l2_b2 = self.place("l2_b2", [1, D])
        self.l3_head = self.place("l3_head", [P, HG])
        self.l3_wg = self.place("l3_wg", [P, FT3, D])
        self.l3_wu = self.place("l3_wu", [P, FT3, D])
        self.l3_wd = self.place("l3_wd", [P, KD, I3])
        self.loaded = {x: T.sem(f"loaded_{x}_{len(self.only)}") for x in sorted({n[0:2] for n in self.tensors})}

    def place(self, name, shape):
        if not name.startswith(self.only):
            return None
        self.tensors[name] = self.sb("w_" + name, shape)
        return self.tensors[name]

    def load(self, eng, name, src):
        t = self.tensors[name]
        eng.dma_start(t[:, :] if len(t.shape) == 2 else t[:, :, :], src).then_inc(self.loaded[name[0:2]], 16)

    def wait(self, eng, *names):
        for x in sorted({n[0:2] for n in names}):
            eng.wait_ge(self.loaded[x], 16 * sum(n[0:2] == x for n in self.tensors))


def load_weights(T, w, dram):
    with T.nc.Block() as block:
        @block.sync
        def _(sp):
            for name in w.tensors:
                w.load(sp, name, dram[name])




def by_partition(a, k):
    return a.reshape(k, a.shape[0] // k, a.shape[1]).transpose(1, 0, 2)


def lay_out(inp):
    import numpy as np
    f = {k: np.asarray(v) for k, v in inp.items()}
    cat = np.concatenate
    a = {}
    a["ids"] = f["x"].reshape(NT, P).T
    a["table"] = f["L0_tok_embedding"]
    a["l0_uv"] = by_partition(cat([f["L0_attn_u_w"], f["L0_attn_v_w"]]).T, KD)
    a["l0_uvb"] = cat([f["L0_attn_u_b"], f["L0_attn_v_b"]]).reshape(2 * D1 // P, P).T
    t = cat([f["L0_attn_t_zero"], f["L0_attn_t_pos"][:, :B - 1]], 1)
    a["l0_t"] = by_partition(np.repeat(t, D1 // TH, axis=0), D1 // P)
    a["l0_o"] = by_partition(f["L0_attn_o_w"].T, D1 // P)
    a["l0_ob"] = f["L0_attn_o_b"][None]
    a["l0_rw"] = by_partition(f["L0_ffn_router_w"], KD)
    a["l0_rb"] = f["L0_ffn_router_b"][None]
    a["l0_db"] = f["L0_ffn_down_bias"]

    def experts_by_partition(x):
        x = x.reshape(x.shape[0], x.shape[1] // P, P, x.shape[2]).transpose(0, 2, 1, 3)
        return x.reshape(x.shape[0] * P, x.shape[2], x.shape[3])

    gu, gub = f["L0_ffn_gate_up_proj"], f["L0_ffn_gate_up_bias"]
    parts = (experts_by_partition(cat([gu[:, :, 0::2], gu[:, :, 1::2]], 2)),
             experts_by_partition(f["L0_ffn_down_proj"]),
             cat([gub[:, 0::2], gub[:, 1::2]], 1).reshape(E0, 4, P).transpose(0, 2, 1))
    a["l0_ew"] = cat([x.reshape(E0 * P, -1) for x in parts], 1)
    a["l1_wg"] = by_partition(f["L1_ffn_wg"].T, KD)
    w1, w3, w2 = (cat([f["L1_ffn_w" + n], f["L1_ffn_sw" + n][None]]) for n in "132")
    a["l1_w13"] = experts_by_partition(cat([w1, w3], 2))
    a["l1_w2"] = experts_by_partition(w2)
    def side_by_side(*xs):
        out = []
        for x in xs:
            if x.shape[1] < P:
                x = cat([x, x], 1)
            k = x.shape[1] // P
            out.append(x.reshape(GROUPS, k, P, x.shape[2]).transpose(0, 2, 1, 3).reshape(GROUPS * P, -1))
        return cat(out, 1)

    def columns(x, n):
        return x.reshape(x.shape[0], GROUPS, n).transpose(1, 0, 2)

    a["l1_kvd"] = by_partition(f["L1_attn_kv_down"], KD)
    a["l1_nw"] = f["L1_attn_norm_w"].reshape(KD, P).T
    a["l1_aw"] = side_by_side(columns(f["L1_attn_wq"], 256), columns(f["L1_attn_wk"], 256), columns(f["L1_attn_wv"], 256),
                              f["L1_attn_wo"].reshape(GROUPS, 256, D))
    inv = (1.0 / (10000.0 ** (np.arange(0, 64, 2, dtype=np.float32) / np.float32(64)))).astype(np.float32)
    ang = np.arange(S, dtype=np.float32)[:, None] * inv[None, :]
    cos, sin = np.cos(ang).T, np.sin(ang).T
    cs = np.stack([cat([cos, cos]), cat([-sin, sin])], 1)
    a["l1_rope"] = np.tile(cat([cs, cs / np.float32(8)], 1), (2, 1, 1)).astype(np.float32)
    a["l2_w"] = by_partition(cat([f["L2_attn_Wq"], f["L2_attn_Wk"], f["L2_attn_Wv"]], 1), KD)
    a["l2_b"] = cat([f["L2_attn_bq"], f["L2_attn_bk"], f["L2_attn_bv"]])[None]
    a["l2_avg"] = (np.arange(P)[:, None] // (S // LM) == np.arange(P * LM // S)[None]).astype(np.float32) / (S // LM)
    a["l2_w1"] = by_partition(f["L2_ffn_W1"].T, KD)
    a["l2_b1"] = f["L2_ffn_b1"].reshape(FF // P, P).T
    a["l2_w2"] = by_partition(f["L2_ffn_W2"].T, FF // P)
    a["l2_b2"] = f["L2_ffn_b2"][None]
    rows = np.zeros((FT3 * P - I3, D), np.float32)
    a["l3_wg"], a["l3_wu"] = (by_partition(cat([f["L3_ffn_w_" + n], rows]), FT3) for n in ("gate", "up"))
    a["l3_wd"] = by_partition(f["L3_ffn_w_down"], KD)
    def padded(x):
        x = x.reshape(D, GROUPS, HG, 16)
        return cat([x, np.zeros_like(x)], 3).reshape(D, GROUPS, P).transpose(1, 0, 2)

    a["l3_head"] = (np.arange(P)[:, None] // (P // HG) == np.arange(HG)[None]).astype(np.float32)
    qkv = f["L3_attn_w_qkv"]
    a["l3_aw"] = side_by_side(padded(qkv[:, 0:D]), padded(qkv[:, D:2 * D]), columns(qkv[:, 2 * D:], 64),
                              f["L3_attn_w_out"].reshape(GROUPS, 64, D))
    return {k: np.ascontiguousarray(v) for k, v in a.items()}



def tower(nc, dram, out):
    with ExitStack() as ctx:
        T = places(nc, ctx)
        w = Weights(T, ("l1", "l2", "l3_head"))
        wgT, wdT = T.sb("wgT", [P, KD, 2, FT3 * P]), T.sb("wdT", [P, FT3, D])
        rows, results = (nc.dram_tensor("expert_" + n, (SEGS * SEG, D), F32).ap() for n in ("rows", "results"))
        constants(T)
        with ExitStack() as start:
            def sb(name, shape, dt=F32):
                return start.enter_context(nc.sbuf_tensor(name, shape, dt))

            w0 = Weights(T, ("l0", "l3_w"), sb)
            load_weights(T, w0, dram)
            load_weights(T, w, dram)
            embed(T, dram["ids"], dram["table"])
            s_zeroed = zero_places(T, rows, sb("zeros", [P, 8 * D]))
            norm(T, add_back=True, rms=(0.0, 1e-8))
            toeplitz_attention(T, w0)
            with layers_semaphores(T):
                arrivals = Arrivals(T, sb, "c0_", results)
                clipped_layer(T, w0, dram["l0_ew"], rows, results, s_zeroed, arrivals,
                              Fp4Scratch(T, sb, "q3w", 1024, 16), wgT, wdT)
                arrivals.take_place(sb("c0_rows", [P, TB, TOPK * D]))
                norm(T, add_back=True, rms=(1e-6, 0.0), col_scale=w.l1_nw, arrivals=arrivals)

        with nc.sbuf_tensor("kv", [P, N], F32) as kv:
            compress_kv(T, w, kv[:, :])
            with layers_semaphores(T):
                attention(T, w, "a1_", True, 64, dram["l1_aw"], w.l1_rope, kv[:, :])
        with layers_semaphores(T), ExitStack() as layer:
            arrivals = Arrivals(T, lambda name, shape, dt: layer.enter_context(nc.sbuf_tensor(name, shape, dt)),
                                "c1_", results)
            routed_layer(T, w, dram["l1_w13"], dram["l1_w2"], rows, results, s_zeroed, arrivals)
            arrivals.take_place(layer.enter_context(nc.sbuf_tensor("c1_rows", [P, TB, TOPK * D], F32)))
            norm(T, arrivals=arrivals)

        landmark_attention(T, w)
        norm(T)
        ternary_ffn(T, w)

        norm(T)
        attention(T, w, "a3_", False, 16, dram["l3_aw"], w.l3_head)
        tmp = Fp4Scratch(T, T.sb, "q3", 1024, 16)
        norm(T, fp4=tmp)
        fp4_ffn(T, w, tmp, wgT, wdT, out)


def kernel(**inputs):
    import numpy as np
    import concourse.bacc as bacc
    from concourse.bass_utils import run_bass_kernel_spmd

    arrays = lay_out(inputs)
    nc = bacc.Bacc("TRN2", target_bir_lowering=False, num_devices=1)
    dram = {n: nc.dram_tensor("in_" + n, a.shape, mybir.dt.from_np(a.dtype), kind="ExternalInput").ap()
            for n, a in arrays.items()}
    out = nc.dram_tensor("out", (N, D), F32, kind="ExternalOutput").ap()
    tower(nc, dram, out)
    got = run_bass_kernel_spmd(nc, [{"in_" + n: a for n, a in arrays.items()}], core_ids=[0])
    return np.asarray(got.results[0]["out"]).reshape(B, S, D)
```
